# Optimizing a Trainium2 kernel written in Bass

```python
import numpy as np
import jax
import jax.numpy as jnp

def _softmax(x, axis=-1):
    return jax.nn.softmax(x, axis=axis)

def _gelu(x):
    return jax.nn.gelu(x, approximate=True)

def _silu(x):
    return jax.nn.silu(x)

def _sigmoid(x):
    return jax.nn.sigmoid(x)

def _layernorm(x, axis=-1, eps=1e-05):
    m = jnp.mean(x, axis=axis, keepdims=True)
    v = jnp.var(x, axis=axis, keepdims=True)
    return (x - m) / jnp.sqrt(v + eps)

def _scatter_add(tgt, idx, src, axis=0):
    return tgt.at[idx].add(src)

def _segment_sum(src, seg, n):
    return jax.ops.segment_sum(src, seg, n)
kernel_name = 'mk_prb_d2_jaxref_r8_7497d0'

def setup_inputs(seed: int=0):
    np.random.seed(seed)
    _w = jnp.asarray

    def _L0_attn_setup():
        import jax, jax.numpy as jnp
        import numpy as np
        N_HEADS = 16
        HEAD_DIM = 64
        ROPE_THETA = 10000.0

        def _rope_cos_sin(seq_len, dim, theta):
            inv_freq = 1.0 / theta ** (jnp.arange(0, dim, 2, dtype=jnp.float32) / dim)
            pos = jnp.arange(seq_len, dtype=jnp.float32)
            freqs = pos[:, None] * inv_freq[None, :]
            emb = jnp.concatenate([freqs, freqs], axis=-1)
            return (jnp.cos(emb), jnp.sin(emb))

        def _rotate_half(x):
            d = x.shape[-1] // 2
            return jnp.concatenate([-x[..., d:], x[..., :d]], axis=-1)
        key = jax.random.key(seed)
        ks = jax.random.split(key, 6)
        B, S, D_MODEL, LATENT = (1, 512, 128, 64)
        q_dim = N_HEADS * HEAD_DIM
        sd = lambda fan_in: 1.0 / np.sqrt(fan_in)
        return {'x': jax.random.normal(ks[0], (B, S, D_MODEL), jnp.float32), 'wq': jax.random.normal(ks[1], (q_dim, D_MODEL), jnp.float32) * sd(D_MODEL), 'w_kv_down': jax.random.normal(ks[2], (LATENT, D_MODEL), jnp.float32) * sd(D_MODEL), 'w_k_up': jax.random.normal(ks[3], (q_dim, LATENT), jnp.float32) * sd(LATENT), 'w_v_up': jax.random.normal(ks[4], (q_dim, LATENT), jnp.float32) * sd(LATENT), 'wo': jax.random.normal(ks[5], (D_MODEL, q_dim), jnp.float32) * sd(q_dim)}
    _L0_attn_in = _L0_attn_setup()

    def _L0_ffn_setup():
        import jax, jax.numpy as jnp
        import numpy as np
        LN_EPS = 0.001
        EPS = 1e-05
        QB = 128.0

        def ste_round(x):
            return x + jax.lax.stop_gradient(jnp.round(x) - x)
        key = jax.random.key(seed)
        k1, k2 = jax.random.split(key)
        x = jax.random.normal(k1, (4, 1024, 128), dtype=jnp.float32)
        weight = jax.random.normal(k2, (128, 128), dtype=jnp.float32) * 0.02
        ln_gamma = jnp.ones((128,), dtype=jnp.float32)
        ln_beta = jnp.zeros((128,), dtype=jnp.float32)
        return {'x': x, 'weight': weight, 'ln_gamma': ln_gamma, 'ln_beta': ln_beta}
    _L0_ffn_in = _L0_ffn_setup()

    def _L1_attn_setup():
        import jax, jax.numpy as jnp
        import numpy as np
        import math
        T, N, D, H = (256, 2, 128, 16)
        HD = D // H
        key = jax.random.key(seed)
        k1, k2, k3, k4, k5 = jax.random.split(key, 5)
        scale = 0.02
        return {'x': jax.random.normal(k1, (T, N, D), dtype=jnp.float32), 'q_weight': jax.random.normal(k2, (D, H, HD), dtype=jnp.float32) * scale, 'v_weight': jax.random.normal(k3, (D, H, HD), dtype=jnp.float32) * scale, 'out_w': jax.random.normal(k4, (D, D), dtype=jnp.float32) * scale, 'out_b': jax.random.normal(k5, (D,), dtype=jnp.float32) * scale}
    _L1_attn_in = _L1_attn_setup()

    def _L1_ffn_setup():
        import jax, jax.numpy as jnp
        import numpy as np
        B, S, DIM = (4, 512, 128)
        BASE_COUPLING = 0.1
        NUM_CYCLES = 3

        def _gelu(x):
            return jax.nn.gelu(x, approximate=False)

        def _coupling_net(h, w1, b1, w2, b2, w3, b3, w4, b4):
            h = _gelu(h @ w1 + b1)
            h = _gelu(h @ w2 + b2)
            h = _gelu(h @ w3 + b3)
            return jax.nn.sigmoid(h @ w4 + b4)

        def _global_net(h, w1, b1, w2, b2, w3, b3):
            h = _gelu(h @ w1 + b1)
            h = _gelu(h @ w2 + b2)
            return jax.nn.sigmoid(h @ w3 + b3)

        def _twist(x):
            o_r, o_i, p_r, p_i = jnp.split(x, 4, axis=-1)
            return jnp.concatenate([p_r, -p_i, -o_r, o_i], axis=-1)
        key = jax.random.key(seed)
        ks = jax.random.split(key, 9)
        d = DIM

        def w(k, fan_in, fan_out):
            return jax.random.normal(k, (fan_in, fan_out), dtype=jnp.float32) / np.sqrt(fan_in).astype(np.float32)
        inp = {'x': jax.random.normal(ks[0], (B, S, d), dtype=jnp.float32)}
        cn_dims = [(d, d), (d, d // 2), (d // 2, d // 4), (d // 4, 1)]
        for i, (a, b) in enumerate(cn_dims):
            inp[f'cn_w{i + 1}'] = w(ks[1 + i], a, b)
            inp[f'cn_b{i + 1}'] = jnp.zeros((b,), dtype=jnp.float32)
        gc_dims = [(d, d // 2), (d // 2, d // 4), (d // 4, 1)]
        for i, (a, b) in enumerate(gc_dims):
            inp[f'gc_w{i + 1}'] = w(ks[5 + i], a, b)
            inp[f'gc_b{i + 1}'] = jnp.zeros((b,), dtype=jnp.float32)
        inp['adaptive_range'] = jnp.full((1,), 0.2, dtype=jnp.float32)
        return inp
    _L1_ffn_in = _L1_ffn_setup()
    _d = {'L0_attn_x': _L0_attn_in['x'], 'L0_attn_wq': _L0_attn_in['wq'], 'L0_attn_w_kv_down': _L0_attn_in['w_kv_down'], 'L0_attn_w_k_up': _L0_attn_in['w_k_up'], 'L0_attn_w_v_up': _L0_attn_in['w_v_up'], 'L0_attn_wo': _L0_attn_in['wo'], 'L0_ffn_weight': _L0_ffn_in['weight'], 'L0_ffn_ln_gamma': _L0_ffn_in['ln_gamma'], 'L0_ffn_ln_beta': _L0_ffn_in['ln_beta'], 'L1_attn_q_weight': _L1_attn_in['q_weight'], 'L1_attn_v_weight': _L1_attn_in['v_weight'], 'L1_attn_out_w': _L1_attn_in['out_w'], 'L1_attn_out_b': _L1_attn_in['out_b'], 'L1_ffn_cn_w1': _L1_ffn_in['cn_w1'], 'L1_ffn_cn_b1': _L1_ffn_in['cn_b1'], 'L1_ffn_cn_w2': _L1_ffn_in['cn_w2'], 'L1_ffn_cn_b2': _L1_ffn_in['cn_b2'], 'L1_ffn_cn_w3': _L1_ffn_in['cn_w3'], 'L1_ffn_cn_b3': _L1_ffn_in['cn_b3'], 'L1_ffn_cn_w4': _L1_ffn_in['cn_w4'], 'L1_ffn_cn_b4': _L1_ffn_in['cn_b4'], 'L1_ffn_gc_w1': _L1_ffn_in['gc_w1'], 'L1_ffn_gc_b1': _L1_ffn_in['gc_b1'], 'L1_ffn_gc_w2': _L1_ffn_in['gc_w2'], 'L1_ffn_gc_b2': _L1_ffn_in['gc_b2'], 'L1_ffn_gc_w3': _L1_ffn_in['gc_w3'], 'L1_ffn_gc_b3': _L1_ffn_in['gc_b3'], 'L1_ffn_adaptive_range': _L1_ffn_in['adaptive_range']}
    _x0 = _d['L0_attn_x']
    _d['L0_attn_x'] = jax.random.normal(jax.random.fold_in(jax.random.key(seed), 1), (1, 2048, 128), dtype=_x0.dtype)
    del _x0
    return _d

def reference(L0_attn_x, L0_attn_wq, L0_attn_w_kv_down, L0_attn_w_k_up, L0_attn_w_v_up, L0_attn_wo, L0_ffn_weight, L0_ffn_ln_gamma, L0_ffn_ln_beta, L1_attn_q_weight, L1_attn_v_weight, L1_attn_out_w, L1_attn_out_b, L1_ffn_cn_w1, L1_ffn_cn_b1, L1_ffn_cn_w2, L1_ffn_cn_b2, L1_ffn_cn_w3, L1_ffn_cn_b3, L1_ffn_cn_w4, L1_ffn_cn_b4, L1_ffn_gc_w1, L1_ffn_gc_b1, L1_ffn_gc_w2, L1_ffn_gc_b2, L1_ffn_gc_w3, L1_ffn_gc_b3, L1_ffn_adaptive_range):

    def _L0_attn_ref(x, wq, w_kv_down, w_k_up, w_v_up, wo):
        import jax, jax.numpy as jnp
        import numpy as np
        N_HEADS = 16
        HEAD_DIM = 64
        ROPE_THETA = 10000.0

        def _rope_cos_sin(seq_len, dim, theta):
            inv_freq = 1.0 / theta ** (jnp.arange(0, dim, 2, dtype=jnp.float32) / dim)
            pos = jnp.arange(seq_len, dtype=jnp.float32)
            freqs = pos[:, None] * inv_freq[None, :]
            emb = jnp.concatenate([freqs, freqs], axis=-1)
            return (jnp.cos(emb), jnp.sin(emb))

        def _rotate_half(x):
            d = x.shape[-1] // 2
            return jnp.concatenate([-x[..., d:], x[..., :d]], axis=-1)
        B, S, _ = x.shape
        H, D = (N_HEADS, HEAD_DIM)
        q = jnp.einsum('bsd,qd->bsq', x, wq).reshape(B, S, H, D).transpose(0, 2, 1, 3)
        kv_latent = jnp.einsum('bsd,ld->bsl', x, w_kv_down)
        k = jnp.einsum('bsl,ql->bsq', kv_latent, w_k_up).reshape(B, S, H, D).transpose(0, 2, 1, 3)
        v = jnp.einsum('bsl,ql->bsq', kv_latent, w_v_up).reshape(B, S, H, D).transpose(0, 2, 1, 3)
        cos, sin = _rope_cos_sin(S, D, ROPE_THETA)
        cos = cos[None, None]
        sin = sin[None, None]
        q = q * cos + _rotate_half(q) * sin
        k = k * cos + _rotate_half(k) * sin
        scores = jnp.einsum('bhsd,bhtd->bhst', q, k) / jnp.sqrt(jnp.float32(D))
        causal = jnp.triu(jnp.full((S, S), -jnp.inf, dtype=jnp.float32), k=1)
        scores = scores + causal[None, None]
        probs = jax.nn.softmax(scores.astype(jnp.float32), axis=-1).astype(q.dtype)
        out = jnp.einsum('bhst,bhtd->bhsd', probs, v)
        out = out.transpose(0, 2, 1, 3).reshape(B, S, H * D)
        return jnp.einsum('bsq,dq->bsd', out, wo)

    def _L0_ffn_ref(x, weight, ln_gamma, ln_beta):
        import jax, jax.numpy as jnp
        import numpy as np
        LN_EPS = 0.001
        EPS = 1e-05
        QB = 128.0

        def ste_round(x):
            return x + jax.lax.stop_gradient(jnp.round(x) - x)
        mu = jnp.mean(x, axis=-1, keepdims=True)
        var = jnp.var(x, axis=-1, keepdims=True)
        xn = (x - mu) * jax.lax.rsqrt(var + LN_EPS) * ln_gamma + ln_beta
        beta = jnp.mean(jnp.abs(weight))
        w_q = jnp.clip(ste_round(weight / (beta + EPS)), -1.0, 1.0)
        gamma = jnp.max(jnp.abs(xn))
        xq = jnp.clip(xn * QB / gamma, -QB + EPS, QB - EPS)
        y = jnp.einsum('bsd,du->bsu', xq, w_q)
        return y * (gamma * beta / QB)

    def _L1_attn_ref(x, q_weight, v_weight, out_w, out_b):
        import jax, jax.numpy as jnp
        import numpy as np
        import math
        T, N, D, H = (256, 2, 128, 16)
        HD = D // H
        head_dim = q_weight.shape[-1]
        inv_sqrt_d = 1.0 / math.sqrt(head_dim)
        q = jnp.einsum('tbm,mhd->tbhd', x, q_weight)
        q_sq = jnp.einsum('tbhd,tbhd->tbh', q, q)
        squared_dist = q_sq[:, None] + q_sq[None, :] - 2.0 * jnp.einsum('tbhd,sbhd->tsbh', q, q)
        attn_logits = -squared_dist * inv_sqrt_d
        attn_weights = jax.nn.softmax(attn_logits, axis=1)
        A = jnp.einsum('mhd,nhd->hmn', q_weight, q_weight) * inv_sqrt_d
        XA = jnp.einsum('tbm,hmn->tbhn', x, A)
        PXA = jnp.einsum('tsbh,sbhm->tbhm', attn_weights, XA)
        PXAV = jnp.einsum('tbhm,mhd->tbhd', PXA, v_weight).reshape(x.shape[0], x.shape[1], -1)
        return PXAV @ out_w.T + out_b

    def _L1_ffn_ref(x, cn_w1, cn_b1, cn_w2, cn_b2, cn_w3, cn_b3, cn_w4, cn_b4, gc_w1, gc_b1, gc_w2, gc_b2, gc_w3, gc_b3, adaptive_range):
        import jax, jax.numpy as jnp
        import numpy as np
        B, S, DIM = (4, 512, 128)
        BASE_COUPLING = 0.1
        NUM_CYCLES = 3

        def _gelu(x):
            return jax.nn.gelu(x, approximate=False)

        def _coupling_net(h, w1, b1, w2, b2, w3, b3, w4, b4):
            h = _gelu(h @ w1 + b1)
            h = _gelu(h @ w2 + b2)
            h = _gelu(h @ w3 + b3)
            return jax.nn.sigmoid(h @ w4 + b4)

        def _global_net(h, w1, b1, w2, b2, w3, b3):
            h = _gelu(h @ w1 + b1)
            h = _gelu(h @ w2 + b2)
            return jax.nn.sigmoid(h @ w3 + b3)

        def _twist(x):
            o_r, o_i, p_r, p_i = jnp.split(x, 4, axis=-1)
            return jnp.concatenate([p_r, -p_i, -o_r, o_i], axis=-1)
        global_context = x.mean(axis=1, keepdims=True)
        gf = _global_net(global_context, gc_w1, gc_b1, gc_w2, gc_b2, gc_w3, gc_b3)
        out = x
        for _ in range(NUM_CYCLES):
            tf = _coupling_net(out, cn_w1, cn_b1, cn_w2, cn_b2, cn_w3, cn_b3, cn_w4, cn_b4)
            combined = 0.7 * gf + 0.3 * tf
            coupling = BASE_COUPLING + adaptive_range * (combined - 0.5) * 2.0
            out = out + coupling * _twist(out)
        return out
    x = L0_attn_x
    xn = _layernorm(x, axis=-1)
    x = x + _L0_attn_ref(xn, L0_attn_wq, L0_attn_w_kv_down, L0_attn_w_k_up, L0_attn_w_v_up, L0_attn_wo) + _L0_ffn_ref(xn, L0_ffn_weight, L0_ffn_ln_gamma, L0_ffn_ln_beta)
    xn = _layernorm(x, axis=-1)
    x = x + _L1_attn_ref(xn, L1_attn_q_weight, L1_attn_v_weight, L1_attn_out_w, L1_attn_out_b) + _L1_ffn_ref(xn, L1_ffn_cn_w1, L1_ffn_cn_b1, L1_ffn_cn_w2, L1_ffn_cn_b2, L1_ffn_cn_w3, L1_ffn_cn_b3, L1_ffn_cn_w4, L1_ffn_cn_b4, L1_ffn_gc_w1, L1_ffn_gc_b1, L1_ffn_gc_w2, L1_ffn_gc_b2, L1_ffn_gc_w3, L1_ffn_gc_b3, L1_ffn_adaptive_range)
    return x

_drawn_inputs = setup_inputs


def setup_inputs(seed=0):
    import zlib

    import numpy as np

    out = dict(_drawn_inputs(seed))
    spreads = {'L0_ffn_ln_gamma': (1.0, 0.2),
     'L0_ffn_ln_beta': (0.0, 0.512),
     'L1_ffn_cn_b1': (0.0, 2.0),
     'L1_ffn_cn_b2': (0.0, 2.0),
     'L1_ffn_cn_b3': (0.0, 2.0),
     'L1_ffn_gc_b1': (0.0, 0.8),
     'L1_ffn_gc_b2': (0.0, 2.0)}
    factors = {'L1_attn_q_weight': 8.0,
     'L1_attn_v_weight': 8.0,
     'L1_attn_out_w': 8.0,
     'L1_attn_out_b': 5.576,
     'L1_ffn_cn_w1': 7.56,
     'L1_ffn_cn_w2': 5.872,
     'L1_ffn_cn_w3': 5.911,
     'L1_ffn_cn_w4': 5.428,
     'L1_ffn_gc_w1': 64.0,
     'L1_ffn_gc_w2': 8.0,
     'L1_ffn_gc_w3': 8.0}
    for name, (base, spread) in spreads.items():
        noise = np.random.default_rng([zlib.crc32(name.encode()), seed]).standard_normal(out[name].shape)
        drawn = base * np.exp(spread * noise) if base else spread * noise
        out[name] = jnp.asarray(drawn.astype(out[name].dtype))
    for name, factor in factors.items():
        out[name] = (out[name] * factor).astype(out[name].dtype)
    return out
```

```python
from contextlib import ExitStack

import concourse.bass as bass
from concourse import mybir

F32 = mybir.dt.float32
BF16 = mybir.dt.bfloat16
F16 = mybir.dt.float16
I32 = mybir.dt.int32
ALU = mybir.AluOpType
ACT = mybir.ActivationFunctionType
AX = mybir.AxisListType

P = 128
S = 2048
D = 128
H = 16
HD = 64
L = 64
PAIRS = H // 2
CH = 512
NCH = S // CH
NT = S // P
UNITS = sum((4 * c + 4) // 2 for c in range(NCH))
LAG = 2
HIGH_LAG = 4
PBUF = 4
MSHIFT = 2048.0
NEG = -1.0e30
LN_EPS, FFN_EPS, EPS, QB = 1e-5, 1e-3, 1e-5, 128.0

UNIT = [(c, k) for c in range(NCH) for k in range(0, 4 * c + 4, 2)]
CHUNK_END = {u: c for u, (c, k) in enumerate(UNIT) if k == 4 * c + 2}
PIECES = [(t, k, min(CH, (t + 1) * P - k)) for t in range(NT) for k in range(0, (t + 1) * P, CH)]
MAX_SLOTS = range(2, 16)
PER_SLOT = 3
ROPES = 4 * NCH


def works_of_slot(w, rope, max_b, max_a):
    e, u = divmod(w, UNITS)
    before, after = [], []
    if rope and w < ROPES:
        before.append(("rope", w))
    if (max_b, max_a)[e] and u in MAX_SLOTS:
        n = (u - MAX_SLOTS[0]) * PER_SLOT
        before += [("max", p) for p in range(n, min(n + PER_SLOT, len(PIECES)))]
    if (max_b, max_a)[e] and u == MAX_SLOTS[-1] + 1:
        before.append(("mrow", 0))
    for lag, kind in ((1, "sum"), (2, "out")):
        v = w - lag
        if v >= 0 and v % UNITS in CHUNK_END:
            after.append((kind, (v // UNITS) * NCH + CHUNK_END[v % UNITS]))
    return before, after


def plan(first, rope, max_b, max_a):
    n, slots = first, []
    for w in range(2 * UNITS):
        before, after = works_of_slot(w, rope, max_b, max_a)
        if w == 2 * UNITS - 1:
            after += [("sum", 2 * NCH - 1), ("out", 2 * NCH - 1)]
        before = [(kind, a, n + j) for j, (kind, a) in enumerate(before)]
        n += len(before)
        after = [(kind, a, n + j) for j, (kind, a) in enumerate(after)]
        n += len(after)
        slots.append((before, after))
    return slots, n


PROLOGUE_WORKS = [("rope", r) for r in range(ROPES)] + [("max", p) for p in range(len(PIECES))] + [("mrow", 0)]
BODY, _end = plan(len(PROLOGUE_WORKS), True, True, True)
PER_PAIR = _end - len(PROLOGUE_WORKS)
assert PER_PAIR % 2 == 0
LAST, _ = plan(len(PROLOGUE_WORKS), False, True, False)
MAXES = len(PIECES)


def build(nc, x, wqT, wqpT, wkT, wkpT, wv, woT, mats, cols, rows, cosT, sinT, out):
    with ExitStack() as ctx:
        def sb(name, shape, dt=F32):
            return ctx.enter_context(nc.sbuf_tensor(name, shape, dt))

        def ps(name, shape):
            return ctx.enter_context(nc.psum_tensor(name, shape, F32))

        def sem(name):
            return ctx.enter_context(nc.semaphore(name))

        ST = ps("ST", [P, 2, 2, CH])
        WK = ps("WK", [P, 2, CH])
        OU = ps("OU", [P, CH])
        RS = ps("RS", [P, CH])

        X = sb("X", [P, NT, D])
        XN = sb("XN", [P, NT, D])
        ACC = sb("ACC", [P, NT, D])
        XNT = sb("XNT", [P, S])
        XH = sb("XH", [P, S], F16)
        XL = sb("XL", [P, S], F16)
        LT = sb("LT", [P, S], F16)
        LS = sb("LS", [P, NT, 2, L], F16)
        COS = sb("COS", [P, S])
        SIN = sb("SIN", [P, S])
        WQH = sb("WQH", [P, 2, H * HD], F16)
        WQL = sb("WQL", [P, 2, H * HD], F16)
        WKH = sb("WKH", [P, 2, H * HD], F16)
        WKL = sb("WKL", [P, 2, H * HD], F16)
        GG = sb("GG", [P, H * D])
        MA = sb("MA", [P, mats.shape[1]])
        CO = sb("CO", [P, cols.shape[1]])
        RW = sb("RW", [1, rows.shape[1]])
        QS = sb("QS", [P, 2, S], F16)
        QM = sb("QM", [HD + 2, 2, S], F16)
        KK = sb("KK", [P, 2, S], F16)
        KL = sb("KL", [HD + 2, 2, S], F16)
        SG = sb("SG", [P, 4, S], F16)
        RA = sb("RA", [P, 2, CH])
        RB = sb("RB", [P, 2, CH])
        PR = sb("PR", [P, PBUF, 2, CH])
        PL = sb("PL", [P, PBUF, 2, CH], F16)
        OS = sb("OS", [P, 2, CH])
        RSS = sb("RSS", [P, 2, CH])
        RL = sb("RL", [P, 2, 4])
        MP = sb("MP", [P, NT, 4])
        NM = sb("NM", [P, NT])
        MM = sb("MM", [P, 2, NT], F16)
        MT = sb("MT", [2 * NT, P], F16)
        ST6 = sb("ST6", [P, NT, 6])
        MV = sb("MV", [P, NT, 2])
        SD = sb("SD", [P, NT])
        RD = sb("RD", [P, NT])
        AM = sb("AM", [P, 4])
        AMG = sb("AMG", [P, 4])
        EX = sb("EX", [P, 4])
        IV = sb("IV", [P, 4])
        SC = sb("SC", [P, 8])
        TC = sb("TC", [P, 16])
        ONE = sb("ONE", [P, 32], BF16)
        IDB = sb("IDB", [P, P], BF16)
        IDH = sb("IDH", [P, P], F16)
        MK = sb("MK", [P, 2, P], BF16)
        SEL = sb("SEL", [P, 1])
        EPSC = sb("EPSC", [P, 2])
        WT = sb("WT", [P, 2 * D])
        RAW = PR[:, :, :, :].rearrange("p b j n -> p (b j n)")
        WQ = RAW[:, 0:2 * H * HD].rearrange("p (a n) -> p a n", a=2)
        WKU = RAW[:, 2 * H * HD:4 * H * HD].rearrange("p (a n) -> p a n", a=2)
        WV = QS[0:HD, :, :].bitcast(F32).rearrange("p s n -> p (s n)").rearrange("p (h a l) -> p h a l", h=H, a=2)
        WO = KK[0:HD, :, :].bitcast(F32).rearrange("p s n -> p (s n)").rearrange("p (h m) -> p h m", h=H)
        Z = SG[:, 0:2, :].bitcast(F32).rearrange("p a n -> p (a n)").rearrange("p (t d) -> p t d", d=D)
        ZT = XNT
        PH = PR[:, :, :, :].bitcast(BF16).rearrange("p b j (n two) -> p b j n two", two=2)[:, :, :, :, 1]

        def mat(n, rows_=P, cols_=D):
            return MA[0:rows_, n * D:n * D + cols_]

        (IDENT, WD2, W_FFN, GAMMA, BETA, MASK_QK, MASK_KQ, Q1, Q1T, V1, WO1T, BLK, PERM,
         CW1, CW2, CW3, CW4, GW1, GW2, GW3) = range(20)
        (C_B1, C_B2, C_B3, C_B4, G_B1, G_B2, G_B3, AR) = range(8)

        x_in, w_in, m_in = sem("x_in"), sem("w_in"), sem("m_in")
        t_in, g_in = sem("t_in"), sem("g_in")
        dve = sem("dve_chain")
        pool = sem("pool_chain")
        var_ready, std_ready = sem("var_ready"), sem("std_ready")
        xn_ready, xnt_ready = sem("xn_ready"), sem("xnt_ready")
        xt_copied = sem("xt_copied")
        split_ready, am_ready, amg_ready = sem("split_ready"), sem("am_ready"), sem("amg_ready")
        wd_ready = sem("wd_ready")
        latt_ready, latt_used = sem("latt_ready"), sem("latt_used")
        lats_ready, lats_used = sem("lats_ready"), sem("lats_used")
        gg_ready, gg_used = sem("gg_ready"), sem("gg_used")
        const_ready = sem("const_ready")
        z_ready, zt_ready, zt_copied = sem("z_ready"), sem("zt_ready"), sem("zt_copied")
        zmax_ready, zmaxg_ready, wf_ready = sem("zmax_ready"), sem("zmaxg_ready"), sem("wf_ready")
        ffn_ready = sem("ffn_ready")
        rope_ready, max_ready, mrow_ready = sem("rope_ready"), sem("max_ready"), sem("mrow_ready")
        sum_ready, out_ready = sem("sum_ready"), sem("out_ready")
        rope_copied, rope_product, rope_summed = sem("rope_copied"), sem("rope_product"), sem("rope_summed")
        high_ready, low_ready = sem("high_ready"), sem("low_ready")
        stacked = [sem("slot0_stacked"), sem("slot1_stacked")]
        piece_done, mneg_ready, mparts_ready = sem("piece_done"), sem("mneg_ready"), sem("mparts_ready")
        mt_copied, mrow_stacked = sem("mt_copied"), sem("mrow_stacked")
        scores_ready, probs_ready, low_probs = sem("scores_ready"), sem("probs_ready"), sem("low_probs")
        unit_summed, chunk_copied = sem("unit_summed"), sem("chunk_copied")
        rl_ready, acc_ready = sem("rl_ready"), sem("acc_ready")
        x1_stats, x1_std, x1n, x1t, x1t_copied = (sem("x1_stats"), sem("x1_std"), sem("x1n"), sem("x1t"),
                                                  sem("x1t_copied"))
        m1_ready, m1_copied = sem("m1_ready"), sem("m1_copied")
        gc_mm, gc_act, gc_done = sem("gc_mm"), sem("gc_act"), sem("gc_done")
        cn_mm, cn_act, cn_tw, cn_out = sem("cn_mm"), sem("cn_act"), sem("cn_twist"), sem("cn_out")
        y_ready, y_done, stored = sem("y_ready"), sem("y_done"), sem("stored")

        block = ctx.enter_context(nc.Block())

        def bank_of(n):
            return n % 2

        def bank_read(kind, a, e, i):
            if kind == "rope":
                return rope_copied, i * ROPES + a + 1
            if kind == "max":
                return piece_done, i * (2 * MAXES) + (e + 1) * MAXES + a + 1
            if kind == "mrow":
                return mt_copied, i * 2 + e + 2
            if kind == "sum":
                return rl_ready, i * (2 * NCH) + a + 1
            return acc_ready, i * (2 * NCH) + NCH + a + 1

        @block.sync
        def _(sp):
            sp.dma_start(X[:, :, :], x.rearrange("(t p) d -> p t d", p=P)).then_inc(x_in, 16)
            sp.dma_start(MA[:, :], mats).then_inc(m_in, 16)
            sp.dma_start(CO[:, :], cols).then_inc(m_in, 16)
            sp.dma_start(RW[:, :], rows).then_inc(m_in, 16)
            sp.dma_start(WQ[:, 0, :], wqT).then_inc(w_in, 16)
            sp.dma_start(WQ[:, 1, :], wqpT).then_inc(w_in, 16)
            for half in range(2):
                sp.dma_start(WKU[half * L:half * L + L, 0, :], wkT).then_inc(w_in, 16)
                sp.dma_start(WKU[half * L:half * L + L, 1, :], wkpT).then_inc(w_in, 16)
            sp.dma_start(COS[:, :], cosT).then_inc(t_in, 16)
            sp.dma_start(SIN[:, :], sinT).then_inc(t_in, 16)
            for half in range(2):
                sp.dma_start(WV[:, :, half, :], wv.rearrange("(h d) l -> d h l", d=HD)).then_inc(g_in, 16)
            sp.dma_start(WO[:, :, :], woT.rearrange("(h d) m -> d h m", d=HD)).then_inc(g_in, 16)

            def stack(slot, i):
                q0 = slot * HD
                for dst, part in ((QS[0:HD, slot, :], 0), (QS[HD:P, slot, :], 1), (QM[0:HD, slot, :], 0),
                                  (KK[0:HD, slot, :], 2), (KK[HD:P, slot, :], 2), (KL[0:HD, slot, :], 3)):
                    sp.dma_start(dst, SG[q0:q0 + HD, part, :]).then_inc(stacked[slot], 16)

            def mrows(slot, h):
                sp.wait_ge(mt_copied, h + 1)
                for j in range(2):
                    sp.dma_start(QM[HD + j:HD + j + 1, slot, :], MT[j * NT:(j + 1) * NT, :])\
                        .then_inc(mrow_stacked, 16)

            sp.wait_ge(low_ready, 2 * NCH)
            sp.wait_ge(high_ready, 2 * NCH)
            stack(0, 0)
            stack(1, 0)
            mrows(0, 0)

            def pair(i, more):
                mrows(1, i * 2 + 1)
                if more:
                    sp.wait_ge(low_ready, i * (2 * NCH) + 4 * NCH)
                    sp.wait_ge(high_ready, i * (2 * NCH) + 4 * NCH)
                    sp.wait_ge(scores_ready, i * (2 * UNITS) + UNITS)
                    stack(0, i)
                    mrows(0, i * 2 + 2)
                    sp.wait_ge(scores_ready, i * (2 * UNITS) + 2 * UNITS)
                    stack(1, i)

            with sp.Fori(0, PAIRS - 1) as i:
                pair(i, True)
            pair(PAIRS - 1, False)
            for c in range(NCH):
                sp.wait_ge(y_done, c + 1)
                sp.dma_start(out.rearrange("(t p) d -> p t d", p=P)[:, 4 * c:4 * c + 4, :],
                             X[:, 4 * c:4 * c + 4, :]).then_inc(stored, 16)
            sp.wait_ge(stored, 16 * NCH)

        @block.tensor
        def _(pe):
            def tile_T(src_tile, c, copied, n):
                bank = ST[:, c // 2, c % 2, :]
                for t in range(4):
                    mm = pe.transpose(bank[:, t * P:(t + 1) * P], src_tile(4 * c + t), mat(IDENT))
                mm.then_inc(n, 1)

            pe.wait_ge(m_in, 48)
            for c in range(NCH):
                pe.wait_ge(xn_ready, 4 * c + 4)
                tile_T(lambda t: XN[:, t, :], c, None, xnt_ready)
            pe.wait_ge(wd_ready, 1)
            for c in range(NCH):
                pe.wait_ge(xt_copied, c + 1)
                pe.wait_ge(split_ready, c + 1)
                pe.matmul(ST[:, c // 2, c % 2, :], WT[:, 0:P], XNT[:, c * CH:(c + 1) * CH],
                          start=True, stop=True).then_inc(latt_ready, 1)
            for g in range(2):
                for t in range(8):
                    mm = pe.matmul(WK[:, g, t * L:(t + 1) * L], XNT[:, (8 * g + t) * P:(8 * g + t + 1) * P],
                                   WT[:, 0:L], start=True, stop=True, skip_group_check=True)
                mm.then_inc(lats_ready, 1)
            pe.wait_ge(g_in, 48)
            for h in range(H):
                bank = (OU, RS)[h // 4 % 2]
                if h % 4 == 0 and h >= 8:
                    pe.wait_ge(gg_used, h // 4 - 1)
                mm = pe.matmul(bank[:, h % 4 * D:(h % 4 + 1) * D],
                               WV[:, h, :, :].rearrange("d a l -> d (a l)"), WO[:, h, :],
                               start=True, stop=True, skip_group_check=True)
                if h % 4 == 3:
                    mm.then_inc(gg_ready, 1)

            for c in range(NCH):
                pe.wait_ge(latt_used, c + 1)
                pe.wait_ge(z_ready, 4 * c + 4)
                tile_T(lambda t: Z[:, t, :], c, None, zt_ready)
            pe.wait_ge(wf_ready, 1)
            for c in range(NCH):
                pe.wait_ge(zt_copied, c + 1)
                for t in range(4):
                    mm = pe.matmul(ST[:, c // 2, c % 2, t * P:(t + 1) * P],
                                   ZT[:, (4 * c + t) * P:(4 * c + t + 1) * P], WT[:, P:2 * P],
                                   start=True, stop=True, skip_group_check=True)
                mm.then_inc(ffn_ready, 1)
            pe.wait_ge(acc_ready, NCH)
            pe.wait_ge(lats_used, 2)
            pe.wait_ge(gg_used, 4)
            pe.wait_ge(const_ready, 1)
            pe.sem_inc(unit_summed, PBUF)

            def rope(r, n, pair_):
                kind, c, swapped = r // (2 * NCH), r // 2 % NCH, r % 2
                bank = WK[:, bank_of(n), :]
                cs = slice(c * CH, (c + 1) * CH)

                def w(t):
                    return t[:, swapped, 0:P] if isinstance(pair_, int) and pair_ == 0 else t[:, swapped, bass.ds(pair_ * P, P)]
                if kind == 0:
                    pe.matmul(bank, w(WQH), XH[:, cs], start=True, stop=False)
                    pe.matmul(bank, w(WQH), XL[:, cs], start=False, stop=False)
                    mm = pe.matmul(bank, w(WQL), XH[:, cs], start=False, stop=True)
                else:
                    pe.matmul(bank, w(WKH), LT[:, cs], start=True, stop=False)
                    mm = pe.matmul(bank, w(WKL), LT[:, cs], start=False, stop=True)
                mm.then_inc(rope_ready, 1)

            def max_piece(p, n, slot):
                t, k, w = PIECES[p]
                bank = WK[:, bank_of(n), 0:w]
                diagonal = k + w == (t + 1) * P
                mm = pe.matmul(bank, QS[:, slot, t * P:(t + 1) * P], KK[:, slot, k:k + w],
                               start=True, stop=not diagonal)
                if diagonal:
                    mm = pe.matmul(WK[:, bank_of(n), w - P:w], IDB[:, :], MK[:, 0, :], start=False, stop=True)
                mm.then_inc(max_ready, 1)

            def mrow(n, h):
                pe.wait_ge(mparts_ready, h + 1)
                pe.transpose(WK[:, bank_of(n), :].bitcast(F16)[0:2 * NT, 0:P],
                             MM[:, :, :].rearrange("p a t -> p (a t)"), IDH[:, :]).then_inc(mrow_ready, 1)

            def scores(g):
                slot, (c, k0) = g // UNITS % 2, UNIT[g % UNITS]
                for j in range(2):
                    k = k0 + j
                    n0 = max(0, k - 4 * c) * P
                    bank = ST[:, g % 2, j, n0:CH]
                    q = slice(c * CH + n0, (c + 1) * CH)
                    diagonal = k >= 4 * c
                    pe.matmul(bank, KK[:, slot, k * P:(k + 1) * P], QS[:, slot, q], start=True, stop=False)
                    mm = pe.matmul(bank, KL[:, slot, k * P:(k + 1) * P], QM[:, slot, q],
                                   start=False, stop=not diagonal)
                    if diagonal:
                        mm = pe.matmul(ST[:, g % 2, j, n0:n0 + P], IDB[:, :], MK[:, 1, :],
                                       start=False, stop=True)
                mm.then_inc(scores_ready, 1)

            def values(g):
                c, k0 = UNIT[g % UNITS]
                b = g % PBUF
                n0 = [max(0, k0 + j - 4 * c) * P for j in range(2)]
                for j in range(2):
                    pe.matmul(OU[:, n0[j]:CH], LS[:, k0 + j, :, :].rearrange("p a l -> p (a l)"),
                              PH[:, b, j, n0[j]:CH], start=(k0 + j == 0), stop=False, skip_group_check=True)
                for j in range(2):
                    pe.matmul(OU[HD * j:HD * j + HD, n0[j]:CH], LS[:, k0 + j, 0, :], PL[:, b, j, n0[j]:CH],
                              start=False, stop=(k0 == 4 * c + 2), skip_group_check=True)
                for j in range(2):
                    row = 0 if c == 0 else 64 * j
                    for part, src in enumerate((PH, PL)):
                        mm = pe.matmul(RS[row + 32 * part:row + 32 * part + 32, n0[j]:CH], ONE[:, :],
                                       src[:, b, j, n0[j]:CH], start=(k0 == 0 and (j == 0 or c > 0)),
                                       stop=(k0 == 4 * c + 2), skip_group_check=True)
                mm.then_inc(unit_summed, 1)

            def sums(ch, n):
                for t in range(4):
                    rows_ = HD if ch % NCH == 0 else P
                    mm = pe.matmul(WK[:, bank_of(n), t:t + 1], RSS[0:rows_, ch % 2, t * P:(t + 1) * P],
                                   SEL[0:rows_, :], start=True, stop=True, skip_group_check=True)
                mm.then_inc(sum_ready, 1)

            def outs(ch, n, i):
                e = ch // NCH
                g = (GG[:, bass.ds(i * (2 * D) + e * D, D)] if not isinstance(i, int)
                     else GG[:, (2 * i + e) * D:(2 * i + e + 1) * D])
                for t in range(4):
                    mm = pe.matmul(WK[:, bank_of(n), t * P:(t + 1) * P], OS[:, ch % 2, t * P:(t + 1) * P], g,
                                   start=True, stop=True, skip_group_check=True)
                mm.then_inc(out_ready, 1)

            def pair(i, slots, more):
                units = i * (2 * UNITS)
                used = []

                def take_bank(kind, a, e):
                    if len(used) < 2:
                        pe.wait_ge(acc_ready, i * (2 * NCH) + NCH)
                        pe.wait_ge(mt_copied, i * 2 + 1)
                    else:
                        pe.wait_ge(*bank_read(*used[-2], i))
                    used.append((kind, a, e))

                for w, (before, after) in enumerate(slots):
                    e = w // UNITS
                    for kind, a, n in before:
                        take_bank(kind, a, e)
                        if kind == "rope":
                            rope(a, n, i + 1)
                        elif kind == "mrow":
                            mrow(n, i * 2 + e + 1)
                        else:
                            if a == 0:
                                pe.wait_ge(stacked[1 - e], i * 96 + 96 * (e + 1))
                            max_piece(a, n, 1 - e)
                    g = w + LAG
                    if g < 2 * UNITS or more:
                        if g % UNITS == 0:
                            pe.wait_ge(mrow_stacked, i * 64 + 32 * (g // UNITS) + 32)
                        pe.wait_ge(probs_ready, units + g - 1)
                        scores(g)
                    c, k0 = UNIT[w % UNITS]
                    if w == 0:
                        pe.wait_ge(acc_ready, i * (2 * NCH) + NCH)
                    elif k0 == 0:
                        pe.wait_ge(chunk_copied, i * (2 * NCH) + e * NCH + c)
                    pe.wait_ge(low_probs, units + w + 1)
                    values(w)
                    for kind, a, n in after:
                        take_bank(kind, a, e)
                        pe.wait_ge(chunk_copied, i * (2 * NCH) + a + 1)
                        if kind == "sum":
                            sums(a, n)
                        else:
                            outs(a, n, i)

            for n, (kind, a) in enumerate(PROLOGUE_WORKS):
                if n >= 2:
                    was, b = PROLOGUE_WORKS[n - 2]
                    pe.wait_ge(rope_product if was == "rope" else piece_done, b + 1)
                if kind == "rope":
                    rope(a, n, 0)
                elif kind == "max":
                    if a == 0:
                        pe.wait_ge(stacked[0], 96)
                    max_piece(a, n, 0)
                else:
                    mrow(n, 0)
            pe.wait_ge(mrow_stacked, 32)
            for g in range(LAG):
                scores(g)

            with pe.Fori(0, PAIRS - 1) as i:
                pair(i, BODY, True)
            pair(PAIRS - 1, LAST, False)

            pe.wait_ge(chunk_copied, H * NCH)
            pe.matmul(OU[:, 0:D], mat(V1), mat(Q1), start=True, stop=True).then_inc(m1_ready, 1)
            pe.wait_ge(m1_copied, 1)
            pe.matmul(OU[:, 0:D], WT[:, 0:D], mat(WO1T), start=True, stop=True).then_inc(m1_ready, 1)
            pe.wait_ge(m1_copied, 2)
            pe.matmul(OU[:, 0:D], mat(Q1T), WT[:, D:2 * D], start=True, stop=True).then_inc(m1_ready, 1)
            pe.wait_ge(probs_ready, H * UNITS)
            for c in range(NCH):
                pe.wait_ge(x1n, 4 * c + 4)
                tile_T(lambda t: XN[:, t, :], c, None, x1t)
            pe.wait_ge(gc_done, 1)
            pe.matmul(RS[0:64, 0:1], mat(GW1, P, 64), TC[:, 4:5], start=True, stop=True).then_inc(gc_mm, 1)
            pe.wait_ge(gc_act, 1)
            pe.matmul(RS[0:32, 0:1], mat(GW2, 64, 32), TC[0:64, 5:6], start=True, stop=True).then_inc(gc_mm, 1)
            pe.wait_ge(gc_act, 2)
            pe.matmul(RS[:, 0:1], mat(GW3, 32, P), TC[0:32, 6:7], start=True, stop=True).then_inc(gc_mm, 1)
            pe.wait_ge(gc_act, 3)
            for cyc in range(3):
                for c in range(NCH):
                    n = cyc * NCH + c
                    cs = slice(c * CH, (c + 1) * CH)
                    bank, twist = ST[:, c // 2, c % 2, :], WK[:, c % 2, :]
                    if cyc == 0:
                        pe.wait_ge(x1t_copied, 4)
                    else:
                        pe.wait_ge(cn_out, n - NCH + 1)
                    if cyc == 0 and c == 0:
                        pe.wait_ge(acc_ready, H * NCH + 4)
                    if n >= 2:
                        pe.wait_ge(cn_out, n - 1)
                    src = XNT if cyc == 0 else COS
                    pe.matmul(twist, mat(PERM), src[:, cs], start=True, stop=True)
                    pe.matmul(bank, mat(CW1), src[:, cs], start=True, stop=True).then_inc(cn_mm, 1)
                    pe.wait_ge(cn_act, 4 * n + 1)
                    pe.matmul(bank[0:64, :], mat(CW2, P, 64), RA[:, 0, :], start=True, stop=True)\
                        .then_inc(cn_mm, 1)
                    pe.wait_ge(cn_act, 4 * n + 2)
                    pe.matmul(bank[0:32, :], mat(CW3, 64, 32), RA[0:64, 1, :], start=True, stop=True)\
                        .then_inc(cn_mm, 1)
                    pe.wait_ge(cn_act, 4 * n + 3)
                    pe.matmul(bank, mat(CW4, 32, P), RB[0:32, 0, :], start=True, stop=True).then_inc(cn_mm, 1)
            pe.wait_ge(m1_copied, 3)
            for c in range(NCH):
                pe.wait_ge(cn_out, 2 * NCH + NCH)
                bank = ST[:, c // 2, c % 2, :]
                for t in range(4):
                    ts = slice((4 * c + t) * P, (4 * c + t + 1) * P)
                    o = bank[:, t * P:(t + 1) * P]
                    pe.matmul(o, XNT[:, ts], GG[:, 0:D], start=True, stop=False, skip_group_check=True)
                    pe.matmul(o, COS[:, ts], mat(IDENT), start=False, stop=False, skip_group_check=True)
                    mm = pe.matmul(o, RW[:, D:2 * D], RW[:, 0:D], start=False, stop=True, skip_group_check=True)
                mm.then_inc(y_ready, 1)

        @block.vector
        def _(v):
            chain = [0]

            def link(ins):
                chain[0] += 1
                ins.then_inc(dve, 1)
                v.wait_ge(dve, chain[0])

            def stats(src, eps_col, ready, std):
                for t in range(NT):
                    last = v.bn_stats(ST6[:, t, :], src[:, t, :])
                link(last)
                for t in range(NT):
                    last = v.bn_aggr(MV[:, t, :], ST6[:, t, :])
                last.then_inc(ready, 1)
                v.wait_ge(std, 1)
                link(v.reciprocal(RD[:, :], SD[:, :]))

            v.memset(EPSC[:, 0:1], LN_EPS)
            v.memset(EPSC[:, 1:2], FFN_EPS)
            v.memset(ONE[:, :], 1.0)
            v.memset(SEL[:, :], 0.0)
            v.memset(MP[:, :, :], -3.0e38)
            v.memset(KL[HD:HD + 2, :, :], MSHIFT)
            link(v.memset(RSS[:, :, :], 0.0))
            for q in range(4):
                last = v.memset(SEL[32 * q:32 * q + 1, :], 1.0)
            link(last)
            v.wait_ge(x_in, 16)
            stats(X, 0, var_ready, std_ready)
            for t in range(NT):
                v.tensor_scalar(XN[:, t, :], X[:, t, :], MV[:, t, 0:1], RD[:, t:t + 1],
                                ALU.subtract, ALU.mult).then_inc(xn_ready, 1)
            v.wait_ge(w_in, 96)
            v.wait_ge(m_in, 48)
            v.tensor_reduce(AM[:, 0:1], WQ[:, 0, :], AX.X, ALU.max, apply_absolute_value=True)
            v.tensor_reduce(AM[:, 1:2], mat(WD2), AX.X, ALU.max, apply_absolute_value=True)
            v.tensor_reduce(AM[:, 2:3], WKU[:, 0, :], AX.X, ALU.max, apply_absolute_value=True)
            v.tensor_reduce(AM[:, 3:4], mat(W_FFN), AX.X, ALU.add, apply_absolute_value=True).then_inc(am_ready, 1)
            v.tensor_copy(IDB[:, :], mat(IDENT))
            v.tensor_copy(IDH[:, :], mat(IDENT))
            v.tensor_copy(MK[:, 0, :], mat(MASK_QK))
            v.tensor_copy(MK[:, 1, :], mat(MASK_KQ)).then_inc(const_ready, 1)
            v.wait_ge(amg_ready, 2)
            link(v.tensor_scalar(AMG[:, 0:3], AMG[:, 0:3], 1e-30, None, ALU.max))
            link(v.tensor_scalar(EX[:, 0:3].bitcast(I32), AMG[:, 0:3].bitcast(I32), 0x7F800000, None,
                                 ALU.bitwise_and))
            link(v.reciprocal(IV[:, 0:3], EX[:, 0:3]))
            v.tensor_scalar(WT[:, 0:P], mat(WD2), IV[:, 1:2], None, ALU.mult).then_inc(wd_ready, 1)
            link(v.tensor_scalar(SC[:, 1:2], EX[:, 0:1], EX[:, 1:2], HD ** -0.5, ALU.mult, ALU.mult))
            link(v.tensor_scalar(SC[:, 0:1], SC[:, 1:2], EX[:, 2:3], None, ALU.mult))
            for c in range(NCH):
                cs = slice(c * CH, (c + 1) * CH)
                v.wait_ge(xt_copied, c + 1)
                link(v.tensor_copy(XH[:, cs], XNT[:, cs]))
                v.tensor_tensor(XL[:, cs], XNT[:, cs], XH[:, cs], ALU.subtract).then_inc(split_ready, 1)
            for c in range(NCH):
                cs = slice(c * CH, (c + 1) * CH)
                bank = ST[:, c // 2, c % 2, :]
                v.wait_ge(latt_ready, c + 1)
                link(v.tensor_copy(LT[:, cs], bank))
                v.tensor_tensor(LT[L:P, cs], bank[L:P, :], LT[L:P, cs], ALU.subtract).then_inc(latt_used, 1)
            for k, (raw, hi, lo) in enumerate(((WQ, WQH, WQL), (WKU, WKH, WKL))):
                iv = IV[:, 2 * k:2 * k + 1]
                for j in range(2):
                    link(v.tensor_scalar(hi[:, j, :], raw[:, j, :], iv, None, ALU.mult))
                    link(v.scalar_tensor_tensor(out=lo[:, j, :], in0=raw[:, j, :], scalar=iv, in1=hi[:, j, :],
                                                op0=ALU.mult, op1=ALU.subtract))
            for g in range(2):
                v.wait_ge(lats_ready, g + 1)
                bank = WK[:, g, :].rearrange("p (t l) -> p t l", l=L)
                link(v.tensor_copy(LS[:, 8 * g:8 * g + 8, 0, :], bank))
                v.tensor_tensor(LS[:, 8 * g:8 * g + 8, 1, :], bank, LS[:, 8 * g:8 * g + 8, 0, :],
                                ALU.subtract).then_inc(lats_used, 1)
            for q in range(4):
                v.wait_ge(gg_ready, q + 1)
                v.tensor_scalar(GG[:, q * CH:(q + 1) * CH], (OU, RS)[q % 2][:, :], EX[:, 1:2], None, ALU.mult)\
                    .then_inc(gg_used, 1)
            for t in range(NT):
                last = v.bn_stats(ST6[:, t, :], XN[:, t, :])
            link(last)
            for t in range(NT):
                last = v.bn_aggr(MV[:, t, :], ST6[:, t, :])
            last.then_inc(var_ready, 1)
            v.wait_ge(std_ready, 2)
            link(v.reciprocal(RD[:, :], SD[:, :]))
            for t in range(NT):
                last = v.tensor_scalar(Z[:, t, :], XN[:, t, :], MV[:, t, 0:1], RD[:, t:t + 1],
                                       ALU.subtract, ALU.mult)
            link(last)
            for t in range(NT):
                last = v.tensor_tensor(Z[:, t, :], Z[:, t, :], mat(GAMMA), ALU.mult)
            link(last)
            for t in range(NT):
                last = v.tensor_tensor(Z[:, t, :], Z[:, t, :], mat(BETA), ALU.add)
            link(last)
            v.tensor_reduce(AM[:, 0:1], Z[:, :, :], AX.XY, ALU.max, apply_absolute_value=True)\
                .then_inc(zmax_ready, 1)
            v.wait_ge(zmaxg_ready, 1)
            link(v.reciprocal(SC[:, 2:3], AMG[:, 0:1]))
            link(v.tensor_scalar(SC[:, 2:3], SC[:, 2:3], QB, None, ALU.mult))
            link(v.tensor_scalar(Z[:, :, :], Z[:, :, :], SC[:, 2:3], QB - EPS, ALU.mult, ALU.min))
            for t in range(NT):
                v.tensor_scalar(Z[:, t, :], Z[:, t, :], EPS - QB, None, ALU.max).then_inc(z_ready, 1)
            link(v.tensor_scalar(SC[:, 3:4], AMG[:, 3:4], 1.0 / (D * D), None, ALU.mult))
            link(v.tensor_scalar(SC[:, 4:5], SC[:, 3:4], EPS, None, ALU.add))
            link(v.reciprocal(SC[:, 4:5], SC[:, 4:5]))
            link(v.tensor_scalar(WT[:, P:2 * P], mat(W_FFN), SC[:, 4:5], 1.0, ALU.mult, ALU.min))
            link(v.tensor_scalar(WT[:, P:2 * P], WT[:, P:2 * P], -1.0, 12582912.0, ALU.max, ALU.add))
            v.tensor_scalar(WT[:, P:2 * P], WT[:, P:2 * P], -12582912.0, None, ALU.add).then_inc(wf_ready, 1)
            link(v.tensor_scalar(SC[:, 5:6], AMG[:, 0:1], SC[:, 3:4], 1.0 / QB, ALU.mult, ALU.mult))
            for c in range(NCH):
                v.wait_ge(ffn_ready, c + 1)
                v.scalar_tensor_tensor(out=ACC[:, 4 * c:4 * c + 4, :].rearrange("p t d -> p (t d)"),
                                       in0=ST[:, c // 2, c % 2, :], scalar=SC[:, 5:6],
                                       in1=X[:, 4 * c:4 * c + 4, :].rearrange("p t d -> p (t d)"),
                                       op0=ALU.mult, op1=ALU.add).then_inc(acc_ready, 1)

            v.wait_ge(t_in, 32)

            def max_of(p, n, h):
                t, k, w = PIECES[p]
                v.wait_ge(max_ready, h * MAXES + p + 1)
                v.tensor_reduce(MP[:, t, k // CH:k // CH + 1], WK[:, bank_of(n), 0:w], AX.X, ALU.max)\
                    .then_inc(piece_done, 1)

            def mparts(h):
                v.wait_ge(piece_done, h * MAXES + MAXES)
                v.tensor_reduce(NM[:, :], MP[:, :, :], AX.X, ALU.max).then_inc(mneg_ready, 1)
                v.wait_ge(mneg_ready, h * 2 + 1)
                v.tensor_scalar(MM[:, 0, :], NM[:, :], -1.0 / MSHIFT, None, ALU.mult).then_inc(mneg_ready, 1)
                v.wait_ge(mneg_ready, h * 2 + 2)
                v.scalar_tensor_tensor(out=MM[:, 1, :], in0=NM[:, :], scalar=-1.0 / MSHIFT, in1=MM[:, 0, :],
                                       op0=ALU.mult, op1=ALU.subtract).then_inc(mparts_ready, 1)

            def mrow_copy(n, h):
                v.wait_ge(mrow_ready, h + 1)
                v.tensor_copy(MT[:, :], WK[:, bank_of(n), :].bitcast(F16)[0:2 * NT, 0:P])\
                    .then_inc(mt_copied, 1)

            def low_of(g, units):
                c, k0 = UNIT[g % UNITS]
                b = g % PBUF
                v.wait_ge(probs_ready, units + g + 1)
                if k0 < 4 * c:
                    last = v.tensor_tensor(PL[:, b, :, :], PR[:, b, :, :], PH[:, b, :, :], ALU.subtract)
                else:
                    for j in range(2):
                        n0 = (k0 + j - 4 * c) * P
                        last = v.tensor_tensor(PL[:, b, j, n0:CH], PR[:, b, j, n0:CH], PH[:, b, j, n0:CH],
                                               ALU.subtract)
                last.then_inc(low_probs, 1)

            def recip(ch, n, chunks):
                v.wait_ge(sum_ready, chunks + ch + 1)
                v.reciprocal(RL[:, ch % 2, :], WK[:, bank_of(n), 0:4]).then_inc(rl_ready, 1)

            def add_out(ch, n, chunks):
                c = ch % NCH
                v.wait_ge(out_ready, chunks + ch + 1)
                v.wait_ge(rl_ready, chunks + ch + 1)
                v.wait_ge(acc_ready, chunks + ch + NCH)
                for t in range(4):
                    a = ACC[:, 4 * c + t, :]
                    last = v.scalar_tensor_tensor(out=a, in0=WK[:, bank_of(n), t * P:(t + 1) * P],
                                                  scalar=RL[:, ch % 2, t:t + 1], in1=a,
                                                  op0=ALU.mult, op1=ALU.add)
                last.then_inc(acc_ready, 1)

            def works(items, i, e):
                h = i * 2 + e + 1
                for kind, a, n in items:
                    if kind == "max":
                        if a == 0:
                            v.wait_ge(mneg_ready, h * 2)
                        max_of(a, n, h)
                        if a == MAXES - 1:
                            v.wait_ge(mrow_ready, h)
                            mparts(h)
                    elif kind == "mrow":
                        v.wait_ge(mrow_stacked, h * 32)
                        mrow_copy(n, h)
                    elif kind == "sum":
                        recip(a, n, i * (2 * NCH))
                    elif kind == "out":
                        add_out(a, n, i * (2 * NCH))

            def pair(i, slots):
                for w, (before, after) in enumerate(slots):
                    low_of(w, i * (2 * UNITS))
                    works(before, i, w // UNITS)
                    works(after, i, w // UNITS)

            for n, (kind, a) in enumerate(PROLOGUE_WORKS):
                if kind == "rope":
                    r, c, swapped = a, a // 2 % NCH, a % 2
                    v.wait_ge(rope_ready, r + 1)
                    if r >= 2 and swapped == 0:
                        v.wait_ge(low_ready, r // 2)
                    v.tensor_tensor(RB[:, swapped, :], WK[:, bank_of(n), :],
                                    (COS, SIN)[swapped][:, c * CH:(c + 1) * CH], ALU.mult)\
                        .then_inc(rope_product, 1)
                elif kind == "max":
                    max_of(a, n, 0)
                    if a == MAXES - 1:
                        mparts(0)
                else:
                    mrow_copy(n, 0)
            with v.Fori(0, PAIRS - 1) as i:
                pair(i, BODY)
            pair(PAIRS - 1, LAST)

            v.wait_ge(acc_ready, H * NCH + 4)
            for t in range(NT):
                last = v.bn_stats(ST6[:, t, :], ACC[:, t, :])
            link(last)
            for t in range(NT):
                last = v.bn_aggr(MV[:, t, :], ST6[:, t, :])
            last.then_inc(x1_stats, 1)
            v.wait_ge(x1_std, 1)
            link(v.reciprocal(RD[:, :], SD[:, :]))
            for t in range(NT):
                v.tensor_scalar(XN[:, t, :], ACC[:, t, :], MV[:, t, 0:1], RD[:, t:t + 1],
                                ALU.subtract, ALU.mult).then_inc(x1n, 1)
            v.wait_ge(m1_ready, 1)
            v.tensor_tensor(WT[:, 0:D], OU[:, 0:D], mat(BLK), ALU.mult).then_inc(m1_copied, 1)
            v.wait_ge(m1_ready, 2)
            v.tensor_copy(WT[:, D:2 * D], OU[:, 0:D]).then_inc(m1_copied, 1)
            v.wait_ge(m1_ready, 3)
            v.tensor_copy(GG[:, 0:D], OU[:, 0:D]).then_inc(m1_copied, 1)
            link(v.tensor_scalar(TC[:, 10:11], CO[:, C_B4:C_B4 + 1], 0.5, None, ALU.mult))
            link(v.tensor_scalar(TC[:, 11:12], CO[:, G_B3:G_B3 + 1], 0.5, None, ALU.mult))
            v.wait_ge(x1t_copied, 4)
            link(v.tensor_reduce(TC[:, 7:8], XNT[:, :], AX.X, ALU.add))
            v.tensor_scalar(TC[:, 4:5], TC[:, 7:8], 1.0 / S, None, ALU.mult).then_inc(gc_done, 1)
            v.wait_ge(gc_act, 3)
            link(v.tensor_scalar(TC[:, 8:9], TC[:, 7:8], 0.7, None, ALU.mult))
            link(v.tensor_scalar(TC[:, 0:1], TC[:, 8:9], CO[:, AR:AR + 1], 0.1, ALU.mult, ALU.add))
            link(v.tensor_scalar(TC[:, 1:2], CO[:, AR:AR + 1], 0.3, None, ALU.mult))
            for n in range(3 * NCH):
                c = n % NCH
                cs = slice(c * CH, (c + 1) * CH)
                src = XNT if n < NCH else COS
                v.wait_ge(cn_act, 4 * n + 4)
                link(v.tensor_scalar(RB[:, 1, :], RB[:, 1, :], TC[:, 1:2], TC[:, 0:1], ALU.mult, ALU.add))
                link(v.tensor_tensor(RB[:, 1, :], RB[:, 1, :], WK[:, c % 2, :], ALU.mult))
                v.tensor_tensor(COS[:, cs], src[:, cs], RB[:, 1, :], ALU.add).then_inc(cn_out, 1)
            for c in range(NCH):
                v.wait_ge(y_ready, c + 1)
                v.tensor_tensor(X[:, 4 * c:4 * c + 4, :].rearrange("p t d -> p (t d)"),
                                ACC[:, 4 * c:4 * c + 4, :].rearrange("p t d -> p (t d)"),
                                ST[:, c // 2, c % 2, :], ALU.add).then_inc(y_done, 1)

        @block.scalar
        def _(act):
            act.wait_ge(var_ready, 1)
            act.activation(SD[:, :], MV[:, :, 1], ACT.Sqrt, bias=EPSC[:, 0:1]).then_inc(std_ready, 1)
            for c in range(NCH):
                act.wait_ge(xnt_ready, c + 1)
                act.activation(XNT[:, c * CH:(c + 1) * CH], ST[:, c // 2, c % 2, :], ACT.Copy)\
                    .then_inc(xt_copied, 1)
            act.wait_ge(var_ready, 2)
            act.activation(SD[:, :], MV[:, :, 1], ACT.Sqrt, bias=EPSC[:, 1:2]).then_inc(std_ready, 1)
            for c in range(NCH):
                act.wait_ge(zt_ready, c + 1)
                act.wait_ge(lats_ready, 2)
                act.wait_ge(split_ready, NCH)
                act.activation(ZT[:, c * CH:(c + 1) * CH], ST[:, c // 2, c % 2, :], ACT.Copy)\
                    .then_inc(zt_copied, 1)

            def high(k, n):
                kind, c = divmod(k, NCH)
                act.wait_ge(rope_summed, n + 1)
                act.activation(SG[:, 2 * kind, c * CH:(c + 1) * CH], RB[:, 0, :], ACT.Copy).then_inc(high_ready, 1)

            def probs(g, units):
                c, k0 = UNIT[g % UNITS]
                act.wait_ge(scores_ready, units + g + 1)
                act.wait_ge(unit_summed, units + g + 1)
                if k0 < 4 * c:
                    last = act.activation(PR[:, g % PBUF, :, :], ST[:, g % 2, :, :], ACT.Exp, scale=SC[:, 0:1])
                else:
                    for j in range(2):
                        n0 = (k0 + j - 4 * c) * P
                        last = act.activation(PR[:, g % PBUF, j, n0:CH], ST[:, g % 2, j, n0:CH], ACT.Exp,
                                              scale=SC[:, 0:1])
                last.then_inc(probs_ready, 1)

            def copy_chunk(ch, w, i):
                act.wait_ge(unit_summed, i * (2 * UNITS) + PBUF + w + 1)
                if ch >= 2:
                    act.wait_ge(out_ready, i * (2 * NCH) + ch - 1)
                else:
                    act.wait_ge(acc_ready, i * (2 * NCH) + NCH)
                rows_ = HD if ch % NCH == 0 else P
                act.activation(RSS[0:rows_, ch % 2, :], RS[0:rows_, :], ACT.Copy)
                act.activation(OS[:, ch % 2, :], OU[:, :], ACT.Copy).then_inc(chunk_copied, 1)

            def rope_copy(r, n, i):
                act.wait_ge(rope_ready, i * ROPES + ROPES + r + 1)
                act.wait_ge(rope_product, i * ROPES + ROPES + r - 1)
                act.activation(RA[:, r % 2, :], WK[:, bank_of(n), :], ACT.Copy).then_inc(rope_copied, 1)

            def pair(i, slots, more):
                for w, (before, after) in enumerate(slots):
                    if more and w >= HIGH_LAG and w % 2 == 0 and (w - HIGH_LAG) // 2 < 2 * NCH:
                        k = (w - HIGH_LAG) // 2
                        if k == 0:
                            act.wait_ge(stacked[0], i * 96 + 96)
                            act.wait_ge(stacked[1], i * 96 + 96)
                        high(k, i * (2 * NCH) + 2 * NCH + k)
                    for kind, a, n in before:
                        if kind == "rope":
                            rope_copy(a, n, i)
                    if w + LAG < 2 * UNITS or more:
                        probs(w + LAG, i * (2 * UNITS))
                    if w % UNITS in CHUNK_END:
                        copy_chunk(w // UNITS * NCH + CHUNK_END[w % UNITS], w, i)

            for k in range(2 * NCH):
                high(k, k)
            for g in range(LAG):
                probs(g, 0)
            with act.Fori(0, PAIRS - 1) as i:
                pair(i, BODY, True)
            pair(PAIRS - 1, LAST, False)

            act.wait_ge(x1_stats, 1)
            act.activation(SD[:, :], MV[:, :, 1], ACT.Sqrt, bias=EPSC[:, 0:1]).then_inc(x1_std, 1)
            for c in range(NCH):
                act.wait_ge(x1t, c + 1)
                act.activation(XNT[:, c * CH:(c + 1) * CH], ST[:, c // 2, c % 2, :], ACT.Copy)\
                    .then_inc(x1t_copied, 1)
            act.wait_ge(gc_mm, 1)
            act.activation(TC[0:64, 5:6], RS[0:64, 0:1], ACT.Gelu, bias=CO[0:64, G_B1:G_B1 + 1]).then_inc(gc_act, 1)
            act.wait_ge(gc_mm, 2)
            act.activation(TC[0:32, 6:7], RS[0:32, 0:1], ACT.Gelu, bias=CO[0:32, G_B2:G_B2 + 1]).then_inc(gc_act, 1)
            act.wait_ge(gc_mm, 3)
            act.activation(TC[:, 7:8], RS[:, 0:1], ACT.Tanh, bias=TC[:, 11:12], scale=0.5).then_inc(gc_act, 1)
            for n in range(3 * NCH):
                c = n % NCH
                bank = ST[:, c // 2, c % 2, :]
                act.wait_ge(cn_mm, 4 * n + 1)
                act.activation(RA[:, 0, :], bank, ACT.Gelu, bias=CO[:, C_B1:C_B1 + 1]).then_inc(cn_act, 1)
                act.wait_ge(cn_mm, 4 * n + 2)
                act.activation(RA[0:64, 1, :], bank[0:64, :], ACT.Gelu, bias=CO[0:64, C_B2:C_B2 + 1])\
                    .then_inc(cn_act, 1)
                act.wait_ge(cn_mm, 4 * n + 3)
                act.activation(RB[0:32, 0, :], bank[0:32, :], ACT.Gelu, bias=CO[0:32, C_B3:C_B3 + 1])\
                    .then_inc(cn_act, 1)
                act.wait_ge(cn_mm, 4 * n + 4)
                if n:
                    act.wait_ge(cn_out, n)
                act.activation(RB[:, 1, :], bank, ACT.Tanh, bias=TC[:, 10:11], scale=0.5).then_inc(cn_act, 1)

        @block.gpsimd
        def _(pool):
            pool.wait_ge(am_ready, 1)
            pool.partition_all_reduce(AMG[:, 0:3], AM[:, 0:3], P, bass.bass_isa.ReduceOp.max).then_inc(amg_ready, 1)
            pool.partition_all_reduce(AMG[:, 3:4], AM[:, 3:4], P, bass.bass_isa.ReduceOp.add).then_inc(amg_ready, 1)
            pool.wait_ge(zmax_ready, 1)
            pool.partition_all_reduce(AMG[:, 0:1], AM[:, 0:1], P, bass.bass_isa.ReduceOp.max)\
                .then_inc(zmaxg_ready, 1)

            def rotated(k):
                kind, c = divmod(k, NCH)
                return 2 * kind, slice(c * CH, (c + 1) * CH)

            def add(k, n):
                pool.wait_ge(rope_product, n * 2 + 2)
                pool.tensor_tensor(RB[:, 0, :], RB[:, 0, :], RB[:, 1, :], ALU.add).then_inc(rope_summed, 1)

            def low(k, n):
                part, cs = rotated(k)
                pool.wait_ge(high_ready, n + 1)
                pool.tensor_tensor(SG[:, part + 1, cs], RB[:, 0, :], SG[:, part, cs], ALU.subtract)\
                    .then_inc(low_ready, 1)

            for k in range(2 * NCH):
                add(k, k)
                low(k, k)
            with pool.Fori(0, PAIRS - 1) as i:
                for k in range(2 * NCH):
                    part, cs = rotated(k)
                    n = i * (2 * NCH) + 2 * NCH + k
                    pool.wait_ge(low_ready, n)
                    for j, table in enumerate((COS, SIN)):
                        pool.wait_ge(rope_copied, i * ROPES + 2 * k + j + 1)
                        pool.tensor_tensor(RB[:, j, :], RA[:, j, :], table[:, cs], ALU.mult)\
                            .then_inc(rope_product, 1)
                    add(k, n)
                    low(k, n)


def causal(transposed):
    import numpy as np
    m = np.triu(np.full((P, P), NEG, np.float32), 1)
    return m.T if transposed else m


def rotary():
    import numpy as np
    inv = (1.0 / np.float32(10000.0) ** (np.arange(0, HD, 2, dtype=np.float32) / np.float32(HD))).astype(np.float32)
    ang = (np.arange(S, dtype=np.float32)[None, :] * inv[:, None]).astype(np.float64)
    cos, sin = np.cos(ang).astype(np.float32), np.sin(ang).astype(np.float32)
    return np.concatenate([cos] * 4), np.concatenate([-sin, sin] * 2)


def twist():
    import numpy as np
    m = np.zeros((D, D), np.float32)
    for target, (source, sign) in enumerate(((2, 1), (3, -1), (0, -1), (1, 1))):
        for j in range(32):
            m[source * 32 + j, target * 32 + j] = sign
    return m


def kernel(**inputs):
    import numpy as np
    import concourse.bacc as bacc
    from concourse import mybir as mb
    from concourse.bass_utils import run_bass_kernel_spmd as run

    g = {k: np.asarray(v) for k, v in inputs.items()}

    def swapped(w):
        return w.reshape(H, 2, HD // 2, -1)[:, ::-1].reshape(H * HD, -1)

    def wide(a):
        a = a if a.ndim == 2 else a[None, :]
        full = np.zeros((P, D), np.float32)
        full[:a.shape[0], :a.shape[1]] = a
        return full

    def every(v, n=P):
        return np.broadcast_to(v.reshape(1, -1), (n, v.size))

    q1, v1 = (g[f"L1_attn_{n}_weight"].reshape(D, D) for n in "qv")
    wd = g["L0_attn_w_kv_down"].T
    blocks = np.kron(np.eye(H, dtype=np.float32), np.full((D // H, D // H), (D // H) ** -0.5, np.float32))
    c, z = "L1_ffn_cn_", "L1_ffn_gc_"
    mats = [np.eye(P, dtype=np.float32), np.concatenate([wd, wd], 1), g["L0_ffn_weight"],
            every(g["L0_ffn_ln_gamma"]), every(g["L0_ffn_ln_beta"]), causal(False), causal(True),
            q1, q1.T, v1, g["L1_attn_out_w"].T, blocks, twist(),
            g[c + "w1"], g[c + "w2"], g[c + "w3"], np.broadcast_to(g[c + "w4"], (32, P)),
            g[z + "w1"], g[z + "w2"], np.broadcast_to(g[z + "w3"], (32, P))]
    vecs = [g[c + "b1"], g[c + "b2"], g[c + "b3"], np.broadcast_to(g[c + "b4"], (P,)),
            g[z + "b1"], g[z + "b2"], np.broadcast_to(g[z + "b3"], (P,)),
            np.broadcast_to(g["L1_ffn_adaptive_range"], (P,))]
    cols = np.zeros((P, len(vecs)), np.float32)
    for n, vec in enumerate(vecs):
        cols[:vec.size, n] = vec
    cos, sin = rotary()
    wq, wk = g["L0_attn_wq"], g["L0_attn_w_k_up"]
    arrays = dict(
        x=g["L0_attn_x"][0], wqT=wq.T, wqpT=swapped(wq).T, wkT=wk.T, wkpT=swapped(wk).T,
        wv=g["L0_attn_w_v_up"], woT=g["L0_attn_wo"].T, mats=np.concatenate([wide(m) for m in mats], 1),
        cols=cols, rows=np.concatenate([g["L1_attn_out_b"], np.ones(P, np.float32)])[None, :],
        cosT=cos, sinT=sin)
    nc = bacc.Bacc("TRN2", target_bir_lowering=False, num_devices=1)
    arrays = {k: np.ascontiguousarray(a) for k, a in arrays.items()}
    args = {k: nc.dram_tensor(k, a.shape, mb.dt.from_np(a.dtype), kind="ExternalInput").ap()
            for k, a in arrays.items()}
    args["out"] = nc.dram_tensor("out", (S, D), F32, kind="ExternalOutput").ap()
    build(nc, **args)
    r = run(nc, [arrays], core_ids=[0])
    return np.asarray(r.results[0]["out"]).reshape(1, S, D)
```

```python
from contextlib import ExitStack

import concourse.bass as bass
from concourse import mybir

F32 = mybir.dt.float32
BF16 = mybir.dt.bfloat16
F16 = mybir.dt.float16
I32 = mybir.dt.int32
ALU = mybir.AluOpType
ACT = mybir.ActivationFunctionType
AX = mybir.AxisListType

P = 128
S = 2048
D = 128
H = 16
HD = 64
L = 64
PAIRS = H // 2
CH = 512
NCH = S // CH
NT = S // P
UNITS = sum((4 * c + 4) // 2 for c in range(NCH))
LAG = 3
WORK_BANKS = 3
POOL_UNITS = (26, 28, 32, 34, 36)
HIGH_LAG = 3
PBUF = 4
RA_BUFS = 4
MSHIFT = 2048.0
SUM_SCALE = 32.0
TWIST_SIGNS = (1.0, -1.0, -1.0, 1.0)
NEG = -1.0e30
LN_EPS, FFN_EPS, EPS, QB = 1e-5, 1e-3, 1e-5, 128.0
CYCLES = 3

UNIT = [(c, k) for c in range(NCH) for k in range(0, 4 * c + 4, 2)]
CHUNK_END = {u: c for u, (c, k) in enumerate(UNIT) if k == 4 * c + 2}
PIECES = [(t, k, min(CH, (t + 1) * P - k)) for t in range(NT) for k in range(0, (t + 1) * P, CH)]
MAXES = len(PIECES)
PER_SLOT = 2
AHEAD = 13
ROPES = 4 * NCH
ROPE_FIRST = 5
SUM_LAG, OUT_LAG = 3, 4
SLOTS = 2 * UNITS
START = 5
CHUNK_MAXED = {max(p for p, (t, _, _) in enumerate(PIECES) if t // 4 == c): c for c in range(NCH)}


def works_of_slot(w, more):
    def pieces(w):
        e, p = divmod((w + AHEAD) * PER_SLOT, MAXES)
        return [(e, p + j) for j in range(PER_SLOT)] if e < 2 or more else []

    first, second, last = [], [], []
    for e, p in pieces(w - 1):
        if p in CHUNK_MAXED:
            first.append(("mrow", CHUNK_MAXED[p], e))
    for (e, p), place in zip(pieces(w), (first, second)):
        place.append(("max", p, e))
    if more and 0 <= w - ROPE_FIRST < ROPES:
        second.append(("rope", w - ROPE_FIRST, 2))
    for lag, kind in ((SUM_LAG, "sum"), (OUT_LAG, "out")):
        e, u = divmod(w - lag, UNITS)
        if e >= 0 and (e < 2 or more) and u in CHUNK_END:
            last.append((kind, CHUNK_END[u], e))
    return first, second, last


def plan(slots, first, more):
    n, uses = first, {}
    for w in slots:
        uses[w] = []
        for place in works_of_slot(w, more):
            uses[w].append([(*use, n + j) for j, use in enumerate(place)])
            n += len(place)
    return uses


def in_order(uses):
    return [use for w in uses for place in uses[w] for use in place]


PROLOGUE = [("rope", r) for r in range(ROPES)]
for _p in range(AHEAD * PER_SLOT):
    PROLOGUE += [("max", _p)] + ([("mrow", CHUNK_MAXED[_p])] if _p in CHUNK_MAXED else [])
POOL_LOWS = [{g - UNITS * e for g in POOL_UNITS if g // UNITS == e} for e in range(2)]


def pool_units(g):
    return g // SLOTS * len(POOL_UNITS) + sum(p < g % SLOTS for p in POOL_UNITS)


BODY = plan(range(START, SLOTS + START), 0, True)
LAST = plan(range(START, SLOTS + START), 0, False)
BEFORE = len(PROLOGUE) + len(in_order(plan(range(START), 0, True)))
FIRST = (len(in_order(BODY)) - BEFORE) % WORK_BANKS
PEELED = plan(range(START), FIRST + len(PROLOGUE), True)
PIECES_BEFORE = (START + AHEAD) * PER_SLOT
ROWS_BEFORE = sum(kind == "mrow" for kind, *_ in PROLOGUE + in_order(PEELED))


def build(nc, x, wqT, wqpT, wkT, wkpT, wv, woT, mats, cols, rows, cosT, sinT, out):
    with ExitStack() as ctx:
        def sb(name, shape, dt=F32):
            return ctx.enter_context(nc.sbuf_tensor(name, shape, dt))

        def ps(name, shape):
            return ctx.enter_context(nc.psum_tensor(name, shape, F32))

        def sem(name):
            return ctx.enter_context(nc.semaphore(name))

        ST = ps("ST", [P, 3, CH])
        WK = ps("WK", [P, WORK_BANKS, CH])
        OU = ps("OU", [P, CH])
        RS = ps("RS", [P, CH])

        X = sb("X", [P, NT, D])
        XN = sb("XN", [P, NT, D])
        ACC = sb("ACC", [P, NT, D])
        XNT = sb("XNT", [P, S])
        XH = sb("XH", [P, S], F16)
        XL = sb("XL", [P, S], F16)
        LT = sb("LT", [P, S], F16)
        LS = sb("LS", [P, NT, 2, L], F16)
        COS = sb("COS", [P, S])
        SIN = sb("SIN", [P, S])
        WQH = sb("WQH", [P, 2, H * HD], F16)
        WQL = sb("WQL", [P, 2, H * HD], F16)
        WKH = sb("WKH", [P, 2, H * HD], F16)
        WKL = sb("WKL", [P, 2, H * HD], F16)
        GGH = sb("GGH", [P, H * D], F16)
        GGL = sb("GGL", [P, H * D], BF16)
        MA = sb("MA", [P, mats.shape[1]])
        CO = sb("CO", [P, cols.shape[1]])
        RW = sb("RW", [1, rows.shape[1]])
        QS = sb("QS", [P, 2, S], F16)
        QM = sb("QM", [HD + 1, 2, S], F16)
        KK = sb("KK", [P, 2, S], F16)
        KL = sb("KL", [HD + 1, 2, S], F16)
        SG = sb("SG", [P, 4, S], F16)
        PR = sb("PR", [P, PBUF, 2, CH])
        PL = sb("PL", [P, PBUF, 2, CH], F16)
        SUMS = sb("SUMS", [P, 2, 2, CH])
        SUMH = sb("SUMH", [P, 2, 2, CH], F16)
        SUML = sb("SUML", [P, 2, 2, CH], BF16)
        RL = sb("RL", [P, 2, 4])
        MP = sb("MP", [P, NT, 4])
        NM = sb("NM", [P, NT])
        MM = sb("MM", [P, 2, 4], F16)
        MT = sb("MT", [4, 2, P], F16)
        ST6 = sb("ST6", [P, NT, 6])
        MV = sb("MV", [P, NT, 2])
        SD = sb("SD", [P, NT])
        RD = sb("RD", [P, NT])
        RD2 = sb("RD2", [P, NT])
        AM = sb("AM", [P, 6])
        AMG = sb("AMG", [P, 6])
        EX = sb("EX", [P, 6])
        IV = sb("IV", [P, 6])
        SC = sb("SC", [P, 8])
        TC = sb("TC", [P, 16])
        ONE = sb("ONE", [P, 32], BF16)
        IDB = sb("IDB", [P, P], BF16)
        IDH = sb("IDH", [P, P], F16)
        MK = sb("MK", [P, 2, P], BF16)
        SEL = sb("SEL", [P, 1])
        SELB = sb("SELB", [P, 1], BF16)
        EPSC = sb("EPSC", [P, 2])
        WT = sb("WT", [P, 2 * D])
        RAW = PR[:, :, :, :].rearrange("p b j n -> p (b j n)")
        WQ = RAW[:, 0:2 * H * HD].rearrange("p (a n) -> p a n", a=2)
        WKU = RAW[:, 2 * H * HD:4 * H * HD].rearrange("p (a n) -> p a n", a=2)
        WV = SUMS[0:HD, :, :, :].rearrange("p b s n -> p (b s n)").rearrange("p (h a l) -> p h a l", h=H, a=2)
        WO = PL[0:HD, :, :, :].bitcast(F32).rearrange("p b j n -> p (b j n)").rearrange("p (h m) -> p h m", h=H)
        Z = XN
        ZT = XNT
        RA = XN[:, :, :].rearrange("p (b t) d -> p b (t d)", b=RA_BUFS)
        RB = XNT[:, :].rearrange("p (b j n) -> p b j n", b=2, j=2)
        RB0 = ACC[:, :, :].rearrange("p (b j t) d -> p b j (t d)", b=2, j=2)
        TW = SG[:, 0:2, :].bitcast(F32).rearrange("p a n -> p (a n)")
        H1 = PR[:, :, 0, :]
        H2 = PR[:, 0:2, 1, :]
        H3 = PR[:, 2, 1, :]
        TH = PL[:, :, :, :].bitcast(F32).rearrange("p b j n -> p b (j n)")
        B4 = (ST[:, 0, :], ST[:, 1, :], ST[:, 2, :], WK[:, 2, :])
        LATS_BANKS = (OU, RS)
        GG_BANKS = (ST[:, 0, :], ST[:, 1, :], ST[:, 2, :], OU[:, :])
        ZT_BANKS = (RS[:, :], ST[:, 0, :], ST[:, 1, :], ST[:, 2, :])
        FFN_BANKS = (OU[:, :], RS[:, :], ST[:, 0, :], ST[:, 1, :])
        NB = (WK[:, 0, :], WK[:, 1, :], OU[:, :], RS[:, :])
        PH = PR[:, :, :, :].bitcast(BF16).rearrange("p b j (n two) -> p b j n two", two=2)[:, :, :, :, 1]

        def mat(n, rows_=P, cols_=D):
            return MA[0:rows_, n * D:n * D + cols_]

        (IDENT, WD2, W_FFN, GAMMA, BETA, MASK_QK, MASK_KQ, Q1, Q1T, V1, WO1T, BLK,
         CW1, CW2, CW3, CW4, GW1, GW2, GW3) = range(19)
        (C_B1, C_B2, C_B3, C_B4, G_B1, G_B2, G_B3, AR, SIGN) = range(9)

        x_in, w_in, m_in = sem("x_in"), sem("w_in"), sem("m_in")
        t_in, g_in = sem("t_in"), sem("g_in")
        dve = sem("dve_chain")
        pool = sem("pool_chain")
        var_ready, std_ready = sem("var_ready"), sem("std_ready")
        xn_ready, xnt_ready, xt_copied = sem("xn_ready"), sem("xnt_ready"), sem("xt_copied")
        split_ready, am_ready, amg_ready = sem("split_ready"), sem("am_ready"), sem("amg_ready")
        iv_ready, wd_ready, w0_high, w0_ready = sem("iv_ready"), sem("wd_ready"), sem("w0_high"), sem("w0_ready")
        latt_ready, latt_high, latt_used = sem("latt_ready"), sem("latt_high"), sem("latt_used")
        lats_ready, lats_high, lats_used = sem("lats_ready"), sem("lats_high"), sem("lats_used")
        gg_ready, gg_scale, gg_high, gg_used = sem("gg_ready"), sem("gg_scale"), sem("gg_high"), sem("gg_used")
        w_scaled, w_high, w_low = sem("w_scaled"), sem("w_high"), sem("w_low")
        const_ready, kl_ready = sem("const_ready"), sem("kl_ready")
        rd2_ready, z_scaled = sem("rd2_ready"), sem("z_scaled")
        z_ready, zt_ready, zt_copied = sem("z_ready"), sem("zt_ready"), sem("zt_copied")
        zmax_ready, zmaxg_ready, wf_ready = sem("zmax_ready"), sem("zmaxg_ready"), sem("wf_ready")
        ffn_ready = sem("ffn_ready")
        rope_ready, max_ready, mrow_ready = sem("rope_ready"), sem("max_ready"), sem("mrow_ready")
        sum_ready, out_ready = sem("sum_ready"), sem("out_ready")
        rope_copied, rope_product, rope_summed = sem("rope_copied"), sem("rope_product"), sem("rope_summed")
        high_ready, low_ready = sem("high_ready"), sem("low_ready")
        stacked = [sem("slot0_stacked"), sem("slot1_stacked")]
        stacked_low = [sem("slot0_low_stacked"), sem("slot1_low_stacked")]
        piece_done, mneg_ready, mparts_ready = sem("piece_done"), sem("mneg_ready"), sem("mparts_ready")
        mt_copied, mrow_stacked = sem("mt_copied"), [sem("mrow_stacked0"), sem("mrow_stacked1")]
        scores_ready, probs_ready = sem("scores_ready"), sem("probs_ready")
        low_probs, low_probs_pool = sem("low_probs"), sem("low_probs_pool")
        ou_copied, rs_copied, sums_high, sums_low = sem("ou_copied"), sem("rs_copied"), sem("sums_high"), sem("sums_low")
        unit_summed = sem("unit_summed")
        rl_ready, acc_ready = sem("rl_ready"), sem("acc_ready")
        x1_stats, x1_std, x1n, x1t, x1t_copied = (sem("x1_stats"), sem("x1_std"), sem("x1n"), sem("x1t"),
                                                  sem("x1t_copied"))
        m1_ready, m1_copied = sem("m1_ready"), sem("m1_copied")
        gc_mm, gc_act, gc_done = sem("gc_mm"), sem("gc_act"), sem("gc_done")
        layer1, layer2, layer3, layer4 = sem("layer1"), sem("layer2"), sem("layer3"), sem("layer4")
        h1_ready, h2_ready, h3_ready, th_ready = sem("h1_ready"), sem("h2_ready"), sem("h3_ready"), sem("th_ready")
        swapped_in, cn_out = [sem(f"swapped_in{c}") for c in range(NCH)], sem("cn_out")
        y_ready, y_done, stored = sem("y_ready"), sem("y_done"), sem("stored")

        block = ctx.enter_context(nc.Block())

        def bank_of(n):
            return n % WORK_BANKS

        def scores_bank(w, j):
            return (2 * (w % SLOTS) + j - 2 * START) % (2 * SLOTS) % 3

        def bank_read(kind, a, e, i):
            if kind == "rope":
                return rope_copied, i * ROPES + a + 1
            if kind == "max":
                return piece_done, i * (2 * MAXES) + e * MAXES + a + 1
            chunks = i * (2 * NCH) + e * NCH + a
            if kind == "mrow":
                return mt_copied, chunks + 1
            return (rl_ready, chunks + 1) if kind == "sum" else (acc_ready, chunks + NCH + 1)

        @block.sync
        def _(sp):
            sp.dma_start(X[:, :, :], x.rearrange("(t p) d -> p t d", p=P)).then_inc(x_in, 16)
            sp.dma_start(MA[:, :], mats).then_inc(m_in, 16)
            sp.dma_start(CO[:, :], cols).then_inc(m_in, 16)
            sp.dma_start(RW[:, :], rows).then_inc(m_in, 16)
            sp.dma_start(WQ[:, 0, :], wqT).then_inc(w_in, 16)
            sp.dma_start(WQ[:, 1, :], wqpT).then_inc(w_in, 16)
            for half in range(2):
                sp.dma_start(WKU[half * L:half * L + L, 0, :], wkT).then_inc(w_in, 16)
                sp.dma_start(WKU[half * L:half * L + L, 1, :], wkpT).then_inc(w_in, 16)
            sp.dma_start(COS[:, :], cosT).then_inc(t_in, 16)
            sp.dma_start(SIN[:, :], sinT).then_inc(t_in, 16)
            for half in range(2):
                sp.dma_start(WV[:, :, half, :], wv.rearrange("(h d) l -> d h l", d=HD)).then_inc(g_in, 16)
            sp.dma_start(WO[:, :, :], woT.rearrange("(h d) m -> d h m", d=HD)).then_inc(g_in, 16)

            def stack_q(slot, i, pair_):
                n = pair_ * (2 * NCH)
                q0 = slot * HD
                sp.wait_ge(high_ready, i * (2 * NCH) + (n + NCH))
                sp.wait_ge(low_ready, i * (2 * NCH) + (n + NCH))
                if pair_:
                    sp.wait_ge(scores_ready, 2 * (i * SLOTS + (slot + 1) * UNITS))
                sp.dma_start(QS[0:HD, slot, :], SG[q0:q0 + HD, 0, :]).then_inc(stacked[slot], 16)
                sp.dma_start(QS[HD:P, slot, :], SG[q0:q0 + HD, 1, :]).then_inc(stacked[slot], 16)

            def stack_k(slot, i, pair_):
                n, q0 = pair_ * (2 * NCH), slot * HD
                sp.wait_ge(high_ready, i * (2 * NCH) + (n + 2 * NCH))
                sp.dma_start(KK[0:HD, slot, :], SG[q0:q0 + HD, 2, :]).then_inc(stacked[slot], 16)
                sp.dma_start(KK[HD:P, slot, :], SG[q0:q0 + HD, 2, :]).then_inc(stacked[slot], 16)
                sp.dma_start(QM[0:HD, slot, :], SG[q0:q0 + HD, 0, :]).then_inc(stacked_low[slot], 16)
                sp.wait_ge(low_ready, i * (2 * NCH) + (n + 2 * NCH))
                sp.dma_start(KL[0:HD, slot, :], SG[q0:q0 + HD, 3, :]).then_inc(stacked_low[slot], 16)

            def mrow(i, e, c):
                sp.wait_ge(mt_copied, i * (2 * NCH) + e * NCH + c + 1)
                sp.dma_start(QM[HD:HD + 1, e % 2, c * CH:(c + 1) * CH], MT[:, c % 2, :]).then_inc(mrow_stacked[c % 2], 16)

            for slot in range(2):
                stack_q(slot, 0, 0)
                stack_k(slot, 0, 0)
            mrow(0, 0, 0)
            mrow(0, 0, 1)
            mrow(0, 0, 2)

            def pair(i, more):
                for e, c in ((0, 3), (1, 0), (1, 1)):
                    mrow(i, e, c)
                if more:
                    stack_q(0, i, 1)
                mrow(i, 1, 2)
                if more:
                    stack_k(0, i, 1)
                for e, c in ((1, 3),) + (((2, 0), (2, 1)) if more else ()):
                    mrow(i, e, c)
                if more:
                    stack_q(1, i, 1)
                    stack_k(1, i, 1)
                    mrow(i, 2, 2)

            with sp.Fori(0, PAIRS - 1) as i:
                pair(i, True)
            pair(PAIRS - 1, False)
            for n in range(CYCLES * NCH):
                c = n % NCH
                cs = slice(c * CH, (c + 1) * CH)
                if n < NCH:
                    sp.wait_ge(x1t_copied, c + 1)
                else:
                    sp.wait_ge(cn_out, n - NCH + 1)
                src = XNT if n < NCH else COS
                for half in range(2):
                    sp.dma_start(TW[64 * half:64 * half + 64, cs], src[64 - 64 * half:P - 64 * half, cs])\
                        .then_inc(swapped_in[c], 16)
            for c in range(NCH):
                sp.wait_ge(y_done, c + 1)
                sp.dma_start(out.rearrange("(t p) d -> p t d", p=P)[:, 4 * c:4 * c + 4, :],
                             X[:, 4 * c:4 * c + 4, :]).then_inc(stored, 16)
            sp.wait_ge(stored, 16 * NCH)

        @block.tensor
        def _(pe):
            def tile_T(src_tile, c, copied, n):
                bank = B4[c]
                for t in range(4):
                    mm = pe.transpose(bank[:, t * P:(t + 1) * P], src_tile(4 * c + t), mat(IDENT))
                mm.then_inc(n, 1)

            pe.wait_ge(m_in, 48)
            for c in range(NCH):
                pe.wait_ge(xn_ready, 4 * c + 4)
                tile_T(lambda t: XN[:, t, :], c, None, xnt_ready)
            pe.wait_ge(wd_ready, 1)
            for c in range(NCH):
                pe.wait_ge(xt_copied, c + 1)
                pe.matmul(B4[c], WT[:, 0:P], XNT[:, c * CH:(c + 1) * CH], start=True, stop=True).then_inc(latt_ready, 1)

            def latent_by_token():
                for g in range(2):
                    for t in range(8):
                        mm = pe.matmul(LATS_BANKS[g][:, t * L:(t + 1) * L],
                                       XNT[:, (8 * g + t) * P:(8 * g + t + 1) * P], WT[:, 0:L],
                                       start=True, stop=True, skip_group_check=True)
                    mm.then_inc(lats_ready, 1)

            def latent_to_model():
                pe.wait_ge(g_in, 48)
                pe.wait_ge(lats_used, 1)
                for h in range(H):
                    mm = pe.matmul(GG_BANKS[h // 4][:, h % 4 * D:(h % 4 + 1) * D],
                                   WV[:, h, :, :].rearrange("d a l -> d (a l)"), WO[:, h, :],
                                   start=True, stop=True, skip_group_check=True)
                    if h % 4 == 3:
                        mm.then_inc(gg_ready, 1)

            def ffn_transposes():
                pe.wait_ge(z_ready, 1)
                pe.wait_ge(lats_used, 2)
                for c in range(NCH):
                    if c:
                        pe.wait_ge(gg_used, c)
                    for t in range(4):
                        mm = pe.transpose(ZT_BANKS[c][:, t * P:(t + 1) * P], Z[:, 4 * c + t, :], mat(IDENT))
                    mm.then_inc(zt_ready, 1)

            def ffn():
                pe.wait_ge(wf_ready, 1)
                pe.wait_ge(gg_used, 4)
                for c in range(NCH):
                    pe.wait_ge(zt_copied, c + 1)
                    for t in range(4):
                        mm = pe.matmul(FFN_BANKS[c][:, t * P:(t + 1) * P],
                                       ZT[:, (4 * c + t) * P:(4 * c + t + 1) * P], WT[:, P:2 * P],
                                       start=True, stop=True, skip_group_check=True)
                    mm.then_inc(ffn_ready, 1)

            def rope(r, n, pair_):
                kind, c, swapped = r // (2 * NCH), r // 2 % NCH, r % 2
                bank = WK[:, bank_of(n), :]
                cs = slice(c * CH, (c + 1) * CH)

                def w(t):
                    return t[:, swapped, 0:P] if isinstance(pair_, int) and pair_ == 0 else t[:, swapped, bass.ds(pair_ * P, P)]
                if kind == 0:
                    pe.matmul(bank, w(WQH), XH[:, cs], start=True, stop=False)
                    pe.matmul(bank, w(WQH), XL[:, cs], start=False, stop=False)
                    mm = pe.matmul(bank, w(WQL), XH[:, cs], start=False, stop=True)
                else:
                    pe.matmul(bank, w(WKH), LT[:, cs], start=True, stop=False)
                    mm = pe.matmul(bank, w(WKL), LT[:, cs], start=False, stop=True)
                mm.then_inc(rope_ready, 1)

            def max_piece(p, n, slot):
                t, k, w = PIECES[p]
                bank = WK[:, bank_of(n), 0:w]
                diagonal = k + w == (t + 1) * P
                mm = pe.matmul(bank, QS[:, slot, t * P:(t + 1) * P], KK[:, slot, k:k + w],
                               start=True, stop=not diagonal)
                if diagonal:
                    mm = pe.matmul(WK[:, bank_of(n), w - P:w], IDB[:, :], MK[:, 0, :], start=False, stop=True)
                mm.then_inc(max_ready, 1)

            def mrow(c, n, chunks):
                pe.wait_ge(mparts_ready, chunks + 1)
                pe.transpose(WK[:, bank_of(n), :].bitcast(F16)[0:4, 0:P], MM[:, c % 2, :], IDH[:, :])\
                    .then_inc(mrow_ready, 1)

            def scores(g, j, units):
                slot, (c, k0) = g // UNITS % 2, UNIT[g % UNITS]
                k, n = k0 + j, scores_bank(g - LAG, j)
                n0 = max(0, k - 4 * c) * P
                q = slice(c * CH + n0, (c + 1) * CH)
                diagonal = k >= 4 * c
                at = (2 * (g - LAG - START) + j) % (2 * SLOTS)
                back = 3 if at >= 3 else at - max(b for b in range(-3, 0) if (b + 2 * SLOTS) % 3 == n)
                if not isinstance(units, int) or 2 * g + j >= back:
                    pe.wait_ge(probs_ready, 2 * (units + g) + j + 1 - back)
                pe.matmul(ST[:, n, n0:CH], KK[:, slot, k * P:(k + 1) * P], QS[:, slot, q], start=True, stop=False)
                mm = pe.matmul(ST[:, n, n0:CH], KL[:, slot, k * P:(k + 1) * P], QM[:, slot, q],
                               start=False, stop=not diagonal)
                if diagonal:
                    mm = pe.matmul(ST[:, n, n0:n0 + P], IDB[:, :], MK[:, 1, :], start=False, stop=True)
                mm.then_inc(scores_ready, 1)

            def values(g, chunks):
                c, k0 = UNIT[g % UNITS]
                new = k0 == 0 and g > 0
                if new:
                    pe.wait_ge(ou_copied, chunks)
                b = g % PBUF
                n0 = [max(0, k0 + j - 4 * c) * P for j in range(2)]
                for j in range(2):
                    pe.matmul(OU[:, n0[j]:CH], LS[:, k0 + j, :, :].rearrange("p a l -> p (a l)"),
                              PH[:, b, j, n0[j]:CH], start=(k0 + j == 0), stop=False, skip_group_check=True)
                for j in range(2):
                    pe.matmul(OU[HD * j:HD * j + HD, n0[j]:CH], LS[:, k0 + j, 0, :], PL[:, b, j, n0[j]:CH],
                              start=False, stop=(k0 == 4 * c + 2), skip_group_check=True)
                if new:
                    pe.wait_ge(rs_copied, chunks)
                for j in range(2):
                    row = 0 if c == 0 else 64 * j
                    for part, src in enumerate((PH, PL)):
                        mm = pe.matmul(RS[row + 32 * part:row + 32 * part + 32, n0[j]:CH], ONE[:, :],
                                       src[:, b, j, n0[j]:CH], start=(k0 == 0 and (j == 0 or c > 0)),
                                       stop=(k0 == 4 * c + 2), skip_group_check=True)
                mm.then_inc(unit_summed, 1)

            def sums(e, c, n):
                rows_ = HD if c == 0 else P
                for t in range(4):
                    for part in (SUMH, SUML):
                        mm = pe.matmul(WK[:, bank_of(n), t:t + 1], part[0:rows_, c % 2, 1, t * P:(t + 1) * P],
                                       SELB[0:rows_, :], start=part is SUMH, stop=part is SUML, skip_group_check=True)
                mm.then_inc(sum_ready, 1)

            def outs(e, c, n, i):
                at = bass.ds(i * (2 * D) + e * D, D) if not isinstance(i, int) else slice((2 * i + e) * D, (2 * i + e + 1) * D)
                for t in range(4):
                    o, ts = WK[:, bank_of(n), t * P:(t + 1) * P], slice(t * P, (t + 1) * P)
                    pe.matmul(o, SUMH[:, c % 2, 0, ts], GGH[:, at], start=True, stop=False, skip_group_check=True)
                    pe.matmul(o, SUMH[:, c % 2, 0, ts], GGL[:, at], start=False, stop=False, skip_group_check=True)
                    mm = pe.matmul(o, SUML[:, c % 2, 0, ts], GGH[:, at], start=False, stop=True, skip_group_check=True)
                mm.then_inc(out_ready, 1)

            def pair(i, slots, more, before=None):
                units = i * SLOTS
                used = list(before or [])

                def work(kind, a, e, n):
                    if len(used) < WORK_BANKS:
                        was = in_order(BODY)[len(used) - WORK_BANKS:][0]
                        assert was[0] == "max" or was[:2] == ("sum", 0)
                        if was[0] == "sum":
                            pe.wait_ge(rl_ready, i * (2 * NCH) + 1)
                        pe.wait_ge(piece_done, i * (2 * MAXES) + PIECES_BEFORE)
                        pe.wait_ge(mt_copied, i * (2 * NCH) + ROWS_BEFORE)
                    else:
                        was, b, f = used[-WORK_BANKS][:3]
                        pe.wait_ge(*((rope_product, b + 1) if f is None else bank_read(was, b, f, i)))
                    used.append((kind, a, e))
                    if kind == "rope":
                        rope(a, n, i + 1)
                    elif kind == "mrow":
                        mrow(a, n, i * (2 * NCH) + e * NCH + a)
                    elif kind == "max":
                        if a == 0:
                            pe.wait_ge(stacked[e % 2], i * 64 + 64 * (e // 2 + 1))
                        max_piece(a, n, e % 2)
                    elif kind == "sum":
                        pe.wait_ge(sums_low, i * (2 * NCH) + e * NCH + a + 1)
                        sums(e, a, n)
                    else:
                        outs(e, a, n, i)

                for w, (first, second, last) in slots.items():
                    g = w + LAG
                    made = g < SLOTS or more
                    for use in first:
                        work(*use)
                    if made:
                        c, k0 = UNIT[g % UNITS]
                        if k0 == 0:
                            if c == 0:
                                pe.wait_ge(stacked_low[g // UNITS % 2], i * 32 + 32 * (g // SLOTS) + 32)
                            pe.wait_ge(mrow_stacked[c % 2], i * 64 + 32 * (g // UNITS) + 16 * (c // 2) + 16)
                        scores(g, 0, units)
                    for use in second:
                        work(*use)
                    if made:
                        scores(g, 1, units)
                    if w < SLOTS or more:
                        (e, u) = divmod(w, UNITS)
                        c, k0 = UNIT[u]
                        if u in POOL_LOWS[e % 2]:
                            pe.wait_ge(low_probs_pool, i * len(POOL_UNITS) + pool_units(w) + 1)
                        else:
                            pe.wait_ge(low_probs, i * (SLOTS - len(POOL_UNITS)) + w - pool_units(w) + 1)
                        values(w, i * (2 * NCH) + e * NCH + c)
                    for use in last:
                        work(*use)

            pe.wait_ge(const_ready, 1)
            for n, (kind, a) in enumerate(PROLOGUE):
                if n >= WORK_BANKS:
                    was, b = PROLOGUE[n - WORK_BANKS]
                    pe.wait_ge({"rope": rope_product, "max": piece_done, "mrow": mt_copied}[was], b + 1)
                if kind == "rope":
                    if n == 0:
                        pe.wait_ge(w0_ready, 2)
                    if bank_of(n + FIRST) == 2:
                        pe.wait_ge(latt_used, NCH)
                    pe.wait_ge(split_ready, a // 2 % NCH + 1)
                    rope(a, n + FIRST, 0)
                    if a == 2 * NCH - 1:
                        latent_by_token()
                    if a == ROPES - 1:
                        latent_to_model()
                elif kind == "max":
                    if a == 0:
                        pe.wait_ge(stacked[0], 64)
                    max_piece(a, n + FIRST, 0)
                    if a == 19:
                        ffn_transposes()
                    if a == 22:
                        ffn()
                else:
                    mrow(a, n + FIRST, a)
            pe.wait_ge(acc_ready, NCH)
            pe.sem_inc(unit_summed, PBUF)
            pe.wait_ge(stacked_low[0], 32)
            pe.wait_ge(kl_ready, 1)
            for g in range(LAG):
                c, k0 = UNIT[g]
                if k0 == 0:
                    pe.wait_ge(mrow_stacked[c % 2], 16)
                scores(g, 0, 0)
                scores(g, 1, 0)
            pair(0, PEELED, True, before=[(kind, a, 0) for kind, a in PROLOGUE])
            with pe.Fori(0, PAIRS - 1) as i:
                pair(i, BODY, True)
            pair(PAIRS - 1, LAST, False)

            pe.wait_ge(ou_copied, H * NCH)
            pe.wait_ge(rs_copied, H * NCH)
            pe.matmul(OU[:, 0:D], mat(V1), mat(Q1), start=True, stop=True).then_inc(m1_ready, 1)
            pe.wait_ge(m1_copied, 1)
            pe.matmul(OU[:, 0:D], WT[:, 0:D], mat(WO1T), start=True, stop=True).then_inc(m1_ready, 1)
            pe.wait_ge(m1_copied, 2)
            pe.matmul(OU[:, 0:D], mat(Q1T), WT[:, D:2 * D], start=True, stop=True).then_inc(m1_ready, 1)
            pe.wait_ge(probs_ready, H * UNITS)
            pe.wait_ge(acc_ready, H * NCH + NCH)
            pe.wait_ge(m1_copied, 3)

            def layer_1(n):
                cs = slice(n % NCH * CH, (n % NCH + 1) * CH)
                if n < NCH:
                    pe.wait_ge(x1t_copied, n + 1)
                else:
                    pe.wait_ge(cn_out, n - NCH + 1)
                pe.matmul(NB[n % NCH], mat(CW1), (XNT if n < NCH else COS)[:, cs], start=True, stop=True)\
                    .then_inc(layer1, 1)

            def layer_2(cyc, p):
                pe.wait_ge(h1_ready, cyc * NCH + 2 * p + 2)
                for j in range(2):
                    mm = pe.matmul(NB[2 * p][64 * j:64 * j + 64, :], mat(CW2, P, 64), H1[:, 2 * p + j, :],
                                   start=True, stop=True, skip_group_check=True)
                mm.then_inc(layer2, 1)

            def layer_3(cyc):
                pe.wait_ge(h2_ready, 2 * cyc + 2)
                for c in range(NCH):
                    rows_ = slice(64 * (c % 2), 64 * (c % 2) + 64)
                    mm = pe.matmul(NB[1][32 * c:32 * c + 32, :], MA[rows_, CW3 * D:CW3 * D + 32], H2[rows_, c // 2, :],
                                   start=True, stop=True, skip_group_check=True)
                mm.then_inc(layer3, 1)

            def layer_4(cyc, c):
                pe.wait_ge(h3_ready, cyc + 1)
                rows_ = slice(32 * c, 32 * c + 32)
                pe.matmul(NB[c], MA[rows_, CW4 * D:(CW4 + 1) * D], H3[rows_, :], start=True, stop=True)\
                    .then_inc(layer4, 1)

            def attention(c):
                for t in range(4):
                    o = B4[c][:, t * P:(t + 1) * P]
                    pe.matmul(o, XNT[:, (4 * c + t) * P:(4 * c + t + 1) * P], WT[:, 0:D], start=t == 0, stop=False,
                              skip_group_check=True)
                    pe.matmul(o, RW[:, D:2 * D], RW[:, 0:D], start=False, stop=False, skip_group_check=True)

            def transposed(c):
                pe.wait_ge(x1n, 4 * c + 4)
                tile_T(lambda t: XN[:, t, :], c, None, x1t)

            transposed(0)
            transposed(1)
            layer_1(0)
            transposed(2)
            layer_1(1)
            transposed(3)
            layer_1(2)
            layer_1(3)
            for cyc in range(CYCLES):
                if cyc:
                    for c in range(NCH):
                        layer_1(cyc * NCH + c)
                layer_2(cyc, 0)
                if cyc == 0:
                    pe.wait_ge(gc_done, 1)
                    pe.matmul(B4[0][0:64, 0:1], mat(GW1, P, 64), TC[:, 4:5], start=True, stop=True)\
                        .then_inc(gc_mm, 1)
                layer_2(cyc, 1)
                if cyc == 0:
                    pe.wait_ge(gc_act, 1)
                    pe.matmul(B4[0][0:32, 0:1], mat(GW2, 64, 32), TC[0:64, 5:6], start=True, stop=True)\
                        .then_inc(gc_mm, 1)
                else:
                    attention(2 * cyc - 1)
                layer_3(cyc)
                if cyc == 0:
                    pe.wait_ge(gc_act, 2)
                    pe.matmul(B4[0][:, 0:1], mat(GW3, 32, P), TC[0:32, 6:7], start=True, stop=True)\
                        .then_inc(gc_mm, 1)
                    pe.wait_ge(gc_act, 3)
                if cyc < 2:
                    attention(2 * cyc)
                for c in range(NCH):
                    layer_4(cyc, c)
            for c in range(NCH):
                pe.wait_ge(cn_out, (CYCLES - 1) * NCH + c + 1)
                for t in range(4):
                    mm = pe.matmul(B4[c][:, t * P:(t + 1) * P], COS[:, (4 * c + t) * P:(4 * c + t + 1) * P],
                                   mat(IDENT), start=False, stop=True, skip_group_check=True)
                mm.then_inc(y_ready, 1)

        @block.vector
        def _(v):
            chain = [0]

            def link(ins):
                chain[0] += 1
                ins.then_inc(dve, 1)
                v.wait_ge(dve, chain[0])

            v.memset(EPSC[:, 0:1], LN_EPS)
            v.memset(EPSC[:, 1:2], FFN_EPS)
            v.memset(ONE[:, :], 1.0)
            link(v.memset(AM[:, :], 0.0))
            link(v.memset(SEL[:, :], 0.0))
            for q in range(4):
                last = v.memset(SEL[32 * q:32 * q + 1, :], 1.0)
            link(last)
            v.wait_ge(x_in, 16)
            for t in range(NT):
                last = v.bn_stats(ST6[:, t, :], X[:, t, :])
            link(last)
            for t in range(NT):
                last = v.bn_aggr(MV[:, t, :], ST6[:, t, :])
            last.then_inc(var_ready, 1)
            v.wait_ge(std_ready, 1)
            link(v.reciprocal(RD[:, :], SD[:, :]))
            for t in range(NT):
                v.tensor_scalar(XN[:, t, :], X[:, t, :], MV[:, t, 0:1], RD[:, t:t + 1],
                                ALU.subtract, ALU.mult).then_inc(xn_ready, 1)
            link(v.tensor_tensor(RD2[:, :], MV[:, :, 1], RD[:, :], ALU.mult))
            v.tensor_tensor(RD2[:, :], RD2[:, :], RD[:, :], ALU.mult).then_inc(var_ready, 1)
            v.wait_ge(m_in, 48)
            v.tensor_reduce(AM[:, 1:2], mat(WD2), AX.X, ALU.max, apply_absolute_value=True)
            v.wait_ge(w_in, 96)
            v.tensor_reduce(AM[:, 0:1], WQ[:, 0, :], AX.X, ALU.max, apply_absolute_value=True)
            v.tensor_reduce(AM[:, 2:3], WKU[:, 0, :], AX.X, ALU.max, apply_absolute_value=True).then_inc(am_ready, 1)
            v.wait_ge(std_ready, 2)
            v.reciprocal(RD2[:, :], SD[:, :]).then_inc(rd2_ready, 1)
            v.tensor_copy(IDB[:, :], mat(IDENT))
            v.tensor_copy(IDH[:, :], mat(IDENT))
            v.tensor_copy(MK[:, 0, :], mat(MASK_QK))
            v.tensor_copy(MK[:, 1, :], mat(MASK_KQ)).then_inc(const_ready, 1)

            def powers_of_two(a, b):
                link(v.tensor_scalar(AMG[:, a:b], AMG[:, a:b], 1e-30, None, ALU.max))
                link(v.tensor_scalar(EX[:, a:b].bitcast(I32), AMG[:, a:b].bitcast(I32), 0x7F800000, None,
                                     ALU.bitwise_and))
                return v.reciprocal(IV[:, a:b], EX[:, a:b])

            v.wait_ge(amg_ready, 1)
            powers_of_two(0, 3).then_inc(iv_ready, 1)
            v.wait_ge(iv_ready, 1)
            v.tensor_scalar(WT[:, 0:P], mat(WD2), IV[:, 1:2], None, ALU.mult).then_inc(wd_ready, 1)
            for c in range(NCH):
                cs = slice(c * CH, (c + 1) * CH)
                v.wait_ge(xt_copied, c + 1)
                v.tensor_tensor(XL[:, cs], XNT[:, cs], XH[:, cs], ALU.subtract).then_inc(split_ready, 1)
            for k, (raw, hi, lo) in enumerate(((WQ, WQH, WQL), (WKU, WKH, WKL))):
                v.wait_ge(w0_high, k + 1)
                v.scalar_tensor_tensor(out=lo[:, :, 0:P], in0=raw[:, :, 0:P], scalar=IV[:, 2 * k:2 * k + 1],
                                       in1=hi[:, :, 0:P], op0=ALU.mult, op1=ALU.subtract).then_inc(w0_ready, 1)
            for c in range(NCH):
                cs = slice(c * CH, (c + 1) * CH)
                v.wait_ge(latt_high, c + 1)
                v.tensor_tensor(LT[L:P, cs], B4[c][L:P, :], LT[L:P, cs], ALU.subtract).then_inc(latt_used, 1)
            link(v.tensor_scalar(SC[:, 1:2], EX[:, 0:1], EX[:, 1:2], HD ** -0.5, ALU.mult, ALU.mult))
            v.tensor_scalar(SC[:, 0:1], SC[:, 1:2], EX[:, 2:3], None, ALU.mult)

            def z_part_1():
                v.wait_ge(z_scaled, 1)
                link(v.tensor_tensor(Z[:, :, :], Z[:, :, :], mat(GAMMA).unsqueeze(1).to_broadcast([P, NT, D]), ALU.mult))
                link(v.tensor_tensor(Z[:, :, :], Z[:, :, :], mat(BETA).unsqueeze(1).to_broadcast([P, NT, D]), ALU.add))
                v.tensor_reduce(AM[:, 0:1], Z[:, :, :], AX.XY, ALU.max, apply_absolute_value=True)\
                    .then_inc(zmax_ready, 1)

            def z_part_2():
                v.wait_ge(zmaxg_ready, 1)
                link(v.reciprocal(SC[:, 2:3], AMG[:, 0:1]))
                link(v.tensor_scalar(SC[:, 2:3], SC[:, 2:3], QB, None, ALU.mult))
                link(v.tensor_scalar(Z[:, :, :], Z[:, :, :], SC[:, 2:3], QB - EPS, ALU.mult, ALU.min))
                v.tensor_scalar(Z[:, :, :], Z[:, :, :], EPS - QB, None, ALU.max).then_inc(z_ready, 1)

            def other_weights():
                v.wait_ge(g_in, 48)
                v.tensor_reduce(AM[0:HD, 3:4], WV[:, :, 0, :], AX.XY, ALU.max, apply_absolute_value=True)
                v.tensor_reduce(AM[0:HD, 4:5], WO[:, :, :], AX.XY, ALU.max, apply_absolute_value=True)
                v.tensor_reduce(AM[:, 5:6], mat(W_FFN), AX.X, ALU.add, apply_absolute_value=True).then_inc(am_ready, 1)

            def scales():
                v.wait_ge(amg_ready, 3)
                link(powers_of_two(3, 5))
                v.tensor_scalar(SC[:, 6:7], IV[:, 3:4], IV[:, 4:5], None, ALU.mult).then_inc(gg_scale, 1)
                v.wait_ge(gg_scale, 1)
                link(v.tensor_scalar(SC[:, 7:8], IV[:, 1:2], 1.0 / SUM_SCALE, None, ALU.mult))
                v.tensor_scalar(SELB[:, :], SEL[:, :], SC[:, 6:7], SC[:, 7:8], ALU.mult, ALU.mult)
                link(v.tensor_scalar(SC[:, 3:4], AMG[:, 5:6], 1.0 / (D * D), None, ALU.mult))
                link(v.tensor_scalar(SC[:, 4:5], SC[:, 3:4], EPS, None, ALU.add))
                link(v.reciprocal(SC[:, 4:5], SC[:, 4:5]))
                link(v.tensor_scalar(WT[:, P:2 * P], mat(W_FFN), SC[:, 4:5], 1.0, ALU.mult, ALU.min))
                link(v.tensor_scalar(WT[:, P:2 * P], WT[:, P:2 * P], -1.0, 12582912.0, ALU.max, ALU.add))
                v.tensor_scalar(WT[:, P:2 * P], WT[:, P:2 * P], -12582912.0, None, ALU.add).then_inc(wf_ready, 1)
                link(v.tensor_scalar(SC[:, 5:6], AMG[:, 0:1], SC[:, 3:4], 1.0 / QB, ALU.mult, ALU.mult))

            def gg_lows():
                for q in range(4):
                    at = slice(q * CH, (q + 1) * CH)
                    v.wait_ge(gg_high, q + 1)
                    v.scalar_tensor_tensor(out=GGL[:, at], in0=GG_BANKS[q], scalar=SC[:, 6:7], in1=GGH[:, at],
                                           op0=ALU.mult, op1=ALU.subtract).then_inc(gg_used, 1)

            def add_ffn():
                v.wait_ge(low_ready, 2 * NCH)
                for c in range(NCH):
                    v.wait_ge(ffn_ready, c + 1)
                    v.scalar_tensor_tensor(out=ACC[:, 4 * c:4 * c + 4, :].rearrange("p t d -> p (t d)"),
                                           in0=FFN_BANKS[c], scalar=SC[:, 5:6],
                                           in1=X[:, 4 * c:4 * c + 4, :].rearrange("p t d -> p (t d)"),
                                           op0=ALU.mult, op1=ALU.add).then_inc(acc_ready, 1)

            v.wait_ge(t_in, 32)
            between = {2: z_part_2, 6: other_weights, 12: scales, 16: gg_lows}

            def max_of(p, n, h):
                t, k, w = PIECES[p]
                v.wait_ge(max_ready, h * MAXES + p + 1)
                v.tensor_reduce(MP[:, t, k // CH:k // CH + 1], WK[:, bank_of(n), 0:w], AX.X, ALU.max)\
                    .then_inc(piece_done, 1)

            def mneg(c, i, e):
                chunks = i * (2 * NCH) + e * NCH + c
                v.wait_ge(piece_done, (i * (2 * MAXES) + e * MAXES) + max(p for p, d in CHUNK_MAXED.items() if d == c) + 1)
                best = MP[:, 4 * c:4 * c + 4, 0]
                if c:
                    v.tensor_reduce(NM[:, 4 * c:4 * c + 4], MP[:, 4 * c:4 * c + 4, 0:c + 1], AX.X, ALU.max)\
                        .then_inc(mneg_ready, 1)
                    best = NM[:, 4 * c:4 * c + 4]
                    v.wait_ge(mneg_ready, i * (2 * NCH - 2) + e * (NCH - 1) + c)
                if not (isinstance(i, int) and i == 0 and e == 0 and c < 2):
                    v.wait_ge(mrow_ready, chunks - 1)
                v.tensor_scalar(MM[:, c % 2, :], best, -1.0 / MSHIFT, None, ALU.mult).then_inc(mparts_ready, 1)

            def mrow_copy(c, n, chunks):
                v.wait_ge(mrow_ready, chunks + 1)
                v.tensor_copy(MT[:, c % 2, :], WK[:, bank_of(n), :].bitcast(F16)[0:4, 0:P]).then_inc(mt_copied, 1)

            def low_of(g, units):
                c, k0 = UNIT[g % UNITS]
                b = g % PBUF
                v.wait_ge(probs_ready, 2 * (units + g + 1))
                if k0 < 4 * c:
                    last = v.tensor_tensor(PL[:, b, :, :], PR[:, b, :, :], PH[:, b, :, :], ALU.subtract)
                else:
                    for j in range(2):
                        n0 = (k0 + j - 4 * c) * P
                        last = v.tensor_tensor(PL[:, b, j, n0:CH], PR[:, b, j, n0:CH], PH[:, b, j, n0:CH],
                                               ALU.subtract)
                last.then_inc(low_probs, 1)

            def recip(c, n, chunks):
                v.wait_ge(sum_ready, chunks + 1)
                v.reciprocal(RL[:, c % 2, :], WK[:, bank_of(n), 0:4]).then_inc(rl_ready, 1)

            def add_out(c, n, chunks):
                v.wait_ge(out_ready, chunks + 1)
                v.wait_ge(rl_ready, chunks + 1)
                v.wait_ge(acc_ready, chunks + NCH)
                for t in range(4):
                    a = ACC[:, 4 * c + t, :]
                    last = v.scalar_tensor_tensor(out=a, in0=WK[:, bank_of(n), t * P:(t + 1) * P],
                                                  scalar=RL[:, c % 2, t:t + 1], in1=a,
                                                  op0=ALU.mult, op1=ALU.add)
                last.then_inc(acc_ready, 1)

            def works(uses, i):
                for kind, a, e, n in uses:
                    h = i * 2 + e
                    chunks = i * (2 * NCH) + e * NCH + a
                    if kind == "max":
                        t, k, _ = PIECES[a]
                        if k == 0 and t % 4 == 0:
                            v.wait_ge(mparts_ready, i * (2 * NCH) + e * NCH + t // 4)
                        max_of(a, n, h)
                        if a in CHUNK_MAXED:
                            mneg(CHUNK_MAXED[a], i, e)
                    elif kind == "mrow":
                        v.wait_ge(mrow_stacked[a % 2], i * 64 + 32 * e + 16 * (a // 2))
                        mrow_copy(a, n, chunks)
                    elif kind == "sum":
                        recip(a, n, chunks)
                    elif kind == "out":
                        add_out(a, n, chunks)

            def pair(i, slots, more):
                for w, (first, second, last) in slots.items():
                    works(first, i)
                    works(second, i)
                    if (w + 1 < SLOTS or more) and (w + 1) % SLOTS not in POOL_UNITS:
                        low_of(w + 1, i * SLOTS)
                    works(last, i)

            for n, (kind, a) in enumerate(PROLOGUE, FIRST):
                if kind == "rope":
                    k, c, swapped = a // 2, a // 2 % NCH, a % 2
                    v.wait_ge(rope_ready, a + 1)
                    if k >= 2 and swapped == 0:
                        v.wait_ge(low_ready, k - 1)
                    v.tensor_tensor(RB0[:, k % 2, swapped, :], WK[:, bank_of(n), :],
                                    (COS, SIN)[swapped][:, c * CH:(c + 1) * CH], ALU.mult)\
                        .then_inc(rope_product, 1)
                    if swapped:
                        v.wait_ge(rope_product, a + 1)
                        v.tensor_tensor(RB0[:, k % 2, 0, :], RB0[:, k % 2, 0, :], RB0[:, k % 2, 1, :], ALU.add)\
                            .then_inc(rope_summed, 1)
                    if a == 3 * NCH - 1:
                        for g in range(2):
                            v.wait_ge(lats_high, g + 1)
                            v.tensor_tensor(LS[:, 8 * g:8 * g + 8, 1, :],
                                            LATS_BANKS[g][:, :].rearrange("p (t l) -> p t l", l=L),
                                            LS[:, 8 * g:8 * g + 8, 0, :], ALU.subtract).then_inc(lats_used, 1)
                    if a == ROPES - 1:
                        z_part_1()
                elif kind == "max":
                    max_of(a, n, 0)
                    if a in CHUNK_MAXED:
                        mneg(CHUNK_MAXED[a], 0, 0)
                    if a in between:
                        between[a]()
                else:
                    if a == 2:
                        v.wait_ge(mrow_stacked[0], 16)
                    mrow_copy(a, n, a)
            add_ffn()
            low_of(0, 0)
            pair(0, PEELED, True)
            with v.Fori(0, PAIRS - 1) as i:
                pair(i, BODY, True)
            pair(PAIRS - 1, LAST, False)

            v.wait_ge(acc_ready, H * NCH + 4)
            for t in range(NT):
                last = v.bn_stats(ST6[:, t, :], ACC[:, t, :])
            link(last)
            for t in range(NT):
                last = v.bn_aggr(MV[:, t, :], ST6[:, t, :])
            last.then_inc(x1_stats, 1)
            v.wait_ge(x1_std, 1)
            link(v.reciprocal(RD[:, :], SD[:, :]))
            for t in range(NT):
                v.tensor_scalar(XN[:, t, :], ACC[:, t, :], MV[:, t, 0:1], RD[:, t:t + 1],
                                ALU.subtract, ALU.mult).then_inc(x1n, 1)
            v.wait_ge(m1_ready, 1)
            v.tensor_tensor(WT[:, 0:D], OU[:, 0:D], mat(BLK), ALU.mult).then_inc(m1_copied, 1)
            v.wait_ge(m1_ready, 2)
            v.tensor_copy(WT[:, D:2 * D], OU[:, 0:D]).then_inc(m1_copied, 1)
            v.wait_ge(m1_ready, 3)
            v.tensor_copy(WT[:, 0:D], OU[:, 0:D]).then_inc(m1_copied, 1)
            link(v.tensor_scalar(TC[:, 10:11], CO[:, C_B4:C_B4 + 1], 0.5, None, ALU.mult))
            link(v.tensor_scalar(TC[:, 11:12], CO[:, G_B3:G_B3 + 1], 0.5, None, ALU.mult))
            for c in range(NCH):
                v.wait_ge(x1t_copied, c + 1)
                last = v.tensor_reduce(TC[:, 12 + c:13 + c], XNT[:, c * CH:(c + 1) * CH], AX.X, ALU.add)
            link(last)
            link(v.tensor_reduce(TC[:, 9:10], TC[:, 12:12 + NCH], AX.X, ALU.add))
            v.tensor_scalar(TC[:, 4:5], TC[:, 9:10], 1.0 / S, None, ALU.mult).then_inc(gc_done, 1)
            v.wait_ge(gc_act, 3)
            link(v.tensor_scalar(TC[:, 8:9], TC[:, 7:8], 0.7, None, ALU.mult))
            link(v.tensor_scalar(TC[:, 0:1], TC[:, 8:9], CO[:, AR:AR + 1], 0.1, ALU.mult, ALU.add))
            link(v.tensor_scalar(TC[:, 0:1], TC[:, 0:1], CO[:, SIGN:SIGN + 1], None, ALU.mult))
            link(v.tensor_scalar(TC[:, 1:2], CO[:, AR:AR + 1], CO[:, SIGN:SIGN + 1], 0.3, ALU.mult, ALU.mult))
            for n in range(CYCLES * NCH):
                c = n % NCH
                cs = slice(c * CH, (c + 1) * CH)
                src = XNT if n < NCH else COS
                v.wait_ge(th_ready, n + 1)
                link(v.tensor_scalar(TH[:, c, :], TH[:, c, :], TC[:, 1:2], TC[:, 0:1], ALU.mult, ALU.add))
                v.wait_ge(swapped_in[c], 32 * (n // NCH) + 32)
                link(v.tensor_tensor(TH[:, c, :], TH[:, c, :], TW[:, cs], ALU.mult))
                v.tensor_tensor(COS[:, cs], src[:, cs], TH[:, c, :], ALU.add).then_inc(cn_out, 1)
            for c in range(NCH):
                v.wait_ge(y_ready, c + 1)
                v.tensor_tensor(X[:, 4 * c:4 * c + 4, :].rearrange("p t d -> p (t d)"),
                                ACC[:, 4 * c:4 * c + 4, :].rearrange("p t d -> p (t d)"),
                                B4[c], ALU.add).then_inc(y_done, 1)

        @block.scalar
        def _(act):
            act.wait_ge(var_ready, 1)
            act.activation(SD[:, :], MV[:, :, 1], ACT.Sqrt, bias=EPSC[:, 0:1]).then_inc(std_ready, 1)
            act.wait_ge(var_ready, 2)
            act.activation(SD[:, :], RD2[:, :], ACT.Sqrt, bias=EPSC[:, 1:2]).then_inc(std_ready, 1)
            for c in range(NCH):
                act.wait_ge(xnt_ready, c + 1)
                act.activation(XNT[:, c * CH:(c + 1) * CH], B4[c], ACT.Copy)
                act.activation(XH[:, c * CH:(c + 1) * CH], B4[c], ACT.Copy).then_inc(xt_copied, 1)
            act.wait_ge(iv_ready, 1)
            for k, (raw, hi) in enumerate(((WQ, WQH), (WKU, WKH))):
                act.activation(hi[:, :, 0:P], raw[:, :, 0:P], ACT.Copy, scale=IV[:, 2 * k:2 * k + 1]).then_inc(w0_high, 1)
            for c in range(NCH):
                act.wait_ge(latt_ready, c + 1)
                act.activation(LT[:, c * CH:(c + 1) * CH], B4[c], ACT.Copy).then_inc(latt_high, 1)

            def high(k, n, rb=RB):
                kind, c = divmod(k, NCH)
                act.wait_ge(rope_summed, n + 1)
                act.activation(SG[:, 2 * kind, c * CH:(c + 1) * CH], rb[:, k % 2, 0, :], ACT.Copy).then_inc(high_ready, 1)

            def probs(g, units):
                c, k0 = UNIT[g % UNITS]
                act.wait_ge(unit_summed, units + g + 1)
                for j in range(2):
                    n0 = max(0, k0 + j - 4 * c) * P
                    act.wait_ge(scores_ready, 2 * (units + g) + j + 1)
                    act.activation(PR[:, g % PBUF, j, n0:CH], ST[:, scores_bank(g - LAG, j), n0:CH], ACT.Exp,
                                   scale=SC[:, 0:1]).then_inc(probs_ready, 1)

            def copy_chunk(e, c, w, i):
                act.wait_ge(unit_summed, i * SLOTS + PBUF + w + 1)
                if not isinstance(i, int) or i > 0 or c >= 2:
                    act.wait_ge(acc_ready, i * (2 * NCH) + e * NCH + c - 1 + NCH)
                n = i * (2 * NCH) + e * NCH + c + 1
                act.activation(SUMS[:, c % 2, 0, :], OU[:, :], ACT.Copy, scale=1.0 / SUM_SCALE).then_inc(ou_copied, 1)
                act.activation(SUMS[:, c % 2, 1, :], RS[:, :], ACT.Copy).then_inc(rs_copied, 1)
                act.wait_ge(ou_copied, n)
                act.wait_ge(rs_copied, n)
                act.activation(SUMH[:, c % 2, :, :], SUMS[:, c % 2, :, :], ACT.Copy).then_inc(sums_high, 1)

            def rope_copy(r, n, i):
                act.wait_ge(rope_ready, i * ROPES + ROPES + r + 1)
                act.wait_ge(rope_product, i * ROPES + ROPES + r - RA_BUFS + 1)
                act.activation(RA[:, r % RA_BUFS, :], WK[:, bank_of(n), :], ACT.Copy).then_inc(rope_copied, 1)

            def pair(i, slots, more):
                for w, (first, second, last) in slots.items():
                    k, odd = divmod(w - ROPE_FIRST - HIGH_LAG, 2)
                    if more and not odd and 0 <= k < 2 * NCH:
                        if k == 0:
                            for slot in range(2):
                                act.wait_ge(stacked[slot], i * 64 + 64)
                                act.wait_ge(stacked_low[slot], i * 32 + 32)
                        high(k, i * (2 * NCH) + 2 * NCH + k)
                    for kind, a, e, n in second:
                        if kind == "rope":
                            rope_copy(a, n, i)
                    if w + LAG < SLOTS or more:
                        probs(w + LAG, i * SLOTS)
                    e, u = divmod(w, UNITS)
                    if u in CHUNK_END and (w < SLOTS or more):
                        copy_chunk(e, CHUNK_END[u], w, i)

            for k in range(2 * NCH):
                high(k, k, RB0)
                if k == NCH:
                    for g in range(2):
                        act.wait_ge(lats_ready, g + 1)
                        act.activation(LS[:, 8 * g:8 * g + 8, 0, :],
                                       LATS_BANKS[g][:, :].rearrange("p (t l) -> p t l", l=L), ACT.Copy)\
                            .then_inc(lats_high, 1)
            act.wait_ge(gg_scale, 1)
            for q in range(4):
                act.wait_ge(gg_ready, q + 1)
                act.activation(GGH[:, q * CH:(q + 1) * CH], GG_BANKS[q], ACT.Copy, scale=SC[:, 6:7]).then_inc(gg_high, 1)
            for k, (raw, hi) in enumerate(((WQ, WQH), (WKU, WKH))):
                act.wait_ge(w_scaled, k + 1)
                for j in range(2):
                    act.activation(hi[:, j, P:H * HD], raw[:, j, P:H * HD], ACT.Copy).then_inc(w_high, 1)
            act.wait_ge(split_ready, NCH)
            for c in range(NCH):
                act.wait_ge(zt_ready, c + 1)
                act.activation(ZT[:, c * CH:(c + 1) * CH], ZT_BANKS[c], ACT.Copy).then_inc(zt_copied, 1)
            act.wait_ge(w_low, 4)
            for g in range(LAG):
                probs(g, 0)
            pair(0, PEELED, True)
            with act.Fori(0, PAIRS - 1) as i:
                pair(i, BODY, True)
            pair(PAIRS - 1, LAST, False)

            act.wait_ge(x1_stats, 1)
            act.activation(SD[:, :], MV[:, :, 1], ACT.Sqrt, bias=EPSC[:, 0:1]).then_inc(x1_std, 1)
            for c in range(NCH):
                act.wait_ge(x1t, c + 1)
                act.activation(XNT[:, c * CH:(c + 1) * CH], B4[c], ACT.Copy)\
                    .then_inc(x1t_copied, 1)

            def gelu(dst, bank, bias, ready):
                act.activation(dst, bank, ACT.Gelu, bias=CO[:, bias:bias + 1]).then_inc(ready, 1)

            for cyc in range(CYCLES):
                for c in range(NCH):
                    act.wait_ge(layer1, cyc * NCH + c + 1)
                    gelu(H1[:, c, :], NB[c], C_B1, h1_ready)
                for p in range(2):
                    act.wait_ge(layer2, 2 * cyc + p + 1)
                    gelu(H2[:, p, :], NB[2 * p], C_B2, h2_ready)
                    if cyc == 0 and p == 0:
                        act.wait_ge(gc_mm, 1)
                        act.activation(TC[0:64, 5:6], B4[0][0:64, 0:1], ACT.Gelu, bias=CO[0:64, G_B1:G_B1 + 1])\
                            .then_inc(gc_act, 1)
                if cyc == 0:
                    act.wait_ge(gc_mm, 2)
                    act.activation(TC[0:32, 6:7], B4[0][0:32, 0:1], ACT.Gelu, bias=CO[0:32, G_B2:G_B2 + 1])\
                        .then_inc(gc_act, 1)
                act.wait_ge(layer3, cyc + 1)
                gelu(H3, NB[1], C_B3, h3_ready)
                if cyc == 0:
                    act.wait_ge(gc_mm, 3)
                    act.activation(TC[:, 7:8], B4[0][:, 0:1], ACT.Tanh, bias=TC[:, 11:12], scale=0.5)\
                        .then_inc(gc_act, 1)
                for c in range(NCH):
                    act.wait_ge(layer4, cyc * NCH + c + 1)
                    if cyc:
                        act.wait_ge(cn_out, (cyc - 1) * NCH + c + 1)
                    act.activation(TH[:, c, :], NB[c], ACT.Tanh, bias=TC[:, 10:11], scale=0.5).then_inc(th_ready, 1)

        @block.gpsimd
        def _(pool):
            pool.memset(KL[HD:HD + 1, :, :], MSHIFT).then_inc(kl_ready, 1)
            pool.wait_ge(kl_ready, 1)
            pool.wait_ge(am_ready, 1)
            pool.partition_all_reduce(AMG[:, 0:3], AM[:, 0:3], P, bass.bass_isa.ReduceOp.max).then_inc(amg_ready, 1)
            pool.wait_ge(amg_ready, 1)
            pool.wait_ge(rd2_ready, 1)
            pool.wait_ge(xnt_ready, NCH)
            for t in range(NT):
                last = pool.tensor_scalar(Z[:, t, :], XN[:, t, :], RD2[:, t:t + 1], None, ALU.mult)
            last.then_inc(z_scaled, 1)

            def rotated(k):
                kind, c = divmod(k, NCH)
                return 2 * kind, slice(c * CH, (c + 1) * CH)

            def add(k, n):
                pool.wait_ge(rope_product, n * 2 + 2)
                pool.tensor_tensor(RB[:, k % 2, 0, :], RB[:, k % 2, 0, :], RB[:, k % 2, 1, :], ALU.add).then_inc(rope_summed, 1)

            def low(k, n, rb=RB):
                part, cs = rotated(k)
                pool.wait_ge(high_ready, n + 1)
                pool.tensor_tensor(SG[:, part + 1, cs], rb[:, k % 2, 0, :], SG[:, part, cs], ALU.subtract)\
                    .then_inc(low_ready, 1)

            for k in range(2 * NCH):
                low(k, k, RB0)
            pool.wait_ge(low_ready, 2 * NCH)
            pool.wait_ge(zmax_ready, 1)
            pool.partition_all_reduce(AMG[:, 0:1], AM[:, 0:1], P, bass.bass_isa.ReduceOp.max)\
                .then_inc(zmaxg_ready, 1)
            pool.wait_ge(zmaxg_ready, 1)
            for k, raw in enumerate((WQ, WKU)):
                pool.tensor_scalar(raw[:, :, P:H * HD], raw[:, :, P:H * HD], IV[:, 2 * k:2 * k + 1], None, ALU.mult)\
                    .then_inc(w_scaled, 1)
            pool.wait_ge(w_scaled, 2)
            pool.wait_ge(am_ready, 2)
            pool.partition_all_reduce(AMG[:, 3:5], AM[:, 3:5], P, bass.bass_isa.ReduceOp.max).then_inc(amg_ready, 1)
            pool.partition_all_reduce(AMG[:, 5:6], AM[:, 5:6], P, bass.bass_isa.ReduceOp.add).then_inc(amg_ready, 1)
            pool.wait_ge(amg_ready, 3)
            for k, (raw, hi, lo) in enumerate(((WQ, WQH, WQL), (WKU, WKH, WKL))):
                for j in range(2):
                    pool.wait_ge(w_high, 2 * k + j + 1)
                    pool.tensor_tensor(lo[:, j, P:H * HD], raw[:, j, P:H * HD], hi[:, j, P:H * HD], ALU.subtract)\
                        .then_inc(w_low, 1)

            def low_of(g, units):
                c, k0 = UNIT[g % UNITS]
                assert k0 < 4 * c
                pool.wait_ge(probs_ready, 2 * (units + g + 1))
                pool.tensor_tensor(PL[:, g % PBUF, :, :], PR[:, g % PBUF, :, :], PH[:, g % PBUF, :, :], ALU.subtract)\
                    .then_inc(low_probs_pool, 1)

            def pair(i, slots, more):
                for w, (first, second, last) in slots.items():
                    if (w + 2 < SLOTS or more) and (w + 2) % SLOTS in POOL_UNITS:
                        low_of(w + 2, i * SLOTS)
                    e, u = divmod(w - 1, UNITS)
                    if u in CHUNK_END and w > 0 and (w - 1 < SLOTS or more):
                        c = CHUNK_END[u]
                        pool.wait_ge(sums_high, i * (2 * NCH) + e * NCH + c + 1)
                        pool.tensor_tensor(SUML[:, c % 2, :, :], SUMS[:, c % 2, :, :], SUMH[:, c % 2, :, :],
                                           ALU.subtract).then_inc(sums_low, 1)
                    for kind, r, e, n in second:
                        if kind == "rope":
                            k, j = divmod(r, 2)
                            part, cs = rotated(k)
                            m = i * (2 * NCH) + 2 * NCH + k
                            pool.wait_ge(low_ready, m - 1)
                            pool.wait_ge(rope_copied, i * ROPES + r + 1)
                            pool.tensor_tensor(RB[:, k % 2, j, :], RA[:, r % RA_BUFS, :], (COS, SIN)[j][:, cs],
                                               ALU.mult).then_inc(rope_product, 1)
                            if j == 1:
                                add(k, m)
                                if k:
                                    low(k - 1, m - 1)
                            if r == ROPES - 1:
                                low(k, m)

            pair(0, PEELED, True)
            with pool.Fori(0, PAIRS - 1) as i:
                pair(i, BODY, True)
            pair(PAIRS - 1, LAST, False)


def causal(transposed):
    import numpy as np
    m = np.triu(np.full((P, P), NEG, np.float32), 1)
    return m.T if transposed else m


def rotary():
    import numpy as np
    inv = (1.0 / np.float32(10000.0) ** (np.arange(0, HD, 2, dtype=np.float32) / np.float32(HD))).astype(np.float32)
    ang = (np.arange(S, dtype=np.float32)[None, :] * inv[:, None]).astype(np.float64)
    cos, sin = np.cos(ang).astype(np.float32), np.sin(ang).astype(np.float32)
    return np.concatenate([cos] * 4), np.concatenate([-sin, sin] * 2)


def kernel(**inputs):
    import numpy as np
    import concourse.bacc as bacc
    from concourse import mybir as mb
    from concourse.bass_utils import run_bass_kernel_spmd as run

    g = {k: np.asarray(v) for k, v in inputs.items()}

    def swapped(w):
        return w.reshape(H, 2, HD // 2, -1)[:, ::-1].reshape(H * HD, -1)

    def wide(a):
        a = a if a.ndim == 2 else a[None, :]
        full = np.zeros((P, D), np.float32)
        full[:a.shape[0], :a.shape[1]] = a
        return full

    def every(v, n=P):
        return np.broadcast_to(v.reshape(1, -1), (n, v.size))

    q1, v1 = (g[f"L1_attn_{n}_weight"].reshape(D, D) for n in "qv")
    wd = g["L0_attn_w_kv_down"].T
    blocks = np.kron(np.eye(H, dtype=np.float32), np.full((D // H, D // H), (D // H) ** -0.5, np.float32))
    c, z = "L1_ffn_cn_", "L1_ffn_gc_"
    mats = [np.eye(P, dtype=np.float32), np.concatenate([wd, wd], 1), g["L0_ffn_weight"],
            every(g["L0_ffn_ln_gamma"]), every(g["L0_ffn_ln_beta"]), causal(False), causal(True),
            q1, q1.T, v1, g["L1_attn_out_w"].T, blocks,
            g[c + "w1"], g[c + "w2"], np.concatenate([g[c + "w3"]] * 2), np.broadcast_to(np.concatenate([g[c + "w4"]] * 4), (P, P)),
            g[z + "w1"], g[z + "w2"], np.broadcast_to(g[z + "w3"], (32, P))]
    vecs = [g[c + "b1"], np.tile(g[c + "b2"], 2), np.tile(g[c + "b3"], 4), np.broadcast_to(g[c + "b4"], (P,)),
            g[z + "b1"], g[z + "b2"], np.broadcast_to(g[z + "b3"], (P,)),
            np.broadcast_to(g["L1_ffn_adaptive_range"], (P,)), np.repeat(TWIST_SIGNS, P // 4)]
    cols = np.zeros((P, len(vecs)), np.float32)
    for n, vec in enumerate(vecs):
        cols[:vec.size, n] = vec
    cos, sin = rotary()
    wq, wk = g["L0_attn_wq"], g["L0_attn_w_k_up"]
    arrays = dict(
        x=g["L0_attn_x"][0], wqT=wq.T, wqpT=swapped(wq).T, wkT=wk.T, wkpT=swapped(wk).T,
        wv=g["L0_attn_w_v_up"], woT=g["L0_attn_wo"].T, mats=np.concatenate([wide(m) for m in mats], 1),
        cols=cols, rows=np.concatenate([g["L1_attn_out_b"], np.ones(P, np.float32)])[None, :],
        cosT=cos, sinT=sin)
    nc = bacc.Bacc("TRN2", target_bir_lowering=False, num_devices=1)
    arrays = {k: np.ascontiguousarray(a) for k, a in arrays.items()}
    args = {k: nc.dram_tensor(k, a.shape, mb.dt.from_np(a.dtype), kind="ExternalInput").ap()
            for k, a in arrays.items()}
    args["out"] = nc.dram_tensor("out", (S, D), F32, kind="ExternalOutput").ap()
    build(nc, **args)
    r = run(nc, [arrays], core_ids=[0])
    return np.asarray(r.results[0]["out"]).reshape(1, S, D)
```

```python
from contextlib import ExitStack

import concourse.bass as bass
from concourse import mybir

F32 = mybir.dt.float32
BF16 = mybir.dt.bfloat16
F16 = mybir.dt.float16
I32 = mybir.dt.int32
ALU = mybir.AluOpType
ACT = mybir.ActivationFunctionType
AX = mybir.AxisListType

P = 128
S = 2048
D = 128
H = 16
HD = 64
L = 64
PAIRS = H // 2
CH = 512
NCH = S // CH
NT = S // P
UNITS = sum((4 * c + 4) // 2 for c in range(NCH))
LAG = 3
WORK_BANKS = 3
POOL_UNITS = (26, 28, 32, 34, 36)
HIGH_LAG = 5
WCOLS = (PAIRS + 1) * P
PBUF = 4
RA_BUFS = 4
MSHIFT = 2048.0
SUM_SCALE = 32.0
TWIST_SIGNS = (1.0, -1.0, -1.0, 1.0)
NEG = -1.0e30
LN_EPS, FFN_EPS, EPS, QB = 1e-5, 1e-3, 1e-5, 128.0
CYCLES = 3

UNIT = [(c, k) for c in range(NCH) for k in range(0, 4 * c + 4, 2)]
CHUNK_END = {u: c for u, (c, k) in enumerate(UNIT) if k == 4 * c + 2}
PIECES = [(t, k, min(CH, (t + 1) * P - k)) for t in range(NT) for k in range(0, (t + 1) * P, CH)]
MAXES = len(PIECES)
PER_SLOT = 2
AHEAD = 13
ROPES = 2 * NCH
SUM_LAG, OUT_LAG = 3, 4
SLOTS = 2 * UNITS
START = 5
ROPE_SLOTS = tuple(5 * k // 2 for k in range(ROPES))
SWAPPED_PER_PAIR = 64 * ROPES // RA_BUFS
ROTATE_LAG = 2
CHUNK_MAXED = {max(p for p, (t, _, _) in enumerate(PIECES) if t // 4 == c): c for c in range(NCH)}


def rope_of_slot(w, lag):
    ahead, at = divmod(w - lag, SLOTS)
    return (ROPE_SLOTS.index(at), ahead + 1) if w >= lag and at in ROPE_SLOTS else None


def works_of_slot(w, more):
    def pieces(w):
        e, p = divmod((w + AHEAD) * PER_SLOT, MAXES)
        return [(e, p + j) for j in range(PER_SLOT)] if e < 2 or more else []

    first, second = [], []
    for e, p in pieces(w - 1):
        if p in CHUNK_MAXED:
            first.append(("mrow", CHUNK_MAXED[p], e))
    for (e, p), place in zip(pieces(w), (first, second)):
        place.append(("max", p, e))
    if more and rope_of_slot(w, 0):
        k, pairs = rope_of_slot(w, 0)
        second.append(("rope", k, 2 * pairs))
    for lag, kind in ((SUM_LAG, "sum"), (OUT_LAG, "out")):
        e, u = divmod(w - lag, UNITS)
        if e >= 0 and (e < 2 or more) and u in CHUNK_END:
            (second if kind == "sum" else first).append((kind, CHUNK_END[u], e))
    return first, second


def plan(slots, first, more):
    n, uses = first, {}
    for w in slots:
        uses[w] = []
        for place in works_of_slot(w, more):
            uses[w].append([(*use, n + j) for j, use in enumerate(place)])
            n += len(place)
    return uses


def in_order(uses):
    return [use for w in uses for place in uses[w] for use in place]


PROLOGUE = [("rope", r) for r in range(2 * ROPES)]
for _p in range(AHEAD * PER_SLOT):
    PROLOGUE += [("max", _p)] + ([("mrow", CHUNK_MAXED[_p])] if _p in CHUNK_MAXED else [])
POOL_LOWS = [{g - UNITS * e for g in POOL_UNITS if g // UNITS == e} for e in range(2)]


def pool_units(g):
    return g // SLOTS * len(POOL_UNITS) + sum(p < g % SLOTS for p in POOL_UNITS)


BODY = plan(range(START, SLOTS + START), 0, True)
LAST = plan(range(START, SLOTS + START), 0, False)
BEFORE = len(PROLOGUE) + len(in_order(plan(range(START), 0, True)))
FIRST = (len(in_order(BODY)) - BEFORE) % WORK_BANKS
PEELED = plan(range(START), FIRST + len(PROLOGUE), True)
FFN_AFTER = (13, 15, 17, 19)
SCORES_AFTER = 21
PIECES_BEFORE = (START + AHEAD) * PER_SLOT
ROWS_BEFORE = sum(kind == "mrow" for kind, *_ in PROLOGUE + in_order(PEELED))


def build(nc, x, wqT, wkT, wv, woT, mats, cols, rows, cosT, sinT, out):
    with ExitStack() as ctx:
        def sb(name, shape, dt=F32):
            return ctx.enter_context(nc.sbuf_tensor(name, shape, dt))

        def ps(name, shape):
            return ctx.enter_context(nc.psum_tensor(name, shape, F32))

        def sem(name):
            return ctx.enter_context(nc.semaphore(name))

        ST = ps("ST", [P, 3, CH])
        WK = ps("WK", [P, WORK_BANKS, CH])
        OU = ps("OU", [P, CH])
        RS = ps("RS", [P, CH])

        X = sb("X", [P, NT, D])
        XN = sb("XN", [P, NT, D])
        ACC = sb("ACC", [P, NT, D])
        XNT = sb("XNT", [P, S])
        XH = sb("XH", [P, S], F16)
        XL = sb("XL", [P, S], F16)
        LT = sb("LT", [P, S], F16)
        LS = sb("LS", [P, NT, 2, L], F16)
        COS = sb("COS", [P, S])
        SIN = sb("SIN", [P, S])
        WQH = sb("WQH", [P, WCOLS], F16)
        WQL = sb("WQL", [P, WCOLS], F16)
        WKH = sb("WKH", [P, WCOLS], F16)
        WKL = sb("WKL", [P, WCOLS], F16)
        GGH = sb("GGH", [P, H * D], F16)
        GGL = sb("GGL", [P, H * D], BF16)
        MA = sb("MA", [P, mats.shape[1]])
        CO = sb("CO", [P, cols.shape[1]])
        RW = sb("RW", [1, rows.shape[1]])
        QS = sb("QS", [P, 2, S], F16)
        QM = sb("QM", [HD + 1, 2, S], F16)
        KK = sb("KK", [P, 2, S], F16)
        KL = sb("KL", [HD + 1, 2, S], F16)
        SG = sb("SG", [P, 4, S], F16)
        PR = sb("PR", [P, PBUF, 2, CH])
        PL = sb("PL", [P, PBUF, 2, CH], F16)
        SUMS = sb("SUMS", [P, 2, 2, CH])
        SUMH = sb("SUMH", [P, 2, 2, CH], F16)
        SUML = sb("SUML", [P, 2, 2, CH], BF16)
        RL = sb("RL", [P, 2, 4])
        MP = sb("MP", [P, NT, 4])
        NM = sb("NM", [P, NT])
        MM = sb("MM", [P, 2, 4], F16)
        MT = sb("MT", [4, 2, P], F16)
        ST6 = sb("ST6", [P, NT, 6])
        MV = sb("MV", [P, NT, 2])
        SD = sb("SD", [P, NT])
        RD = sb("RD", [P, NT])
        RD2 = sb("RD2", [P, NT])
        AM = sb("AM", [P, 6])
        AMG = sb("AMG", [P, 6])
        EX = sb("EX", [P, 6])
        IV = sb("IV", [P, 6])
        SC = sb("SC", [P, 8])
        TC = sb("TC", [P, 16])
        ONE = sb("ONE", [P, 32], BF16)
        IDB = sb("IDB", [P, P], BF16)
        IDH = sb("IDH", [P, P], F16)
        MK = sb("MK", [P, 2, P], BF16)
        SEL = sb("SEL", [P, 1])
        SELB = sb("SELB", [P, 1], BF16)
        EPSC = sb("EPSC", [P, 2])
        WT = sb("WT", [P, 2 * D])
        M1 = sb("M1", [P, 2, D])
        RAW = PR[:, :, :, :].rearrange("p b j n -> p (b j n)")
        WQ = RAW[:, 0:WCOLS]
        WKU = RAW[:, WCOLS:2 * WCOLS]
        WV = SUMS[0:HD, :, :, :].rearrange("p b s n -> p (b s n)").rearrange("p (h a l) -> p h a l", h=H, a=2)
        WO = PL[0:HD, :, :, :].bitcast(F32).rearrange("p b j n -> p (b j n)").rearrange("p (h m) -> p h m", h=H)
        Z = XN
        ZT = XNT
        RA = XN[:, :, :].rearrange("p (b t) d -> p b (t d)", b=RA_BUFS)
        RB = XNT[:, :].rearrange("p (b j n) -> p b j n", b=2, j=2)
        RB0 = ACC[:, :, :].rearrange("p (b j t) d -> p b j (t d)", b=2, j=2)
        RSW = X[:, :, :].rearrange("p (b t) d -> p b (t d)", b=RA_BUFS)
        TW = SG[:, 0:2, :].bitcast(F32).rearrange("p a n -> p (a n)")
        H1 = PR[:, :, 0, :]
        H2 = PR[:, 0:2, 1, :]
        S0 = XN[:, :, :].rearrange("p (c t) d -> p c (t d)", c=NCH)
        H3 = PR[:, 2, 1, :]
        TH = PL[:, :, :, :].bitcast(F32).rearrange("p b j n -> p b (j n)")
        B4 = (ST[:, 0, :], ST[:, 1, :], ST[:, 2, :], WK[:, 2, :])
        LATS_BANKS = (OU, RS)
        GG_BANKS = (ST[:, 0, :], ST[:, 1, :], ST[:, 2, :], OU[:, :])
        ZT_BANKS = (RS[:, :], ST[:, 0, :], ST[:, 1, :], ST[:, 2, :])
        FFN_BANKS = (OU[:, :], RS[:, :], OU[:, :], RS[:, :])
        NB = (WK[:, 0, :], WK[:, 1, :], OU[:, :], RS[:, :])
        PH = PR[:, :, :, :].bitcast(BF16).rearrange("p b j (n two) -> p b j n two", two=2)[:, :, :, :, 1]

        def mat(n, rows_=P, cols_=D):
            return MA[0:rows_, n * D:n * D + cols_]

        (IDENT, WD2, W_FFN, MASK_QK, MASK_KQ, Q1, Q1T, V1, WO1T, BLK,
         CW1, CW2, CW3, CW4, GW1, GW2, GW3) = range(17)
        (C_B1, C_B2, C_B3, C_B4, G_B1, G_B2, G_B3, AR, SIGN, GAMMA, BETA) = range(11)

        x_in, w_in, m_in = sem("x_in"), sem("w_in"), sem("m_in")
        t_in, g_in = sem("t_in"), sem("g_in")
        dve = sem("dve_chain")
        var_ready, std_ready = sem("var_ready"), sem("std_ready")
        xn_ready, xnt_ready, xt_copied = sem("xn_ready"), sem("xnt_ready"), sem("xt_copied")
        split_ready, am_ready, amg_ready = sem("split_ready"), sem("am_ready"), sem("amg_ready")
        iv_ready, wd_ready, w0_high, w0_ready = sem("iv_ready"), sem("wd_ready"), sem("w0_high"), sem("w0_ready")
        latt_ready, latt_high, latt_used = sem("latt_ready"), sem("latt_high"), sem("latt_used")
        lats_ready, lats_high, lats_used = sem("lats_ready"), sem("lats_high"), sem("lats_used")
        gg_ready, gg_scale, gg_high, gg_used = sem("gg_ready"), sem("gg_scale"), sem("gg_high"), sem("gg_used")
        w_scaled, w_high, w_low = sem("w_scaled"), sem("w_high"), sem("w_low")
        const_ready, kl_ready = sem("const_ready"), sem("kl_ready")
        rd2_ready, z_scaled = sem("rd2_ready"), sem("z_scaled")
        z_ready, zt_ready, zt_copied = sem("z_ready"), sem("zt_ready"), sem("zt_copied")
        zmax_ready, zmaxg_ready, wf_ready = sem("zmax_ready"), sem("zmaxg_ready"), sem("wf_ready")
        ffn_ready = sem("ffn_ready")
        rope_ready, max_ready, mrow_ready = sem("rope_ready"), sem("max_ready"), sem("mrow_ready")
        sum_ready, out_ready = sem("sum_ready"), sem("out_ready")
        rope_copied, rope_product, rope_summed = sem("rope_copied"), sem("rope_product"), sem("rope_summed")
        halves_swapped = [sem(f"halves_swapped{b}") for b in range(RA_BUFS)]
        high_ready, low_ready = sem("high_ready"), sem("low_ready")
        stacked = [sem("slot0_stacked"), sem("slot1_stacked")]
        stacked_low = [sem("slot0_low_stacked"), sem("slot1_low_stacked")]
        piece_done, mneg_ready, mparts_ready = sem("piece_done"), sem("mneg_ready"), sem("mparts_ready")
        mt_copied, mrow_stacked = sem("mt_copied"), [sem("mrow_stacked0"), sem("mrow_stacked1")]
        scores_ready, probs_ready = sem("scores_ready"), sem("probs_ready")
        low_probs, low_probs_pool = sem("low_probs"), sem("low_probs_pool")
        ou_copied, rs_copied, sums_high, sums_low = sem("ou_copied"), sem("rs_copied"), sem("sums_high"), sem("sums_low")
        unit_summed = sem("unit_summed")
        rl_ready, acc_ready = sem("rl_ready"), sem("acc_ready")
        x1_stats, x1_std, x1n, x1t, x1t_copied = (sem("x1_stats"), sem("x1_std"), sem("x1n"), sem("x1t"),
                                                  sem("x1t_copied"))
        m1_ready, m1_copied = sem("m1_ready"), sem("m1_copied")
        gc_mm, gc_act, gc_done = sem("gc_mm"), sem("gc_act"), sem("gc_done")
        layer1, layer2, layer3, layer4 = sem("layer1"), sem("layer2"), sem("layer3"), sem("layer4")
        h1_ready, h2_ready, h3_ready, th_ready = sem("h1_ready"), sem("h2_ready"), sem("h3_ready"), sem("th_ready")
        s0_ready = sem("s0_ready")
        swapped_in, cn_out = [sem(f"swapped_in{c}") for c in range(NCH)], sem("cn_out")
        y_ready, y_done, stored = sem("y_ready"), sem("y_done"), sem("stored")

        block = ctx.enter_context(nc.Block())

        def first_blocks(w):
            return w[:, :].rearrange("p (b n) -> p b n", n=P)[:, ::PAIRS, :]

        def bank_of(n):
            return n % WORK_BANKS

        def scores_bank(w, j):
            return (2 * (w % SLOTS) + j - 2 * START) % (2 * SLOTS) % 3

        def bank_read(kind, a, e, i, back=0):
            if kind == "rope":
                return rope_copied, i * ROPES + ((e // 2 - 1 - back) * ROPES + a + 1)
            if kind == "max":
                return piece_done, i * (2 * MAXES) + ((e - 2 * back) * MAXES + a + 1)
            chunks = (e - 2 * back) * NCH + a + 1
            if kind == "mrow":
                return mt_copied, i * (2 * NCH) + chunks
            return (rl_ready, i * (2 * NCH) + chunks) if kind == "sum" else (acc_ready, i * (2 * NCH) + (chunks + NCH))

        @block.sync
        def _(sp):
            sp.dma_start(X[:, :, :], x.rearrange("(t p) d -> p t d", p=P)).then_inc(x_in, 16)
            sp.dma_start(MA[:, :], mats).then_inc(m_in, 16)
            sp.dma_start(CO[:, :], cols).then_inc(m_in, 16)
            sp.dma_start(RW[:, :], rows).then_inc(m_in, 16)
            sp.dma_start(WQ[:, :], wqT).then_inc(w_in, 16)
            for half in range(2):
                sp.dma_start(WKU[half * L:half * L + L, :], wkT).then_inc(w_in, 16)
            sp.dma_start(COS[:, :], cosT).then_inc(t_in, 16)
            sp.dma_start(SIN[:, :], sinT).then_inc(t_in, 16)
            for half in range(2):
                sp.dma_start(WV[:, :, half, :], wv.rearrange("(h d) l -> d h l", d=HD)).then_inc(g_in, 16)
            sp.dma_start(WO[:, :, :], woT.rearrange("(h d) m -> d h m", d=HD)).then_inc(g_in, 16)

            def stack_q(slot, i, pair_):
                n = pair_ * (2 * NCH)
                q0 = slot * HD
                sp.wait_ge(high_ready, i * (2 * NCH) + (n + NCH))
                sp.wait_ge(low_ready, i * (2 * NCH) + (n + NCH))
                if pair_:
                    sp.wait_ge(scores_ready, 2 * (i * SLOTS + (slot + 1) * UNITS))
                sp.dma_start(QS[0:HD, slot, :], SG[q0:q0 + HD, 0, :]).then_inc(stacked[slot], 16)
                sp.dma_start(QS[HD:P, slot, :], SG[q0:q0 + HD, 1, :]).then_inc(stacked[slot], 16)

            def stack_k(slot, i, pair_):
                n, q0 = pair_ * (2 * NCH), slot * HD
                sp.wait_ge(high_ready, i * (2 * NCH) + (n + 2 * NCH))
                sp.dma_start(KK[0:HD, slot, :], SG[q0:q0 + HD, 2, :]).then_inc(stacked[slot], 16)
                sp.dma_start(KK[HD:P, slot, :], SG[q0:q0 + HD, 2, :]).then_inc(stacked[slot], 16)
                sp.dma_start(QM[0:HD, slot, :], SG[q0:q0 + HD, 0, :]).then_inc(stacked_low[slot], 16)
                sp.wait_ge(low_ready, i * (2 * NCH) + (n + 2 * NCH))
                sp.dma_start(KL[0:HD, slot, :], SG[q0:q0 + HD, 3, :]).then_inc(stacked_low[slot], 16)

            def mrow(i, e, c):
                sp.wait_ge(mt_copied, i * (2 * NCH) + e * NCH + c + 1)
                sp.dma_start(QM[HD:HD + 1, e % 2, c * CH:(c + 1) * CH], MT[:, c % 2, :]).then_inc(mrow_stacked[c % 2], 16)

            for slot in range(2):
                stack_q(slot, 0, 0)
                stack_k(slot, 0, 0)
            mrow(0, 0, 0)
            mrow(0, 0, 1)
            mrow(0, 0, 2)

            def swap(i, k, pairs=1):
                sp.wait_ge(rope_copied, i * ROPES + ((pairs - 1) * ROPES + k + 1))
                b = k % RA_BUFS
                for q in range(4):
                    to, of = q * (HD // 2), (q ^ 1) * (HD // 2)
                    sp.dma_start(RSW[to:to + HD // 2, b, :], RA[of:of + HD // 2, b, :]).then_inc(halves_swapped[b], 16)

            def pair(i, more):
                for (e, c), swaps in (((0, 3), (2,)), ((1, 0), (3,)), ((1, 1), (4, 5))):
                    for k in swaps if more else ():
                        swap(i, k)
                    mrow(i, e, c)
                if more:
                    swap(i, 6)
                    swap(i, 7)
                    stack_q(0, i, 1)
                mrow(i, 1, 2)
                if more:
                    stack_k(0, i, 1)
                for e, c in ((1, 3),) + (((2, 0), (2, 1)) if more else ()):
                    mrow(i, e, c)
                if more:
                    stack_q(1, i, 1)
                    stack_k(1, i, 1)
                    mrow(i, 2, 2)
                    swap(i, 0, 2)
                    swap(i, 1, 2)

            swap(0, 0)
            swap(0, 1)
            with sp.Fori(0, PAIRS - 1) as i:
                pair(i, True)
            pair(PAIRS - 1, False)
            for n in range(CYCLES * NCH):
                c = n % NCH
                cs = slice(c * CH, (c + 1) * CH)
                if n < NCH:
                    sp.wait_ge(x1t_copied, c + 1)
                else:
                    sp.wait_ge(cn_out, n - NCH + 1)
                src = XNT if n < NCH else COS
                for half in range(2):
                    sp.dma_start(TW[64 * half:64 * half + 64, cs], src[64 - 64 * half:P - 64 * half, cs])\
                        .then_inc(swapped_in[c], 16)
            for c in range(NCH):
                sp.wait_ge(y_done, c + 1)
                sp.dma_start(out.rearrange("(t p) d -> p t d", p=P)[:, 4 * c:4 * c + 4, :],
                             X[:, 4 * c:4 * c + 4, :]).then_inc(stored, 16)
            sp.wait_ge(stored, 16 * NCH)

        @block.tensor
        def _(pe):
            def tile_T(src_tile, c, ready):
                bank = B4[c]
                for t in range(4):
                    mm = pe.transpose(bank[:, t * P:(t + 1) * P], src_tile(4 * c + t), mat(IDENT))
                mm.then_inc(ready, 1)

            pe.wait_ge(m_in, 48)
            for c in range(NCH):
                pe.wait_ge(xn_ready, 4 * c + 4)
                tile_T(lambda t: XN[:, t, :], c, xnt_ready)
            pe.matmul(RS[:, 0:D], mat(V1), mat(Q1), start=True, stop=True).then_inc(m1_ready, 1)
            pe.wait_ge(wd_ready, 1)
            for c in range(NCH):
                pe.wait_ge(xt_copied, c + 1)
                pe.matmul(B4[c], WT[:, 0:P], XNT[:, c * CH:(c + 1) * CH], start=True, stop=True).then_inc(latt_ready, 1)

            pe.wait_ge(m1_copied, 1)
            pe.matmul(RS[:, 0:D], M1[:, 0, :], mat(WO1T), start=True, stop=True).then_inc(m1_ready, 1)

            def latent_by_token():
                pe.wait_ge(m1_copied, 3)
                for g in range(2):
                    for t in range(8):
                        mm = pe.matmul(LATS_BANKS[g][:, t * L:(t + 1) * L],
                                       XNT[:, (8 * g + t) * P:(8 * g + t + 1) * P], WT[:, 0:L],
                                       start=True, stop=True, skip_group_check=True)
                    mm.then_inc(lats_ready, 1)

            def latent_to_model():
                pe.wait_ge(g_in, 48)
                for h in range(H):
                    if h % 4 == 0:
                        pe.wait_ge(zt_copied, min(h // 4 + 2, NCH))
                    mm = pe.matmul(GG_BANKS[h // 4][:, h % 4 * D:(h % 4 + 1) * D],
                                   WV[:, h, :, :].rearrange("d a l -> d (a l)"), WO[:, h, :],
                                   start=True, stop=True, skip_group_check=True)
                    if h % 4 == 3:
                        mm.then_inc(gg_ready, 1)

            def ffn_transposes():
                pe.wait_ge(z_scaled, 1)
                pe.wait_ge(lats_used, 2)
                pe.wait_ge(latt_used, NCH)
                for c in range(NCH):
                    for t in range(4):
                        mm = pe.transpose(ZT_BANKS[c][:, t * P:(t + 1) * P], Z[:, 4 * c + t, :], mat(IDENT))
                    mm.then_inc(zt_ready, 1)

            def ffn(c):
                pe.wait_ge(wf_ready, 1)
                pe.wait_ge(gg_used, 4)
                pe.wait_ge(z_ready, 1)
                if c >= 2:
                    pe.wait_ge(acc_ready, c - 1)
                for t in range(4):
                    mm = pe.matmul(FFN_BANKS[c][:, t * P:(t + 1) * P],
                                   ZT[:, (4 * c + t) * P:(4 * c + t + 1) * P], WT[:, P:2 * P],
                                   start=True, stop=True, skip_group_check=True)
                mm.then_inc(ffn_ready, 1)

            def rope(kind, c, n, block_):
                bank = WK[:, bank_of(n), :]
                cs = slice(c * CH, (c + 1) * CH)

                def w(t):
                    return t[:, block_ * P:block_ * P + P] if isinstance(block_, int) else t[:, bass.ds(block_ * P, P)]
                if kind == 0:
                    pe.matmul(bank, w(WQH), XH[:, cs], start=True, stop=False)
                    pe.matmul(bank, w(WQH), XL[:, cs], start=False, stop=False)
                    mm = pe.matmul(bank, w(WQL), XH[:, cs], start=False, stop=True)
                else:
                    pe.matmul(bank, w(WKH), LT[:, cs], start=True, stop=False)
                    mm = pe.matmul(bank, w(WKL), LT[:, cs], start=False, stop=True)
                mm.then_inc(rope_ready, 1)

            def max_piece(p, n, slot):
                t, k, w = PIECES[p]
                bank = WK[:, bank_of(n), 0:w]
                diagonal = k + w == (t + 1) * P
                mm = pe.matmul(bank, QS[:, slot, t * P:(t + 1) * P], KK[:, slot, k:k + w],
                               start=True, stop=not diagonal)
                if diagonal:
                    mm = pe.matmul(WK[:, bank_of(n), w - P:w], IDB[:, :], MK[:, 0, :], start=False, stop=True)
                mm.then_inc(max_ready, 1)

            def mrow(c, n, chunks):
                pe.wait_ge(mparts_ready, chunks + 1)
                pe.transpose(WK[:, bank_of(n), :].bitcast(F16)[0:4, 0:P], MM[:, c % 2, :], IDH[:, :])\
                    .then_inc(mrow_ready, 1)

            def scores(g, j, units):
                slot, (c, k0) = g // UNITS % 2, UNIT[g % UNITS]
                k, n = k0 + j, scores_bank(g - LAG, j)
                n0 = max(0, k - 4 * c) * P
                q = slice(c * CH + n0, (c + 1) * CH)
                diagonal = k >= 4 * c
                at = (2 * (g - LAG - START) + j) % (2 * SLOTS)
                back = 3 if at >= 3 else at - max(b for b in range(-3, 0) if (b + 2 * SLOTS) % 3 == n)
                if not isinstance(units, int) or 2 * g + j >= back:
                    pe.wait_ge(probs_ready, 2 * (units + g) + j + 1 - back)
                pe.matmul(ST[:, n, n0:CH], KK[:, slot, k * P:(k + 1) * P], QS[:, slot, q], start=True, stop=False)
                mm = pe.matmul(ST[:, n, n0:CH], KL[:, slot, k * P:(k + 1) * P], QM[:, slot, q],
                               start=False, stop=not diagonal)
                if diagonal:
                    mm = pe.matmul(ST[:, n, n0:n0 + P], IDB[:, :], MK[:, 1, :], start=False, stop=True)
                mm.then_inc(scores_ready, 1)

            def values(g, chunks):
                c, k0 = UNIT[g % UNITS]
                new = k0 == 0 and g > 0
                if new:
                    pe.wait_ge(ou_copied, chunks)
                b = g % PBUF
                n0 = [max(0, k0 + j - 4 * c) * P for j in range(2)]
                for j in range(2):
                    pe.matmul(OU[:, n0[j]:CH], LS[:, k0 + j, :, :].rearrange("p a l -> p (a l)"),
                              PH[:, b, j, n0[j]:CH], start=(k0 + j == 0), stop=False, skip_group_check=True)
                for j in range(2):
                    pe.matmul(OU[HD * j:HD * j + HD, n0[j]:CH], LS[:, k0 + j, 0, :], PL[:, b, j, n0[j]:CH],
                              start=False, stop=(k0 == 4 * c + 2), skip_group_check=True)
                if new:
                    pe.wait_ge(rs_copied, chunks)
                for j in range(2):
                    row = 0 if c == 0 else 64 * j
                    for part, src in enumerate((PH, PL)):
                        mm = pe.matmul(RS[row + 32 * part:row + 32 * part + 32, n0[j]:CH], ONE[:, :],
                                       src[:, b, j, n0[j]:CH], start=(k0 == 0 and (j == 0 or c > 0)),
                                       stop=(k0 == 4 * c + 2), skip_group_check=True)
                mm.then_inc(unit_summed, 1)

            def sums(c, n):
                rows_ = HD if c == 0 else P
                for t in range(4):
                    for part in (SUMH, SUML):
                        mm = pe.matmul(WK[:, bank_of(n), t:t + 1], part[0:rows_, c % 2, 1, t * P:(t + 1) * P],
                                       SELB[0:rows_, :], start=part is SUMH, stop=part is SUML, skip_group_check=True)
                mm.then_inc(sum_ready, 1)

            def outs(e, c, n, i):
                at = bass.ds(i * (2 * D) + e * D, D) if not isinstance(i, int) else slice((2 * i + e) * D, (2 * i + e + 1) * D)
                for t in range(4):
                    o, ts = WK[:, bank_of(n), t * P:(t + 1) * P], slice(t * P, (t + 1) * P)
                    pe.matmul(o, SUMH[:, c % 2, 0, ts], GGH[:, at], start=True, stop=False, skip_group_check=True)
                    pe.matmul(o, SUMH[:, c % 2, 0, ts], GGL[:, at], start=False, stop=False, skip_group_check=True)
                    mm = pe.matmul(o, SUML[:, c % 2, 0, ts], GGH[:, at], start=False, stop=True, skip_group_check=True)
                mm.then_inc(out_ready, 1)

            def pair(i, slots, more, before=None):
                units = i * SLOTS
                used = list(before or [])

                def work(kind, a, e, n):
                    if len(used) < WORK_BANKS:
                        was = [use for use in in_order(BODY) if bank_of(use[3]) == bank_of(n)][-1]
                        pe.wait_ge(*bank_read(*was[:3], i, back=1))
                        pe.wait_ge(piece_done, i * (2 * MAXES) + PIECES_BEFORE)
                        pe.wait_ge(mt_copied, i * (2 * NCH) + ROWS_BEFORE)
                    else:
                        pe.wait_ge(*bank_read(*used[-WORK_BANKS], i))
                    used.append((kind, a, e))
                    if kind == "rope":
                        rope(a // NCH, a % NCH, n, i + e // 2)
                    elif kind == "mrow":
                        mrow(a, n, i * (2 * NCH) + e * NCH + a)
                    elif kind == "max":
                        if a == 0:
                            pe.wait_ge(stacked[e % 2], i * 64 + 64 * (e // 2 + 1))
                        max_piece(a, n, e % 2)
                    elif kind == "sum":
                        pe.wait_ge(sums_low, i * (2 * NCH) + e * NCH + a + 1)
                        sums(a, n)
                    else:
                        outs(e, a, n, i)

                for w, (first, second) in slots.items():
                    g = w + LAG
                    made = g < SLOTS or more
                    for use in first:
                        work(*use)
                    if made:
                        c, k0 = UNIT[g % UNITS]
                        if k0 == 0:
                            if c == 0:
                                pe.wait_ge(stacked_low[g // UNITS % 2], i * 32 + 32 * (g // SLOTS) + 32)
                            pe.wait_ge(mrow_stacked[c % 2], i * 64 + 32 * (g // UNITS) + 16 * (c // 2) + 16)
                        scores(g, 0, units)
                    for use in second:
                        work(*use)
                    if made:
                        scores(g, 1, units)
                    if w < SLOTS or more:
                        (e, u) = divmod(w, UNITS)
                        c, k0 = UNIT[u]
                        if u in POOL_LOWS[e % 2]:
                            pe.wait_ge(low_probs_pool, i * len(POOL_UNITS) + pool_units(w) + 1)
                        else:
                            pe.wait_ge(low_probs, i * (SLOTS - len(POOL_UNITS)) + w - pool_units(w) + 1)
                        values(w, i * (2 * NCH) + e * NCH + c)

            pe.wait_ge(const_ready, 1)
            for n, (kind, a) in enumerate(PROLOGUE):
                if n >= WORK_BANKS:
                    was, b = PROLOGUE[n - WORK_BANKS]
                    pe.wait_ge({"rope": rope_product, "max": piece_done, "mrow": mt_copied}[was], b + 1)
                if kind == "rope":
                    if n == 0:
                        pe.wait_ge(w0_ready, 2)
                    if bank_of(n + FIRST) == 2:
                        pe.wait_ge(latt_used, NCH)
                    pe.wait_ge(split_ready, a // 2 % NCH + 1)
                    rope(a // (2 * NCH), a // 2 % NCH, n + FIRST, a % 2 * PAIRS)
                    if a == NCH:
                        pe.wait_ge(m1_copied, 2)
                        pe.matmul(RS[:, 0:D], mat(Q1T), M1[:, 1, :], start=True, stop=True).then_inc(m1_ready, 1)
                    if a == 2 * NCH - 1:
                        latent_by_token()
                    if a == 2 * ROPES - 1:
                        ffn_transposes()
                        latent_to_model()
                elif kind == "max":
                    if a == 0:
                        pe.wait_ge(stacked[0], 64)
                    max_piece(a, n + FIRST, 0)
                    if a in FFN_AFTER:
                        ffn(FFN_AFTER.index(a))
                    if a == SCORES_AFTER:
                        pe.sem_inc(unit_summed, PBUF)
                        pe.wait_ge(stacked_low[0], 32)
                        pe.wait_ge(kl_ready, 1)
                    if SCORES_AFTER <= a < SCORES_AFTER + LAG:
                        g = a - SCORES_AFTER
                        c, k0 = UNIT[g]
                        if k0 == 0:
                            pe.wait_ge(mrow_stacked[c % 2], 16)
                        scores(g, 0, 0)
                        scores(g, 1, 0)
                else:
                    mrow(a, n + FIRST, a)
            pe.wait_ge(acc_ready, NCH)
            pair(0, PEELED, True, before=[(kind, a, 0) for kind, a in PROLOGUE])
            with pe.Fori(0, PAIRS - 1) as i:
                pair(i, BODY, True)
            pair(PAIRS - 1, LAST, False)

            pe.wait_ge(ou_copied, H * NCH)
            pe.wait_ge(rs_copied, H * NCH)
            pe.wait_ge(probs_ready, 2 * H * UNITS)
            pe.wait_ge(acc_ready, H * NCH + NCH)

            def layer_1(n):
                cs = slice(n % NCH * CH, (n % NCH + 1) * CH)
                if n < NCH:
                    pe.wait_ge(x1t_copied, n + 1)
                else:
                    pe.wait_ge(cn_out, n - NCH + 1)
                pe.matmul(NB[n % NCH], mat(CW1), (XNT if n < NCH else COS)[:, cs], start=True, stop=True)\
                    .then_inc(layer1, 1)

            def layer_2(cyc, p):
                pe.wait_ge(h1_ready, cyc * NCH + 2 * p + 2)
                for j in range(2):
                    mm = pe.matmul(NB[2 * p][64 * j:64 * j + 64, :], mat(CW2, P, 64), H1[:, 2 * p + j, :],
                                   start=True, stop=True, skip_group_check=True)
                mm.then_inc(layer2, 1)

            def layer_3(cyc):
                pe.wait_ge(h2_ready, 2 * cyc + 2)
                for c in range(NCH):
                    rows_ = slice(64 * (c % 2), 64 * (c % 2) + 64)
                    mm = pe.matmul(NB[1][32 * c:32 * c + 32, :], MA[rows_, CW3 * D:CW3 * D + 32], H2[rows_, c // 2, :],
                                   start=True, stop=True, skip_group_check=True)
                mm.then_inc(layer3, 1)

            def layer_4(cyc, c):
                pe.wait_ge(h3_ready, cyc + 1)
                rows_ = slice(32 * c, 32 * c + 32)
                pe.matmul(NB[c], MA[rows_, CW4 * D:(CW4 + 1) * D], H3[rows_, :], start=True, stop=True)\
                    .then_inc(layer4, 1)

            def attention(c):
                for t in range(4):
                    o = B4[c][:, t * P:(t + 1) * P]
                    pe.matmul(o, XNT[:, (4 * c + t) * P:(4 * c + t + 1) * P], M1[:, 0, :], start=t == 0, stop=False,
                              skip_group_check=True)
                    pe.matmul(o, RW[:, D:2 * D], RW[:, 0:D], start=False, stop=False, skip_group_check=True)

            def plus(part, c, ready):
                pe.wait_ge(ready, (CYCLES - 1) * NCH + c + 1)
                for t in range(4):
                    mm = pe.matmul(B4[c][:, t * P:(t + 1) * P], part[:, c, t * P:(t + 1) * P], mat(IDENT),
                                   start=False, stop=part is TH, skip_group_check=True)
                return mm

            def transposed(c):
                pe.wait_ge(x1n, 4 * c + 4)
                tile_T(lambda t: XN[:, t, :], c, x1t)

            transposed(0)
            transposed(1)
            layer_1(0)
            transposed(2)
            layer_1(1)
            transposed(3)
            layer_1(2)
            layer_1(3)
            for cyc in range(CYCLES):
                if cyc:
                    for c in range(NCH):
                        layer_1(cyc * NCH + c)
                layer_2(cyc, 0)
                if cyc == 0:
                    pe.wait_ge(gc_done, 1)
                    pe.matmul(B4[0][0:64, 0:1], mat(GW1, P, 64), TC[:, 4:5], start=True, stop=True)\
                        .then_inc(gc_mm, 1)
                layer_2(cyc, 1)
                if cyc == 0:
                    pe.wait_ge(gc_act, 1)
                    pe.matmul(B4[0][0:32, 0:1], mat(GW2, 64, 32), TC[0:64, 5:6], start=True, stop=True)\
                        .then_inc(gc_mm, 1)
                elif cyc == 1:
                    attention(1)
                else:
                    plus(S0, 0, s0_ready)
                    plus(S0, 1, s0_ready)
                layer_3(cyc)
                if cyc == 0:
                    attention(3)
                    pe.wait_ge(gc_act, 2)
                    pe.matmul(B4[0][:, 0:1], mat(GW3, 32, P), TC[0:32, 6:7], start=True, stop=True)\
                        .then_inc(gc_mm, 1)
                    pe.wait_ge(gc_act, 3)
                if cyc < 2:
                    attention(2 * cyc)
                else:
                    plus(S0, 2, s0_ready)
                    plus(S0, 3, s0_ready)
                for c in range(NCH):
                    layer_4(cyc, c)
            for c in range(NCH):
                plus(TH, c, cn_out).then_inc(y_ready, 1)

        @block.vector
        def _(v):
            chain = [0]

            def link(ins):
                chain[0] += 1
                ins.then_inc(dve, 1)
                v.wait_ge(dve, chain[0])

            v.memset(EPSC[:, 0:1], LN_EPS)
            v.memset(EPSC[:, 1:2], FFN_EPS)
            v.memset(ONE[:, :], 1.0)
            link(v.memset(AM[:, :], 0.0))
            link(v.memset(SEL[:, :], 0.0))
            for q in range(4):
                last = v.memset(SEL[32 * q:32 * q + 1, :], 1.0)
            link(last)
            v.wait_ge(x_in, 16)
            for t in range(NT):
                last = v.bn_stats(ST6[:, t, :], X[:, t, :])
            link(last)
            for t in range(NT):
                last = v.bn_aggr(MV[:, t, :], ST6[:, t, :])
            last.then_inc(var_ready, 1)
            v.wait_ge(std_ready, 1)
            link(v.reciprocal(RD[:, :], SD[:, :]))
            for t in range(NT):
                v.tensor_scalar(XN[:, t, :], X[:, t, :], MV[:, t, 0:1], RD[:, t:t + 1],
                                ALU.subtract, ALU.mult).then_inc(xn_ready, 1)
            link(v.tensor_tensor(RD2[:, :], MV[:, :, 1], RD[:, :], ALU.mult))
            v.tensor_tensor(RD2[:, :], RD2[:, :], RD[:, :], ALU.mult).then_inc(var_ready, 1)
            v.wait_ge(m_in, 48)
            v.tensor_reduce(AM[:, 1:2], mat(WD2), AX.X, ALU.max, apply_absolute_value=True)
            v.wait_ge(w_in, 48)
            v.tensor_reduce(AM[:, 0:1], WQ[:, :], AX.X, ALU.max, apply_absolute_value=True)
            v.tensor_reduce(AM[:, 2:3], WKU[:, :], AX.X, ALU.max, apply_absolute_value=True).then_inc(am_ready, 1)
            v.wait_ge(std_ready, 2)
            v.reciprocal(RD2[:, :], SD[:, :]).then_inc(rd2_ready, 1)
            v.tensor_copy(IDB[:, :], mat(IDENT))
            v.tensor_copy(IDH[:, :], mat(IDENT))
            v.tensor_copy(MK[:, 0, :], mat(MASK_QK))
            v.tensor_copy(MK[:, 1, :], mat(MASK_KQ)).then_inc(const_ready, 1)

            def powers_of_two(a, b):
                link(v.tensor_scalar(AMG[:, a:b], AMG[:, a:b], 1e-30, None, ALU.max))
                link(v.tensor_scalar(EX[:, a:b].bitcast(I32), AMG[:, a:b].bitcast(I32), 0x7F800000, None,
                                     ALU.bitwise_and))
                return v.reciprocal(IV[:, a:b], EX[:, a:b])

            v.wait_ge(amg_ready, 1)
            powers_of_two(0, 3).then_inc(iv_ready, 1)
            v.wait_ge(iv_ready, 1)
            v.tensor_scalar(WT[:, 0:P], mat(WD2), IV[:, 1:2], None, ALU.mult).then_inc(wd_ready, 1)
            v.wait_ge(m1_ready, 1)
            v.tensor_tensor(M1[:, 0, :], RS[:, 0:D], mat(BLK), ALU.mult).then_inc(m1_copied, 1)
            for c in range(NCH):
                cs = slice(c * CH, (c + 1) * CH)
                v.wait_ge(xt_copied, c + 1)
                v.tensor_tensor(XL[:, cs], XNT[:, cs], XH[:, cs], ALU.subtract).then_inc(split_ready, 1)
            for k, (raw, hi, lo) in enumerate(((WQ, WQH, WQL), (WKU, WKH, WKL))):
                v.wait_ge(w0_high, k + 1)
                v.scalar_tensor_tensor(out=first_blocks(lo), in0=first_blocks(raw), scalar=IV[:, 2 * k:2 * k + 1],
                                       in1=first_blocks(hi), op0=ALU.mult, op1=ALU.subtract).then_inc(w0_ready, 1)
            for c in range(NCH):
                cs = slice(c * CH, (c + 1) * CH)
                v.wait_ge(latt_high, c + 1)
                v.tensor_tensor(LT[L:P, cs], B4[c][L:P, :], LT[L:P, cs], ALU.subtract).then_inc(latt_used, 1)
            v.wait_ge(m1_ready, 2)
            v.tensor_copy(M1[:, 1, :], RS[:, 0:D]).then_inc(m1_copied, 1)
            link(v.tensor_scalar(SC[:, 1:2], EX[:, 0:1], EX[:, 1:2], HD ** -0.5, ALU.mult, ALU.mult))
            v.tensor_scalar(SC[:, 0:1], SC[:, 1:2], EX[:, 2:3], None, ALU.mult)

            def z_part_1():
                v.wait_ge(zt_copied, NCH)
                v.tensor_reduce(AM[:, 0:1], ZT[:, :], AX.X, ALU.max, apply_absolute_value=True)\
                    .then_inc(zmax_ready, 1)

            def z_part_2():
                v.wait_ge(zmaxg_ready, 1)
                link(v.reciprocal(SC[:, 2:3], AMG[:, 0:1]))
                link(v.tensor_scalar(SC[:, 2:3], SC[:, 2:3], QB, None, ALU.mult))
                link(v.tensor_scalar(ZT[:, :], ZT[:, :], SC[:, 2:3], QB - EPS, ALU.mult, ALU.min))
                v.tensor_scalar(ZT[:, :], ZT[:, :], EPS - QB, None, ALU.max).then_inc(z_ready, 1)

            def other_weights():
                v.wait_ge(g_in, 48)
                v.tensor_reduce(AM[0:HD, 3:4], WV[:, :, 0, :], AX.XY, ALU.max, apply_absolute_value=True)
                v.tensor_reduce(AM[0:HD, 4:5], WO[:, :, :], AX.XY, ALU.max, apply_absolute_value=True)
                v.tensor_reduce(AM[:, 5:6], mat(W_FFN), AX.X, ALU.add, apply_absolute_value=True).then_inc(am_ready, 1)

            def scales():
                v.wait_ge(amg_ready, 3)
                link(powers_of_two(3, 5))
                v.tensor_scalar(SC[:, 6:7], IV[:, 3:4], IV[:, 4:5], None, ALU.mult).then_inc(gg_scale, 1)
                v.wait_ge(gg_scale, 1)
                link(v.tensor_scalar(SC[:, 7:8], IV[:, 1:2], 1.0 / SUM_SCALE, None, ALU.mult))
                v.tensor_scalar(SELB[:, :], SEL[:, :], SC[:, 6:7], SC[:, 7:8], ALU.mult, ALU.mult)
                link(v.tensor_scalar(SC[:, 3:4], AMG[:, 5:6], 1.0 / (D * D), None, ALU.mult))
                link(v.tensor_scalar(SC[:, 4:5], SC[:, 3:4], EPS, None, ALU.add))
                link(v.reciprocal(SC[:, 4:5], SC[:, 4:5]))
                link(v.tensor_scalar(WT[:, P:2 * P], mat(W_FFN), SC[:, 4:5], 1.0, ALU.mult, ALU.min))
                link(v.tensor_scalar(WT[:, P:2 * P], WT[:, P:2 * P], -1.0, 12582912.0, ALU.max, ALU.add))
                v.tensor_scalar(WT[:, P:2 * P], WT[:, P:2 * P], -12582912.0, None, ALU.add).then_inc(wf_ready, 1)
                link(v.tensor_scalar(SC[:, 5:6], AMG[:, 0:1], SC[:, 3:4], 1.0 / QB, ALU.mult, ALU.mult))

            def gg_lows():
                for q in range(4):
                    at = slice(q * CH, (q + 1) * CH)
                    v.wait_ge(gg_high, q + 1)
                    v.scalar_tensor_tensor(out=GGL[:, at], in0=GG_BANKS[q], scalar=SC[:, 6:7], in1=GGH[:, at],
                                           op0=ALU.mult, op1=ALU.subtract).then_inc(gg_used, 1)

            def add_ffn(c):
                if c == 0:
                    v.wait_ge(low_ready, 2 * NCH)
                v.wait_ge(ffn_ready, c + 1)
                v.scalar_tensor_tensor(out=ACC[:, 4 * c:4 * c + 4, :].rearrange("p t d -> p (t d)"),
                                       in0=FFN_BANKS[c], scalar=SC[:, 5:6],
                                       in1=X[:, 4 * c:4 * c + 4, :].rearrange("p t d -> p (t d)"),
                                       op0=ALU.mult, op1=ALU.add).then_inc(acc_ready, 1)

            v.wait_ge(t_in, 32)
            between = {2: z_part_2, 5: scales, 9: gg_lows}

            def max_of(p, n, h):
                t, k, w = PIECES[p]
                v.wait_ge(max_ready, h * MAXES + p + 1)
                v.tensor_reduce(MP[:, t, k // CH:k // CH + 1], WK[:, bank_of(n), 0:w], AX.X, ALU.max)\
                    .then_inc(piece_done, 1)

            def mneg(c, i, e):
                chunks = i * (2 * NCH) + e * NCH + c
                v.wait_ge(piece_done, (i * (2 * MAXES) + e * MAXES) + max(p for p, d in CHUNK_MAXED.items() if d == c) + 1)
                best = MP[:, 4 * c:4 * c + 4, 0]
                if c:
                    v.tensor_reduce(NM[:, 4 * c:4 * c + 4], MP[:, 4 * c:4 * c + 4, 0:c + 1], AX.X, ALU.max)\
                        .then_inc(mneg_ready, 1)
                    best = NM[:, 4 * c:4 * c + 4]
                    v.wait_ge(mneg_ready, i * (2 * NCH - 2) + e * (NCH - 1) + c)
                if not (isinstance(i, int) and i == 0 and e == 0 and c < 2):
                    v.wait_ge(mrow_ready, chunks - 1)
                v.tensor_scalar(MM[:, c % 2, :], best, -1.0 / MSHIFT, None, ALU.mult).then_inc(mparts_ready, 1)

            def mrow_copy(c, n, chunks):
                v.wait_ge(mrow_ready, chunks + 1)
                v.tensor_copy(MT[:, c % 2, :], WK[:, bank_of(n), :].bitcast(F16)[0:4, 0:P]).then_inc(mt_copied, 1)

            def low_of(g, units):
                c, k0 = UNIT[g % UNITS]
                b = g % PBUF
                v.wait_ge(probs_ready, 2 * (units + g + 1))
                if k0 < 4 * c:
                    last = v.tensor_tensor(PL[:, b, :, :], PR[:, b, :, :], PH[:, b, :, :], ALU.subtract)
                else:
                    for j in range(2):
                        n0 = (k0 + j - 4 * c) * P
                        last = v.tensor_tensor(PL[:, b, j, n0:CH], PR[:, b, j, n0:CH], PH[:, b, j, n0:CH],
                                               ALU.subtract)
                last.then_inc(low_probs, 1)

            def recip(c, n, chunks):
                v.wait_ge(sum_ready, chunks + 1)
                v.reciprocal(RL[:, c % 2, :], WK[:, bank_of(n), 0:4]).then_inc(rl_ready, 1)

            def add_out(c, n, chunks):
                v.wait_ge(out_ready, chunks + 1)
                v.wait_ge(rl_ready, chunks + 1)
                v.wait_ge(acc_ready, chunks + NCH)
                for t in range(4):
                    a = ACC[:, 4 * c + t, :]
                    last = v.scalar_tensor_tensor(out=a, in0=WK[:, bank_of(n), t * P:(t + 1) * P],
                                                  scalar=RL[:, c % 2, t:t + 1], in1=a,
                                                  op0=ALU.mult, op1=ALU.add)
                last.then_inc(acc_ready, 1)

            def works(uses, i):
                for kind, a, e, n in uses:
                    h = i * 2 + e
                    chunks = i * (2 * NCH) + e * NCH + a
                    if kind == "max":
                        t, k, _ = PIECES[a]
                        if k == 0 and t % 4 == 0:
                            v.wait_ge(mparts_ready, i * (2 * NCH) + e * NCH + t // 4)
                        max_of(a, n, h)
                        if a in CHUNK_MAXED:
                            mneg(CHUNK_MAXED[a], i, e)
                    elif kind == "mrow":
                        v.wait_ge(mrow_stacked[a % 2], i * 64 + 32 * e + 16 * (a // 2))
                        mrow_copy(a, n, chunks)
                    elif kind == "sum":
                        recip(a, n, chunks)
                    elif kind == "out":
                        add_out(a, n, chunks)

            def stats(c):
                v.wait_ge(acc_ready, (H - 1) * NCH + c + 1 + NCH)
                for t in range(4 * c, 4 * c + 4):
                    last = v.bn_stats(ST6[:, t, :], ACC[:, t, :])
                link(last)
                for t in range(4 * c, 4 * c + 4):
                    last = v.bn_aggr(MV[:, t, :], ST6[:, t, :])
                last.then_inc(x1_stats, 1)

            def pair(i, slots, more):
                for w, (first, second) in slots.items():
                    works(first, i)
                    works(second, i)
                    if (w + 1 < SLOTS or more) and (w + 1) % SLOTS not in POOL_UNITS:
                        low_of(w + 1, i * SLOTS)
                    for kind, c, e, _ in first:
                        if kind == "out" and e == 1 and not more and c < NCH - 1:
                            stats(c)

            for n, (kind, a) in enumerate(PROLOGUE, FIRST):
                if kind == "rope":
                    k, c, swapped = a // 2, a // 2 % NCH, a % 2
                    v.wait_ge(rope_ready, a + 1)
                    if k >= 2 and swapped == 0:
                        v.wait_ge(low_ready, k - 1)
                    v.tensor_tensor(RB0[:, k % 2, swapped, :], WK[:, bank_of(n), :],
                                    (COS, SIN)[swapped][:, c * CH:(c + 1) * CH], ALU.mult)\
                        .then_inc(rope_product, 1)
                    if swapped:
                        v.wait_ge(rope_product, a + 1)
                        v.tensor_tensor(RB0[:, k % 2, 0, :], RB0[:, k % 2, 0, :], RB0[:, k % 2, 1, :], ALU.add)\
                            .then_inc(rope_summed, 1)
                    if a == NCH + 1:
                        v.wait_ge(m1_ready, 3)
                        v.tensor_copy(M1[:, 0, :], RS[:, 0:D]).then_inc(m1_copied, 1)
                    if a == 2 * ROPES - 1:
                        other_weights()
                        z_part_1()
                    if a == 3 * NCH - 1:
                        for g in range(2):
                            v.wait_ge(lats_high, g + 1)
                            v.tensor_tensor(LS[:, 8 * g:8 * g + 8, 1, :],
                                            LATS_BANKS[g][:, :].rearrange("p (t l) -> p t l", l=L),
                                            LS[:, 8 * g:8 * g + 8, 0, :], ALU.subtract).then_inc(lats_used, 1)
                elif kind == "max":
                    max_of(a, n, 0)
                    if a in CHUNK_MAXED:
                        mneg(CHUNK_MAXED[a], 0, 0)
                    if a in between:
                        between[a]()
                    if a - 2 in FFN_AFTER:
                        add_ffn(FFN_AFTER.index(a - 2))
                else:
                    if a == 2:
                        v.wait_ge(mrow_stacked[0], 16)
                    mrow_copy(a, n, a)
            low_of(0, 0)
            pair(0, PEELED, True)
            with v.Fori(0, PAIRS - 1) as i:
                pair(i, BODY, True)
            pair(PAIRS - 1, LAST, False)

            stats(NCH - 1)
            v.wait_ge(x1_std, 1)
            link(v.reciprocal(RD[:, :], SD[:, :]))
            for t in range(NT):
                v.tensor_scalar(XN[:, t, :], ACC[:, t, :], MV[:, t, 0:1], RD[:, t:t + 1],
                                ALU.subtract, ALU.mult).then_inc(x1n, 1)
            link(v.tensor_scalar(TC[:, 10:11], CO[:, C_B4:C_B4 + 1], 0.5, None, ALU.mult))
            link(v.tensor_scalar(TC[:, 11:12], CO[:, G_B3:G_B3 + 1], 0.5, None, ALU.mult))
            for c in range(NCH):
                v.wait_ge(x1t_copied, c + 1)
                last = v.tensor_reduce(TC[:, 12 + c:13 + c], XNT[:, c * CH:(c + 1) * CH], AX.X, ALU.add)
            link(last)
            link(v.tensor_reduce(TC[:, 9:10], TC[:, 12:12 + NCH], AX.X, ALU.add))
            v.tensor_scalar(TC[:, 4:5], TC[:, 9:10], 1.0 / S, None, ALU.mult).then_inc(gc_done, 1)
            v.wait_ge(gc_act, 3)
            link(v.tensor_scalar(TC[:, 8:9], TC[:, 7:8], 0.7, None, ALU.mult))
            link(v.tensor_scalar(TC[:, 0:1], TC[:, 8:9], CO[:, AR:AR + 1], 0.1, ALU.mult, ALU.add))
            link(v.tensor_scalar(TC[:, 0:1], TC[:, 0:1], CO[:, SIGN:SIGN + 1], None, ALU.mult))
            link(v.tensor_scalar(TC[:, 1:2], CO[:, AR:AR + 1], CO[:, SIGN:SIGN + 1], 0.3, ALU.mult, ALU.mult))
            for cyc in range(CYCLES):
                for c in range(NCH):
                    cs = slice(c * CH, (c + 1) * CH)
                    if cyc:
                        v.wait_ge(cn_out, (cyc - 1) * NCH + c + 1)
                    v.wait_ge(swapped_in[c], 32 * cyc + 32)
                    v.scalar_tensor_tensor(out=S0[:, c, :], in0=TW[:, cs], scalar=TC[:, 0:1],
                                           in1=(COS if cyc else XNT)[:, cs], op0=ALU.mult, op1=ALU.add)\
                        .then_inc(s0_ready, 1)
                    last = v.tensor_scalar(TW[:, cs], TW[:, cs], TC[:, 1:2], None, ALU.mult)
                link(last)
                for c in range(NCH):
                    cs = slice(c * CH, (c + 1) * CH)
                    v.wait_ge(th_ready, cyc * NCH + c + 1)
                    prod = v.tensor_tensor(TH[:, c, :], TH[:, c, :], TW[:, cs], ALU.mult)
                    if cyc < CYCLES - 1:
                        link(prod)
                        v.tensor_tensor(COS[:, cs], S0[:, c, :], TH[:, c, :], ALU.add).then_inc(cn_out, 1)
                    else:
                        prod.then_inc(cn_out, 1)
            for c in range(NCH):
                v.wait_ge(y_ready, c + 1)
                v.tensor_tensor(X[:, 4 * c:4 * c + 4, :].rearrange("p t d -> p (t d)"),
                                ACC[:, 4 * c:4 * c + 4, :].rearrange("p t d -> p (t d)"),
                                B4[c], ALU.add).then_inc(y_done, 1)

        @block.scalar
        def _(act):
            act.wait_ge(var_ready, 1)
            act.activation(SD[:, :], MV[:, :, 1], ACT.Sqrt, bias=EPSC[:, 0:1]).then_inc(std_ready, 1)
            act.wait_ge(var_ready, 2)
            act.activation(SD[:, :], RD2[:, :], ACT.Sqrt, bias=EPSC[:, 1:2]).then_inc(std_ready, 1)
            for c in range(NCH):
                act.wait_ge(xnt_ready, c + 1)
                act.activation(XNT[:, c * CH:(c + 1) * CH], B4[c], ACT.Copy)
                act.activation(XH[:, c * CH:(c + 1) * CH], B4[c], ACT.Copy).then_inc(xt_copied, 1)
            act.wait_ge(iv_ready, 1)
            for k, (raw, hi) in enumerate(((WQ, WQH), (WKU, WKH))):
                act.activation(first_blocks(hi), first_blocks(raw), ACT.Copy, scale=IV[:, 2 * k:2 * k + 1])\
                    .then_inc(w0_high, 1)
            for c in range(NCH):
                act.wait_ge(latt_ready, c + 1)
                act.activation(LT[:, c * CH:(c + 1) * CH], B4[c], ACT.Copy).then_inc(latt_high, 1)

            def high(k, n, rb=RB):
                kind, c = divmod(k, NCH)
                act.wait_ge(rope_summed, n + 1)
                act.activation(SG[:, 2 * kind, c * CH:(c + 1) * CH], rb[:, k % 2, 0, :], ACT.Copy).then_inc(high_ready, 1)

            def probs(g, units):
                c, k0 = UNIT[g % UNITS]
                act.wait_ge(unit_summed, units + g + 1)
                for j in range(2):
                    n0 = max(0, k0 + j - 4 * c) * P
                    act.wait_ge(scores_ready, 2 * (units + g) + j + 1)
                    act.activation(PR[:, g % PBUF, j, n0:CH], ST[:, scores_bank(g - LAG, j), n0:CH], ACT.Exp,
                                   scale=SC[:, 0:1]).then_inc(probs_ready, 1)

            def copy_chunk(e, c, w, i):
                act.wait_ge(unit_summed, i * SLOTS + PBUF + w + 1)
                if not isinstance(i, int) or i > 0 or c >= 2:
                    act.wait_ge(acc_ready, i * (2 * NCH) + e * NCH + c - 1 + NCH)
                n = i * (2 * NCH) + e * NCH + c + 1
                act.activation(SUMS[:, c % 2, 0, :], OU[:, :], ACT.Copy, scale=1.0 / SUM_SCALE).then_inc(ou_copied, 1)
                act.activation(SUMS[:, c % 2, 1, :], RS[:, :], ACT.Copy).then_inc(rs_copied, 1)
                act.wait_ge(ou_copied, n)
                act.wait_ge(rs_copied, n)
                act.activation(SUMH[:, c % 2, :, :], SUMS[:, c % 2, :, :], ACT.Copy).then_inc(sums_high, 1)

            def rope_copy(k, e, n, i):
                m = (e // 2 - 1) * ROPES + k
                act.wait_ge(rope_ready, i * ROPES + (2 * ROPES + m + 1))
                act.wait_ge(rope_product, i * (2 * ROPES) + (2 * ROPES + 2 * (m - RA_BUFS) + 2))
                act.activation(RA[:, k % RA_BUFS, :], WK[:, bank_of(n), :], ACT.Copy).then_inc(rope_copied, 1)

            def pair(i, slots, more):
                for w, (first, second) in slots.items():
                    if more and rope_of_slot(w, HIGH_LAG):
                        k, pairs = rope_of_slot(w, HIGH_LAG)
                        if k == 0:
                            for slot in range(2):
                                act.wait_ge(stacked[slot], i * 64 + 64 * pairs)
                                act.wait_ge(stacked_low[slot], i * 32 + 32 * pairs)
                        high(k, i * ROPES + (pairs * ROPES + k))
                    for kind, a, e, n in second:
                        if kind == "rope":
                            rope_copy(a, e, n, i)
                    if w + LAG < SLOTS or more:
                        probs(w + LAG, i * SLOTS)
                    e, u = divmod(w, UNITS)
                    if u in CHUNK_END and (w < SLOTS or more):
                        copy_chunk(e, CHUNK_END[u], w, i)

            for k in range(2 * NCH):
                high(k, k, RB0)
                if k == NCH:
                    for g in range(2):
                        act.wait_ge(lats_ready, g + 1)
                        act.activation(LS[:, 8 * g:8 * g + 8, 0, :],
                                       LATS_BANKS[g][:, :].rearrange("p (t l) -> p t l", l=L), ACT.Copy)\
                            .then_inc(lats_high, 1)
            act.wait_ge(split_ready, NCH)
            for c in range(NCH):
                act.wait_ge(zt_ready, c + 1)
                act.activation(ZT[:, c * CH:(c + 1) * CH], ZT_BANKS[c], ACT.Identity, bias=CO[:, BETA:BETA + 1],
                               scale=CO[:, GAMMA:GAMMA + 1]).then_inc(zt_copied, 1)
            for k, (raw, hi) in enumerate(((WQ, WQH), (WKU, WKH))):
                act.wait_ge(w_scaled, k + 1)
                act.activation(hi[:, P:H * HD], raw[:, P:H * HD], ACT.Copy).then_inc(w_high, 1)
            act.wait_ge(gg_scale, 1)
            for q in range(4):
                act.wait_ge(gg_ready, q + 1)
                act.activation(GGH[:, q * CH:(q + 1) * CH], GG_BANKS[q], ACT.Copy, scale=SC[:, 6:7]).then_inc(gg_high, 1)
            act.wait_ge(w_low, 2)
            for g in range(LAG):
                probs(g, 0)
            pair(0, PEELED, True)
            with act.Fori(0, PAIRS - 1) as i:
                pair(i, BODY, True)
            pair(PAIRS - 1, LAST, False)

            act.wait_ge(x1_stats, NCH)
            act.activation(SD[:, :], MV[:, :, 1], ACT.Sqrt, bias=EPSC[:, 0:1]).then_inc(x1_std, 1)
            act.activation(TC[:, 15:16], EPSC[:, 0:1], ACT.Gelu)
            for c in range(NCH):
                act.wait_ge(x1t, c + 1)
                act.activation(XNT[:, c * CH:(c + 1) * CH], B4[c], ACT.Copy)\
                    .then_inc(x1t_copied, 1)

            def gelu(dst, bank, bias, ready):
                act.activation(dst, bank, ACT.Gelu, bias=CO[:, bias:bias + 1]).then_inc(ready, 1)

            for cyc in range(CYCLES):
                for c in range(NCH):
                    act.wait_ge(layer1, cyc * NCH + c + 1)
                    gelu(H1[:, c, :], NB[c], C_B1, h1_ready)
                for p in range(2):
                    act.wait_ge(layer2, 2 * cyc + p + 1)
                    gelu(H2[:, p, :], NB[2 * p], C_B2, h2_ready)
                    if cyc == 0 and p == 0:
                        act.wait_ge(gc_mm, 1)
                        act.activation(TC[0:64, 5:6], B4[0][0:64, 0:1], ACT.Gelu, bias=CO[0:64, G_B1:G_B1 + 1])\
                            .then_inc(gc_act, 1)
                if cyc == 0:
                    act.wait_ge(gc_mm, 2)
                    act.activation(TC[0:32, 6:7], B4[0][0:32, 0:1], ACT.Gelu, bias=CO[0:32, G_B2:G_B2 + 1])\
                        .then_inc(gc_act, 1)
                act.wait_ge(layer3, cyc + 1)
                gelu(H3, NB[1], C_B3, h3_ready)
                if cyc == 0:
                    act.wait_ge(gc_mm, 3)
                    act.activation(TC[:, 7:8], B4[0][:, 0:1], ACT.Tanh, bias=TC[:, 11:12], scale=0.5)\
                        .then_inc(gc_act, 1)
                for c in range(NCH):
                    act.wait_ge(layer4, cyc * NCH + c + 1)
                    if cyc:
                        act.wait_ge(cn_out, (cyc - 1) * NCH + c + 1)
                    act.activation(TH[:, c, :], NB[c], ACT.Tanh, bias=TC[:, 10:11], scale=0.5).then_inc(th_ready, 1)

        @block.gpsimd
        def _(pool):
            pool.memset(KL[HD:HD + 1, :, :], MSHIFT).then_inc(kl_ready, 1)
            pool.wait_ge(kl_ready, 1)
            pool.wait_ge(am_ready, 1)
            pool.partition_all_reduce(AMG[:, 0:3], AM[:, 0:3], P, bass.bass_isa.ReduceOp.max).then_inc(amg_ready, 1)
            pool.wait_ge(amg_ready, 1)
            pool.wait_ge(rd2_ready, 1)
            pool.wait_ge(xnt_ready, NCH)
            for t in range(NT):
                last = pool.tensor_scalar(Z[:, t, :], XN[:, t, :], RD2[:, t:t + 1], None, ALU.mult)
            last.then_inc(z_scaled, 1)

            def rotated(k):
                kind, c = divmod(k, NCH)
                return 2 * kind, slice(c * CH, (c + 1) * CH)

            def add(k, n):
                pool.wait_ge(rope_product, n * 2 + 2)
                pool.tensor_tensor(RB[:, k % 2, 0, :], RB[:, k % 2, 0, :], RB[:, k % 2, 1, :], ALU.add).then_inc(rope_summed, 1)

            def low(k, n, rb=RB):
                part, cs = rotated(k)
                pool.wait_ge(high_ready, n + 1)
                pool.tensor_tensor(SG[:, part + 1, cs], rb[:, k % 2, 0, :], SG[:, part, cs], ALU.subtract)\
                    .then_inc(low_ready, 1)

            for k in range(2 * NCH):
                low(k, k, RB0)

            def scale_weights(k):
                raw = (WQ, WKU)[k]
                pool.tensor_scalar(raw[:, P:H * HD], raw[:, P:H * HD], IV[:, 2 * k:2 * k + 1], None, ALU.mult)\
                    .then_inc(w_scaled, 1)

            pool.wait_ge(low_ready, 2 * NCH)
            pool.wait_ge(am_ready, 2)
            pool.partition_all_reduce(AMG[:, 3:5], AM[:, 3:5], P, bass.bass_isa.ReduceOp.max).then_inc(amg_ready, 1)
            pool.partition_all_reduce(AMG[:, 5:6], AM[:, 5:6], P, bass.bass_isa.ReduceOp.add).then_inc(amg_ready, 1)
            pool.wait_ge(amg_ready, 3)
            scale_weights(0)
            pool.wait_ge(w_scaled, 1)
            pool.wait_ge(zmax_ready, 1)
            pool.partition_all_reduce(AMG[:, 0:1], AM[:, 0:1], P, bass.bass_isa.ReduceOp.max)\
                .then_inc(zmaxg_ready, 1)
            pool.wait_ge(zmaxg_ready, 1)
            scale_weights(1)
            for k, (raw, hi, lo) in enumerate(((WQ, WQH, WQL), (WKU, WKH, WKL))):
                pool.wait_ge(w_high, k + 1)
                pool.tensor_tensor(lo[:, P:H * HD], raw[:, P:H * HD], hi[:, P:H * HD], ALU.subtract).then_inc(w_low, 1)

            def low_of(g, units):
                c, k0 = UNIT[g % UNITS]
                assert k0 < 4 * c
                pool.wait_ge(probs_ready, 2 * (units + g + 1))
                pool.tensor_tensor(PL[:, g % PBUF, :, :], PR[:, g % PBUF, :, :], PH[:, g % PBUF, :, :], ALU.subtract)\
                    .then_inc(low_probs_pool, 1)

            def pair(i, slots, more):
                for w, (first, second) in slots.items():
                    if (w + 2 < SLOTS or more) and (w + 2) % SLOTS in POOL_UNITS:
                        low_of(w + 2, i * SLOTS)
                    e, u = divmod(w - 1, UNITS)
                    if u in CHUNK_END and w > 0 and (w - 1 < SLOTS or more):
                        c = CHUNK_END[u]
                        pool.wait_ge(sums_high, i * (2 * NCH) + e * NCH + c + 1)
                        pool.tensor_tensor(SUML[:, c % 2, :, :], SUMS[:, c % 2, :, :], SUMH[:, c % 2, :, :],
                                           ALU.subtract).then_inc(sums_low, 1)
                    if more and rope_of_slot(w, HIGH_LAG + 1):
                        k, pairs = rope_of_slot(w, HIGH_LAG + 1)
                        low(k, i * ROPES + (pairs * ROPES + k))
                    if more and rope_of_slot(w, ROTATE_LAG):
                        k, pairs = rope_of_slot(w, ROTATE_LAG)
                        m = i * ROPES + (pairs * ROPES + k)
                        part, cs = rotated(k)
                        b = k % RA_BUFS
                        pool.wait_ge(low_ready, m - 1)
                        pool.wait_ge(rope_copied, i * ROPES + ((pairs - 1) * ROPES + k + 1))
                        pool.tensor_tensor(RB[:, k % 2, 0, :], RA[:, b, :], COS[:, cs], ALU.mult).then_inc(rope_product, 1)
                        pool.wait_ge(halves_swapped[b], i * SWAPPED_PER_PAIR + ((pairs - 1) * SWAPPED_PER_PAIR + 64 * (k // RA_BUFS) + 64))
                        pool.tensor_tensor(RB[:, k % 2, 1, :], RSW[:, b, :], SIN[:, cs], ALU.mult)\
                            .then_inc(rope_product, 1)
                        add(k, m)

            pair(0, PEELED, True)
            with pool.Fori(0, PAIRS - 1) as i:
                pair(i, BODY, True)
            pair(PAIRS - 1, LAST, False)


def causal(transposed):
    import numpy as np
    m = np.triu(np.full((P, P), NEG, np.float32), 1)
    return m.T if transposed else m


def rotary():
    import numpy as np
    inv = (1.0 / np.float32(10000.0) ** (np.arange(0, HD, 2, dtype=np.float32) / np.float32(HD))).astype(np.float32)
    ang = (np.arange(S, dtype=np.float32)[None, :] * inv[:, None]).astype(np.float64)
    cos, sin = np.cos(ang).astype(np.float32), np.sin(ang).astype(np.float32)
    return np.concatenate([cos] * 4), np.concatenate([-sin, sin] * 2)


def kernel(**inputs):
    import numpy as np
    import concourse.bacc as bacc
    from concourse import mybir as mb
    from concourse.bass_utils import run_bass_kernel_spmd as run

    g = {k: np.asarray(v) for k, v in inputs.items()}

    def with_swapped(w):
        swapped = w[:P].reshape(2, 2, HD // 2, -1)[:, ::-1].reshape(P, -1)
        return np.concatenate([w, swapped]).T

    def wide(a):
        a = a if a.ndim == 2 else a[None, :]
        full = np.zeros((P, D), np.float32)
        full[:a.shape[0], :a.shape[1]] = a
        return full

    q1, v1 = (g[f"L1_attn_{n}_weight"].reshape(D, D) for n in "qv")
    wd = g["L0_attn_w_kv_down"].T
    blocks = np.kron(np.eye(H, dtype=np.float32), np.full((D // H, D // H), (D // H) ** -0.5, np.float32))
    c, z = "L1_ffn_cn_", "L1_ffn_gc_"
    mats = [np.eye(P, dtype=np.float32), np.concatenate([wd, wd], 1), g["L0_ffn_weight"],
            causal(False), causal(True),
            q1, q1.T, v1, g["L1_attn_out_w"].T, blocks,
            g[c + "w1"], g[c + "w2"], np.concatenate([g[c + "w3"]] * 2), np.broadcast_to(np.concatenate([g[c + "w4"]] * 4), (P, P)),
            g[z + "w1"], g[z + "w2"], np.broadcast_to(g[z + "w3"], (32, P))]
    vecs = [g[c + "b1"], np.tile(g[c + "b2"], 2), np.tile(g[c + "b3"], 4), np.broadcast_to(g[c + "b4"], (P,)),
            g[z + "b1"], g[z + "b2"], np.broadcast_to(g[z + "b3"], (P,)),
            np.broadcast_to(g["L1_ffn_adaptive_range"], (P,)), np.repeat(TWIST_SIGNS, P // 4),
            g["L0_ffn_ln_gamma"], g["L0_ffn_ln_beta"]]
    cols = np.zeros((P, len(vecs)), np.float32)
    for n, vec in enumerate(vecs):
        cols[:vec.size, n] = vec
    cos, sin = rotary()
    wq, wk = g["L0_attn_wq"], g["L0_attn_w_k_up"]
    arrays = dict(
        x=g["L0_attn_x"][0], wqT=with_swapped(wq), wkT=with_swapped(wk),
        wv=g["L0_attn_w_v_up"], woT=g["L0_attn_wo"].T, mats=np.concatenate([wide(m) for m in mats], 1),
        cols=cols, rows=np.concatenate([g["L1_attn_out_b"], np.ones(P, np.float32)])[None, :],
        cosT=cos, sinT=sin)
    nc = bacc.Bacc("TRN2", target_bir_lowering=False, num_devices=1)
    arrays = {k: np.ascontiguousarray(a) for k, a in arrays.items()}
    args = {k: nc.dram_tensor(k, a.shape, mb.dt.from_np(a.dtype), kind="ExternalInput").ap()
            for k, a in arrays.items()}
    args["out"] = nc.dram_tensor("out", (S, D), F32, kind="ExternalOutput").ap()
    build(nc, **args)
    r = run(nc, [arrays], core_ids=[0])
    return np.asarray(r.results[0]["out"]).reshape(1, S, D)
```
